# Optimizing a Trainium2 kernel written in Bass

```python
import numpy as np
import jax
import jax.numpy as jnp

def _softmax(x, axis=-1):
    return jax.nn.softmax(x, axis=axis)

def _gelu(x):
    return jax.nn.gelu(x, approximate=True)

def _silu(x):
    return jax.nn.silu(x)

def _sigmoid(x):
    return jax.nn.sigmoid(x)

def _layernorm(x, axis=-1, eps=1e-05):
    m = jnp.mean(x, axis=axis, keepdims=True)
    v = jnp.var(x, axis=axis, keepdims=True)
    return (x - m) / jnp.sqrt(v + eps)

def _scatter_add(tgt, idx, src, axis=0):
    return tgt.at[idx].add(src)

def _segment_sum(src, seg, n):
    return jax.ops.segment_sum(src, seg, n)
kernel_name = 'mk_macaron_d4_jaxref_r8_9af52e'

def setup_inputs(seed: int=0):
    np.random.seed(seed)
    _w = jnp.asarray

    def _L0_attn_setup():
        import jax, jax.numpy as jnp
        import numpy as np
        B, S, H, R = (2, 512, 256, 256)
        NB, CW = (16, 4)
        BW = R // NB

        def _block_diag_linear(x, w, b):
            xb = x.reshape(x.shape[0], x.shape[1], NB, BW)
            out = jnp.einsum('bsni,nij->bsnj', xb, w) + b
            return out.reshape(x.shape)

        def _causal_conv1d(x, conv_w, conv_b):
            xp = jnp.pad(x, ((0, 0), (CW - 1, 0), (0, 0)))
            out = conv_b
            for i in range(CW):
                out = out + conv_w[i] * xp[:, i:i + x.shape[1], :]
            return out

        def _rg_lru_scan(x, x_gate_pre, a_gate_pre, a_param):
            gate_x = jax.nn.sigmoid(x_gate_pre)
            gate_a = jax.nn.sigmoid(a_gate_pre)
            log_a = -8.0 * gate_a * jax.nn.softplus(a_param)
            a = jnp.exp(log_a)
            multiplier = jnp.sqrt(-jnp.expm1(2.0 * log_a))
            norm_x = x * gate_x * multiplier

            def combine(c1, c2):
                a1, b1 = c1
                a2, b2 = c2
                return (a1 * a2, a2 * b1 + b2)
            _, h = jax.lax.associative_scan(combine, (a, norm_x), axis=1)
            return h
        key = jax.random.key(seed)
        ks = jax.random.split(key, 9)
        x = jax.random.normal(ks[0], (B, S, H), dtype=jnp.float32)
        W_xy = jax.random.normal(ks[1], (2 * R, H), dtype=jnp.float32) / np.sqrt(H)
        ig_w = jax.random.normal(ks[2], (NB, BW, BW), dtype=jnp.float32) / np.sqrt(BW)
        ig_b = jnp.zeros((NB, BW), dtype=jnp.float32)
        ag_w = jax.random.normal(ks[3], (NB, BW, BW), dtype=jnp.float32) / np.sqrt(BW)
        ag_b = jnp.zeros((NB, BW), dtype=jnp.float32)
        unif = jax.random.uniform(ks[4], (R,), dtype=jnp.float32)
        a_real = 0.5 * jnp.log(unif * (0.999 ** 2 - 0.9 ** 2) + 0.9 ** 2 + 1e-08)
        a_param = jnp.log(jnp.expm1(-a_real))
        conv_w = jax.random.normal(ks[5], (CW, R), dtype=jnp.float32) / np.sqrt(CW * R)
        conv_b = jnp.zeros((R,), dtype=jnp.float32)
        W_resid = 0.02 * jax.random.normal(ks[6], (H, R), dtype=jnp.float32)
        return {'x': x, 'W_xy': W_xy, 'ig_w': ig_w, 'ig_b': ig_b, 'ag_w': ag_w, 'ag_b': ag_b, 'a_param': a_param, 'conv_w': conv_w, 'conv_b': conv_b, 'W_resid': W_resid}
    _L0_attn_in = _L0_attn_setup()

    def _L0_ffn_setup():
        import jax, jax.numpy as jnp
        import numpy as np
        DIM_IN = 256
        DIM_HIDDEN = 1024
        key = jax.random.key(seed)
        k_x, k_g, k_u, k_d = jax.random.split(key, 4)
        s_in = 1.0 / np.sqrt(DIM_IN)
        s_hid = 1.0 / np.sqrt(DIM_HIDDEN)
        x = jax.random.normal(k_x, (4, 256, DIM_IN), dtype=jnp.float32)
        w_gate = jax.random.uniform(k_g, (DIM_HIDDEN, DIM_IN), jnp.float32, -s_in, s_in)
        w_up = jax.random.uniform(k_u, (DIM_HIDDEN, DIM_IN), jnp.float32, -s_in, s_in)
        w_down = jax.random.uniform(k_d, (DIM_IN, DIM_HIDDEN), jnp.float32, -s_hid, s_hid)
        return {'x': x, 'w_gate': w_gate, 'w_up': w_up, 'w_down': w_down}
    _L0_ffn_in = _L0_ffn_setup()

    def _L1_attn_setup():
        import jax, jax.numpy as jnp
        import numpy as np
        B, S, D = (4, 512, 256)
        THETA = 10000.0
        LN_EPS = 1e-05

        def _layernorm(x, w, b):
            mu = jnp.mean(x, axis=-1, keepdims=True)
            var = jnp.mean(jnp.square(x - mu), axis=-1, keepdims=True)
            return (x - mu) * jax.lax.rsqrt(var + LN_EPS) * w + b

        def _rope_half(x):
            rot_dim = x.shape[-1] // 2
            seq = x.shape[-2]
            inv_freq = 1.0 / THETA ** (jnp.arange(0, rot_dim, 2, dtype=jnp.float32) / rot_dim)
            freqs = jnp.arange(seq, dtype=jnp.float32)[:, None] * inv_freq[None, :]
            freqs = jnp.repeat(freqs, 2, axis=-1)
            cos, sin = (jnp.cos(freqs), jnp.sin(freqs))
            xl, xr = (x[..., :rot_dim], x[..., rot_dim:])
            x1, x2 = (xl[..., 0::2], xl[..., 1::2])
            rh = jnp.stack((-x2, x1), axis=-1).reshape(xl.shape)
            return jnp.concatenate([xl * cos + rh * sin, xr], axis=-1)

        def _cos_sim(x):
            return x / jnp.linalg.norm(x, axis=-1, keepdims=True)
        key = jax.random.key(seed)
        k0, k1, k2 = jax.random.split(key, 3)
        X = jax.random.normal(k0, (B, S, D), jnp.float32)
        ln_w = jnp.ones((D,), jnp.float32)
        ln_b = jnp.zeros((D,), jnp.float32)
        W_in = jax.random.normal(k1, (D, 3 * D), jnp.float32) * D ** (-0.5)
        b_in = jnp.zeros((3 * D,), jnp.float32)
        W_out = jax.random.normal(k2, (D, D), jnp.float32) * D ** (-0.5)
        b_out = jnp.zeros((D,), jnp.float32)
        return {'X': X, 'ln_w': ln_w, 'ln_b': ln_b, 'W_in': W_in, 'b_in': b_in, 'W_out': W_out, 'b_out': b_out}
    _L1_attn_in = _L1_attn_setup()

    def _L1_ffn_setup():
        import jax, jax.numpy as jnp
        import numpy as np
        TOP_K = 2
        key = jax.random.key(seed)
        ks = jax.random.split(key, 7)
        B, S, H = (2, 256, 256)
        E, A, NS = (8, 64, 2048)
        x = jax.random.normal(ks[0], (B, S, H), jnp.float32)
        gate_w = jax.random.normal(ks[1], (E, H), jnp.float32) * 0.01
        W = jax.random.normal(ks[2], (H, H), jnp.float32) * 0.02
        atoms = jax.random.normal(ks[3], (A, NS), jnp.float32) * 0.02
        expert_atom_weights = jax.random.normal(ks[4], (E, A), jnp.float32) * 0.1
        importance = jax.random.normal(ks[5], (E, NS), jnp.float32) * 0.1
        mask_idx = jax.random.randint(ks[6], (NS,), 0, H * H, jnp.int32)
        return dict(x=x, gate_w=gate_w, W=W, atoms=atoms, expert_atom_weights=expert_atom_weights, importance=importance, mask_idx=mask_idx)
    _L1_ffn_in = _L1_ffn_setup()

    def _L2_attn_setup():
        import jax, jax.numpy as jnp
        import numpy as np
        B, T, D = (4, 256, 256)
        H = 16
        HD = D // H
        key = jax.random.key(seed)
        ks = jax.random.split(key, 10)
        s = 0.02
        return {'x': jax.random.normal(ks[0], (B, T, D), dtype=jnp.float32), 'Wq': jax.random.normal(ks[1], (D, D), dtype=jnp.float32) * s, 'bq': jnp.zeros((D,), dtype=jnp.float32), 'Wk': jax.random.normal(ks[2], (D, D), dtype=jnp.float32) * s, 'bk': jnp.zeros((D,), dtype=jnp.float32), 'Wv': jax.random.normal(ks[3], (D, D), dtype=jnp.float32) * s, 'bv': jnp.zeros((D,), dtype=jnp.float32), 'Wo': jax.random.normal(ks[4], (D, D), dtype=jnp.float32) * s, 'bo': jnp.zeros((D,), dtype=jnp.float32)}
    _L2_attn_in = _L2_attn_setup()

    def _L2_ffn_setup():
        import jax, jax.numpy as jnp
        import numpy as np
        D = 256
        F = 176
        E = 8
        K = 2
        FS = 352
        B, S = (2, 128)
        key = jax.random.key(seed)
        ks = jax.random.split(key, 9)
        sc = 0.02
        return {'x': jax.random.normal(ks[0], (B, S, D), dtype=jnp.float32), 'Wr': jax.random.normal(ks[1], (E, D), dtype=jnp.float32) * sc, 'Wg': jax.random.normal(ks[2], (E, F, D), dtype=jnp.float32) * sc, 'Wu': jax.random.normal(ks[3], (E, F, D), dtype=jnp.float32) * sc, 'Wd': jax.random.normal(ks[4], (E, D, F), dtype=jnp.float32) * sc, 'Wsg': jax.random.normal(ks[5], (FS, D), dtype=jnp.float32) * sc, 'Wsu': jax.random.normal(ks[6], (FS, D), dtype=jnp.float32) * sc, 'Wsd': jax.random.normal(ks[7], (D, FS), dtype=jnp.float32) * sc}
    _L2_ffn_in = _L2_ffn_setup()

    def _L3_attn_setup():
        import jax, jax.numpy as jnp
        import numpy as np
        import math
        D_MODEL = 256
        N_HEADS = 16
        D_HEAD = 128
        BATCH = 2
        SEQ = 256
        key = jax.random.key(seed)
        ks = jax.random.split(key, 5)
        std = 0.02
        x = jax.random.normal(ks[0], (BATCH, SEQ, D_MODEL), dtype=jnp.float32)
        W_Q = std * jax.random.normal(ks[1], (N_HEADS, D_HEAD, D_MODEL), dtype=jnp.float32)
        W_K = std * jax.random.normal(ks[2], (N_HEADS, D_HEAD, D_MODEL), dtype=jnp.float32)
        W_V = std * jax.random.normal(ks[3], (N_HEADS, D_HEAD, D_MODEL), dtype=jnp.float32)
        W_O = std * jax.random.normal(ks[4], (N_HEADS, D_MODEL, D_HEAD), dtype=jnp.float32)
        return {'x': x, 'W_Q': W_Q, 'W_K': W_K, 'W_V': W_V, 'W_O': W_O}
    _L3_attn_in = _L3_attn_setup()

    def _L3_ffn_setup():
        import jax, jax.numpy as jnp
        import numpy as np
        EPS = 1e-08

        def ternary_quantize(w):
            threshold = 0.7 * jnp.mean(jnp.abs(w), axis=-1, keepdims=True)
            q = jnp.where(w > threshold, 1.0, jnp.where(w < -threshold, -1.0, 0.0)).astype(w.dtype)
            return w + jax.lax.stop_gradient(q - w)
        key = jax.random.key(seed)
        k1, k2, k3 = jax.random.split(key, 3)
        B, S, D_in, D_out = (4, 256, 256, 256)
        x = jax.random.normal(k1, (B, S, D_in), dtype=jnp.float32)
        bound = np.sqrt(6.0 / D_in)
        weight = jax.random.uniform(k2, (D_out, D_in), dtype=jnp.float32, minval=-bound, maxval=bound)
        bias = jax.random.normal(k3, (D_out,), dtype=jnp.float32) * 0.01
        return {'x': x, 'weight': weight, 'bias': bias}
    _L3_ffn_in = _L3_ffn_setup()
    _d = {'L0_attn_x': _L0_attn_in['x'], 'L0_attn_W_xy': _L0_attn_in['W_xy'], 'L0_attn_ig_w': _L0_attn_in['ig_w'], 'L0_attn_ig_b': _L0_attn_in['ig_b'], 'L0_attn_ag_w': _L0_attn_in['ag_w'], 'L0_attn_ag_b': _L0_attn_in['ag_b'], 'L0_attn_a_param': _L0_attn_in['a_param'], 'L0_attn_conv_w': _L0_attn_in['conv_w'], 'L0_attn_conv_b': _L0_attn_in['conv_b'], 'L0_attn_W_resid': _L0_attn_in['W_resid'], 'L0_ffn_w_gate': _L0_ffn_in['w_gate'], 'L0_ffn_w_up': _L0_ffn_in['w_up'], 'L0_ffn_w_down': _L0_ffn_in['w_down'], 'L1_attn_ln_w': _L1_attn_in['ln_w'], 'L1_attn_ln_b': _L1_attn_in['ln_b'], 'L1_attn_W_in': _L1_attn_in['W_in'], 'L1_attn_b_in': _L1_attn_in['b_in'], 'L1_attn_W_out': _L1_attn_in['W_out'], 'L1_attn_b_out': _L1_attn_in['b_out'], 'L1_ffn_gate_w': _L1_ffn_in['gate_w'], 'L1_ffn_W': _L1_ffn_in['W'], 'L1_ffn_atoms': _L1_ffn_in['atoms'], 'L1_ffn_expert_atom_weights': _L1_ffn_in['expert_atom_weights'], 'L1_ffn_importance': _L1_ffn_in['importance'], 'L1_ffn_mask_idx': _L1_ffn_in['mask_idx'], 'L2_attn_Wq': _L2_attn_in['Wq'], 'L2_attn_bq': _L2_attn_in['bq'], 'L2_attn_Wk': _L2_attn_in['Wk'], 'L2_attn_bk': _L2_attn_in['bk'], 'L2_attn_Wv': _L2_attn_in['Wv'], 'L2_attn_bv': _L2_attn_in['bv'], 'L2_attn_Wo': _L2_attn_in['Wo'], 'L2_attn_bo': _L2_attn_in['bo'], 'L2_ffn_Wr': _L2_ffn_in['Wr'], 'L2_ffn_Wg': _L2_ffn_in['Wg'], 'L2_ffn_Wu': _L2_ffn_in['Wu'], 'L2_ffn_Wd': _L2_ffn_in['Wd'], 'L2_ffn_Wsg': _L2_ffn_in['Wsg'], 'L2_ffn_Wsu': _L2_ffn_in['Wsu'], 'L2_ffn_Wsd': _L2_ffn_in['Wsd'], 'L3_attn_W_Q': _L3_attn_in['W_Q'], 'L3_attn_W_K': _L3_attn_in['W_K'], 'L3_attn_W_V': _L3_attn_in['W_V'], 'L3_attn_W_O': _L3_attn_in['W_O'], 'L3_ffn_weight': _L3_ffn_in['weight'], 'L3_ffn_bias': _L3_ffn_in['bias']}
    _x0 = _d['L0_attn_x']
    _d['L0_attn_x'] = jax.random.normal(jax.random.fold_in(jax.random.key(seed), 1), (2, 512, 256), dtype=_x0.dtype)
    del _x0
    return _d

def reference(L0_attn_x, L0_attn_W_xy, L0_attn_ig_w, L0_attn_ig_b, L0_attn_ag_w, L0_attn_ag_b, L0_attn_a_param, L0_attn_conv_w, L0_attn_conv_b, L0_attn_W_resid, L0_ffn_w_gate, L0_ffn_w_up, L0_ffn_w_down, L1_attn_ln_w, L1_attn_ln_b, L1_attn_W_in, L1_attn_b_in, L1_attn_W_out, L1_attn_b_out, L1_ffn_gate_w, L1_ffn_W, L1_ffn_atoms, L1_ffn_expert_atom_weights, L1_ffn_importance, L1_ffn_mask_idx, L2_attn_Wq, L2_attn_bq, L2_attn_Wk, L2_attn_bk, L2_attn_Wv, L2_attn_bv, L2_attn_Wo, L2_attn_bo, L2_ffn_Wr, L2_ffn_Wg, L2_ffn_Wu, L2_ffn_Wd, L2_ffn_Wsg, L2_ffn_Wsu, L2_ffn_Wsd, L3_attn_W_Q, L3_attn_W_K, L3_attn_W_V, L3_attn_W_O, L3_ffn_weight, L3_ffn_bias):

    def _L0_attn_ref(x, W_xy, ig_w, ig_b, ag_w, ag_b, a_param, conv_w, conv_b, W_resid):
        import jax, jax.numpy as jnp
        import numpy as np
        B, S, H, R = (2, 512, 256, 256)
        NB, CW = (16, 4)
        BW = R // NB

        def _block_diag_linear(x, w, b):
            xb = x.reshape(x.shape[0], x.shape[1], NB, BW)
            out = jnp.einsum('bsni,nij->bsnj', xb, w) + b
            return out.reshape(x.shape)

        def _causal_conv1d(x, conv_w, conv_b):
            xp = jnp.pad(x, ((0, 0), (CW - 1, 0), (0, 0)))
            out = conv_b
            for i in range(CW):
                out = out + conv_w[i] * xp[:, i:i + x.shape[1], :]
            return out

        def _rg_lru_scan(x, x_gate_pre, a_gate_pre, a_param):
            gate_x = jax.nn.sigmoid(x_gate_pre)
            gate_a = jax.nn.sigmoid(a_gate_pre)
            log_a = -8.0 * gate_a * jax.nn.softplus(a_param)
            a = jnp.exp(log_a)
            multiplier = jnp.sqrt(-jnp.expm1(2.0 * log_a))
            norm_x = x * gate_x * multiplier

            def combine(c1, c2):
                a1, b1 = c1
                a2, b2 = c2
                return (a1 * a2, a2 * b1 + b2)
            _, h = jax.lax.associative_scan(combine, (a, norm_x), axis=1)
            return h
        xy = jnp.einsum('bsh,rh->bsr', x, W_xy)
        xr, y = jnp.split(xy, 2, axis=-1)
        xc = _causal_conv1d(xr, conv_w, conv_b)
        x_gate_pre = _block_diag_linear(xc, ig_w, ig_b)
        a_gate_pre = _block_diag_linear(xc, ag_w, ag_b)
        h = _rg_lru_scan(xc, x_gate_pre, a_gate_pre, a_param)
        out = jnp.einsum('bsr,hr->bsh', jax.nn.gelu(y, approximate=False) * h, W_resid)
        return out

    def _L0_ffn_ref(x, w_gate, w_up, w_down):
        import jax, jax.numpy as jnp
        import numpy as np
        DIM_IN = 256
        DIM_HIDDEN = 1024
        gate = jnp.einsum('bsd,hd->bsh', x, w_gate)
        up = jnp.einsum('bsd,hd->bsh', x, w_up)
        gated = jax.nn.silu(gate) * up
        return jnp.einsum('bsh,dh->bsd', gated, w_down)

    def _L1_attn_ref(X, ln_w, ln_b, W_in, b_in, W_out, b_out):
        import jax, jax.numpy as jnp
        import numpy as np
        B, S, D = (4, 512, 256)
        THETA = 10000.0
        LN_EPS = 1e-05

        def _layernorm(x, w, b):
            mu = jnp.mean(x, axis=-1, keepdims=True)
            var = jnp.mean(jnp.square(x - mu), axis=-1, keepdims=True)
            return (x - mu) * jax.lax.rsqrt(var + LN_EPS) * w + b

        def _rope_half(x):
            rot_dim = x.shape[-1] // 2
            seq = x.shape[-2]
            inv_freq = 1.0 / THETA ** (jnp.arange(0, rot_dim, 2, dtype=jnp.float32) / rot_dim)
            freqs = jnp.arange(seq, dtype=jnp.float32)[:, None] * inv_freq[None, :]
            freqs = jnp.repeat(freqs, 2, axis=-1)
            cos, sin = (jnp.cos(freqs), jnp.sin(freqs))
            xl, xr = (x[..., :rot_dim], x[..., rot_dim:])
            x1, x2 = (xl[..., 0::2], xl[..., 1::2])
            rh = jnp.stack((-x2, x1), axis=-1).reshape(xl.shape)
            return jnp.concatenate([xl * cos + rh * sin, xr], axis=-1)

        def _cos_sim(x):
            return x / jnp.linalg.norm(x, axis=-1, keepdims=True)
        h = _layernorm(X, ln_w, ln_b)
        qkv = h @ W_in + b_in
        Q, K, V = jnp.split(qkv, 3, axis=-1)
        Q = _rope_half(Q)
        K = _rope_half(K)
        A = jnp.sum(_cos_sim(K) * V, axis=-2)
        Y = A[:, None, :] * Q
        Y = Y @ W_out + b_out
        return Y + X

    def _L1_ffn_ref(x, gate_w, W, atoms, expert_atom_weights, importance, mask_idx):
        import jax, jax.numpy as jnp
        import numpy as np
        TOP_K = 2
        B, S, H = x.shape
        xt = x.reshape(-1, H)
        logits = jnp.clip(xt @ gate_w.T, -50.0, 50.0)
        top_w, top_idx = jax.lax.top_k(logits, TOP_K)
        rw = jax.nn.softmax(top_w, axis=-1)
        deltas = jax.nn.softmax(expert_atom_weights, axis=-1) @ atoms
        weighted = deltas * jax.nn.sigmoid(importance)
        rows = mask_idx // H
        cols = mask_idx % H
        vals = jnp.einsum('tk,tks->ts', rw, weighted[top_idx])
        xg = xt[:, cols]
        contrib = jax.ops.segment_sum((xg * vals).T, rows, num_segments=H)
        out = xt @ W.T + contrib.T
        return out.reshape(B, S, H)

    def _L2_attn_ref(x, Wq, bq, Wk, bk, Wv, bv, Wo, bo):
        import jax, jax.numpy as jnp
        import numpy as np
        B, T, D = (4, 256, 256)
        H = 16
        HD = D // H
        b, t, _ = x.shape

        def split_heads(y):
            return y.reshape(b, t, H, HD).transpose(0, 2, 1, 3)
        q = split_heads(x @ Wq.T + bq)
        k = split_heads(x @ Wk.T + bk)
        v = split_heads(x @ Wv.T + bv)
        scale = 1.0 / jnp.sqrt(jnp.float32(HD))
        scores = jnp.einsum('bhqd,bhkd->bhqk', q, k) * scale
        causal = jnp.triu(jnp.ones((t, t), dtype=bool), k=1)
        scores = jnp.where(causal, -jnp.inf, scores)
        attn = jax.nn.softmax(scores, axis=-1)
        ctx = jnp.einsum('bhqk,bhkd->bhqd', attn, v)
        ctx = ctx.transpose(0, 2, 1, 3).reshape(b, t, D)
        return ctx @ Wo.T + bo

    def _L2_ffn_ref(x, Wr, Wg, Wu, Wd, Wsg, Wsu, Wsd):
        import jax, jax.numpy as jnp
        import numpy as np
        D = 256
        F = 176
        E = 8
        K = 2
        FS = 352
        B, S = (2, 128)
        silu = jax.nn.silu
        sg = silu(jnp.einsum('bsd,fd->bsf', x, Wsg))
        su = jnp.einsum('bsd,fd->bsf', x, Wsu)
        shared_out = jnp.einsum('bsf,df->bsd', sg * su, Wsd)
        logits = jnp.einsum('bsd,ed->bse', x, Wr)
        scores = jax.nn.softmax(logits, axis=-1)
        topk_scores, topk_idx = jax.lax.top_k(scores, K)
        w_full = jnp.sum(jax.nn.one_hot(topk_idx, E, dtype=x.dtype) * topk_scores[..., None], axis=-2)
        g = silu(jnp.einsum('bsd,efd->bsef', x, Wg))
        u = jnp.einsum('bsd,efd->bsef', x, Wu)
        out_e = jnp.einsum('bsef,edf->bsed', g * u, Wd)
        routed_out = jnp.einsum('bsed,bse->bsd', out_e, w_full)
        return routed_out + shared_out

    def _L3_attn_ref(x, W_Q, W_K, W_V, W_O):
        import jax, jax.numpy as jnp
        import numpy as np
        import math
        D_MODEL = 256
        N_HEADS = 16
        D_HEAD = 128
        BATCH = 2
        SEQ = 256
        d_head = W_Q.shape[1]
        seq_len = x.shape[1]
        scale = 1.0 / math.sqrt(d_head)
        q = jnp.einsum('bsd,hed->bhse', x, W_Q)
        k = jnp.einsum('bsd,hed->bhse', x, W_K)
        v = jnp.einsum('bsd,hed->bhse', x, W_V)
        scores = jnp.einsum('bhse,bhme->bhsm', q, k) * scale
        causal = jnp.triu(jnp.ones((seq_len, seq_len), dtype=bool), k=1)
        scores = jnp.where(causal, jnp.float32(-1000000000.0), scores)
        pattern = jax.nn.softmax(scores, axis=-1)
        z = jnp.einsum('bhsm,bhme->bhse', pattern, v)
        out = jnp.einsum('bhse,hde->bsd', z, W_O)
        return out

    def _L3_ffn_ref(x, weight, bias):
        import jax, jax.numpy as jnp
        import numpy as np
        EPS = 1e-08

        def ternary_quantize(w):
            threshold = 0.7 * jnp.mean(jnp.abs(w), axis=-1, keepdims=True)
            q = jnp.where(w > threshold, 1.0, jnp.where(w < -threshold, -1.0, 0.0)).astype(w.dtype)
            return w + jax.lax.stop_gradient(q - w)
        q_weight = ternary_quantize(weight)
        return jnp.einsum('bsi,oi->bso', x, q_weight) + bias
    x = L0_attn_x
    x = x + 0.5 * _L0_ffn_ref(_layernorm(x, axis=-1), L0_ffn_w_gate, L0_ffn_w_up, L0_ffn_w_down)
    x = x + _L0_attn_ref(_layernorm(x, axis=-1), L0_attn_W_xy, L0_attn_ig_w, L0_attn_ig_b, L0_attn_ag_w, L0_attn_ag_b, L0_attn_a_param, L0_attn_conv_w, L0_attn_conv_b, L0_attn_W_resid)
    x = x + 0.5 * _L0_ffn_ref(_layernorm(x, axis=-1), L0_ffn_w_gate, L0_ffn_w_up, L0_ffn_w_down)
    x = x + 0.5 * _L1_ffn_ref(_layernorm(x, axis=-1), L1_ffn_gate_w, L1_ffn_W, L1_ffn_atoms, L1_ffn_expert_atom_weights, L1_ffn_importance, L1_ffn_mask_idx)
    x = x + _L1_attn_ref(_layernorm(x, axis=-1), L1_attn_ln_w, L1_attn_ln_b, L1_attn_W_in, L1_attn_b_in, L1_attn_W_out, L1_attn_b_out)
    x = x + 0.5 * _L1_ffn_ref(_layernorm(x, axis=-1), L1_ffn_gate_w, L1_ffn_W, L1_ffn_atoms, L1_ffn_expert_atom_weights, L1_ffn_importance, L1_ffn_mask_idx)
    x = x + 0.5 * _L2_ffn_ref(_layernorm(x, axis=-1), L2_ffn_Wr, L2_ffn_Wg, L2_ffn_Wu, L2_ffn_Wd, L2_ffn_Wsg, L2_ffn_Wsu, L2_ffn_Wsd)
    x = x + _L2_attn_ref(_layernorm(x, axis=-1), L2_attn_Wq, L2_attn_bq, L2_attn_Wk, L2_attn_bk, L2_attn_Wv, L2_attn_bv, L2_attn_Wo, L2_attn_bo)
    x = x + 0.5 * _L2_ffn_ref(_layernorm(x, axis=-1), L2_ffn_Wr, L2_ffn_Wg, L2_ffn_Wu, L2_ffn_Wd, L2_ffn_Wsg, L2_ffn_Wsu, L2_ffn_Wsd)
    x = x + 0.5 * _L3_ffn_ref(_layernorm(x, axis=-1), L3_ffn_weight, L3_ffn_bias)
    x = x + _L3_attn_ref(_layernorm(x, axis=-1), L3_attn_W_Q, L3_attn_W_K, L3_attn_W_V, L3_attn_W_O)
    x = x + 0.5 * _L3_ffn_ref(_layernorm(x, axis=-1), L3_ffn_weight, L3_ffn_bias)
    return x

_drawn_inputs = setup_inputs


def setup_inputs(seed=0):
    import zlib

    import numpy as np

    out = dict(_drawn_inputs(seed))
    spreads = {'L0_attn_ig_b': (0.0, 0.8),
     'L0_attn_ag_b': (0.0, 0.8),
     'L0_attn_conv_b': (0.0, 0.1),
     'L1_attn_ln_w': (1.0, 0.2),
     'L1_attn_ln_b': (0.0, 0.1),
     'L1_attn_b_in': (0.0, 0.1),
     'L1_attn_b_out': (0.0, 0.1),
     'L2_attn_bq': (0.0, 0.8),
     'L2_attn_bk': (0.0, 2.0),
     'L2_attn_bv': (0.0, 0.8),
     'L2_attn_bo': (0.0, 0.273)}
    factors = {'L0_attn_ig_w': 8.0,
     'L0_attn_ag_w': 8.0,
     'L0_attn_conv_w': 5.523,
     'L1_ffn_gate_w': 8.0,
     'L1_ffn_atoms': 8.0,
     'L1_ffn_expert_atom_weights': 8.0,
     'L1_ffn_importance': 8.0,
     'L2_attn_Wq': 8.0,
     'L2_attn_Wk': 8.0,
     'L2_attn_Wv': 8.0,
     'L2_attn_Wo': 6.154,
     'L2_ffn_Wr': 8.0,
     'L2_ffn_Wg': 8.0,
     'L2_ffn_Wu': 8.0,
     'L2_ffn_Wd': 8.0,
     'L2_ffn_Wsg': 8.0,
     'L2_ffn_Wsu': 8.0,
     'L2_ffn_Wsd': 8.0,
     'L3_attn_W_Q': 8.0,
     'L3_attn_W_K': 8.0,
     'L3_attn_W_V': 8.0,
     'L3_attn_W_O': 8.0,
     'L3_ffn_bias': 64.0}
    for name, (base, spread) in spreads.items():
        noise = np.random.default_rng([zlib.crc32(name.encode()), seed]).standard_normal(out[name].shape)
        drawn = base * np.exp(spread * noise) if base else spread * noise
        out[name] = jnp.asarray(drawn.astype(out[name].dtype))
    for name, factor in factors.items():
        out[name] = (out[name] * factor).astype(out[name].dtype)
    return out
```

```python
from contextlib import ExitStack

import numpy as np

import concourse.bass as bass
from concourse import mybir

ALU = mybir.AluOpType
ACT = mybir.ActivationFunctionType
AX_X = mybir.AxisListType.X
F32 = mybir.dt.float32
F32R = mybir.dt.float32r
BF16 = mybir.dt.bfloat16
I32 = mybir.dt.int32
U32 = mybir.dt.uint32

P = 128
NB = 2
T = 512
D = 256
TT = T // P
DC = D // P
EPS = 1e-5
NEG = -1e30

N_UNITS = 24
FFN0, RGLRU, MOE1, LIN1, MOE2, ATT2, FFN3, ATT3 = "ffn0", "rglru", "moe1", "lin1", "moe2", "att2", "ffn3", "att3"
SUBLAYERS = [FFN0, RGLRU, FFN0, MOE1, LIN1, MOE1, MOE2, ATT2, MOE2, FFN3, ATT3, FFN3]
KIND = [SUBLAYERS[u // 2] for u in range(N_UNITS)]

HID0 = 1024
E = 8
NS = 2048
NA = 64
FE, FS = 176, 352
CH0 = HID0 // P
CH2 = -(-(E * FE + FS) // P)
H = 16
HD2 = D // H
HD3 = 128
SCALE2 = float(HD2) ** -0.5
SCALE3 = float(HD3) ** -0.5

SLOT = 1024
W_GATE, W_UP, W_DOWN, W_IND = 0, DC * P, 2 * DC * P, 2 * DC * P + D
PAIR_COLS = (2 * DC * 2 * P, DC * 2 * P)
RES = {"rglru": (2048, 2), "wt": (2 * D, 2), "lin1": (2304, 4), "att2": (2048, 2), "wo3": (H * D, 4)}
RES_AT = {"rglru": 0, "wt": E * 2 * D, "lin1": 0, "att2": 0, "wo3": 0}

ORDER = [("u", 0), ("u", 1), ("r", "rglru"), ("r", "wt"), ("u", 4), ("u", 5), ("r", "lin1"), ("u", 12), ("u", 13),
         ("r", "att2"), ("u", 16), ("u", 17), ("r", "wo3"), ("u", 20), ("u", 21)]
CHUNKS = {FFN0: CH0, MOE2: CH2, ATT3: H}
RAW0, RING0, FFN_AT = {}, {}, {}
_raw = _ring = _ffn = 0
for _kind, _what in ORDER:
    RAW0[_what] = _raw
    if _kind == "u":
        RING0[_what] = _ring
        _n = CHUNKS[KIND[_what]]
        _ring += _n
        if KIND[_what] != ATT3:
            FFN_AT[_what] = _ffn
            _ffn += _n
        _raw += _n
    else:
        _raw += RES[_what][1]

KEYS = [P * (i + 1) for i in range(TT)]
S_COLS = [max(2 * P, k) for k in KEYS]
S_AT = [(3, 0), (3, 256), (4, 0), (5, 0)]
P_AT = [sum(KEYS[:i]) for i in range(TT + 1)]
PT_N = [T - P * kb for kb in range(TT)]
PT_AT = [sum(PT_N[:i]) for i in range(TT + 1)]
FILLS = [[0], [1], [2, 3]]


def build(nc, a, out, stop=N_UNITS):
    with ExitStack() as ctx:
        def sb(name, shape, dt=F32):
            return ctx.enter_context(nc.sbuf_tensor(name, shape, dt))

        sems = {}

        def sem(name):
            if name not in sems:
                sems[name] = ctx.enter_context(nc.semaphore(name))
            return sems[name]

        def positive(count):
            return not isinstance(count, int) or count > 0

        ps = ctx.enter_context(nc.psum_tensor("ps", [P, 8, 512], F32))

        x = sb("x", [P, NB * TT, D])
        xn = sb("xn", [P, NB, TT, D])
        xh = sb("xh", [P, NB, DC, T], F32R)
        xl = sb("xl", [P, NB, DC, T], F32R)
        stats = sb("stats", [P, NB, TT, 6])
        mv = sb("mv", [P, NB, TT, 2])
        veps = sb("veps", [P, NB, TT])
        rstd = sb("rstd", [P, NB, TT])
        nhalf = sb("nhalf", [P, TT])
        raw = sb("raw", [P, 2, SLOT])
        wh = sb("wh", [P, 2, SLOT], F32R)
        wl = sb("wl", [P, 2, SLOT], F32R)
        rch = sb("rch", [P, 2304], F32R)
        rcl = sb("rcl", [P, 2304], F32R)
        drh = sb("drh", [P, E * 2 * D + 2 * D], F32R)
        drl = sb("drl", [P, E * 2 * D + 2 * D], F32R)
        qt = sb("qt", [P, DC, D], F32R)
        ident = sb("ident", [P, P])
        identb = sb("identb", [P, P], BF16)
        tri = sb("tri", [P, P])
        maskcol = sb("maskcol", [P, P])
        maskb = sb("maskb", [P, P], BF16)
        ones = sb("ones", [P, P])
        iota8 = sb("iota8", [P, TT, E])
        headmask = sb("headmask", [P, 8])
        router_w = sb("router_w", [P, 2, DC, E])
        bias3 = sb("bias3", [P, D])
        def f32(ap):
            return ap.bitcast(F32)

        block = ctx.enter_context(nc.Block())

        def sublayer_tensors(**shapes):
            with ExitStack() as own:
                return [own.enter_context(nc.sbuf_tensor(name, shape, dt)) for name, (shape, dt) in shapes.items()]

        small = sb("small", [P, 512])
        lg = small[:, 0:32].rearrange("p (i e) -> p i e", i=TT)
        top8 = small[:, 32:64].rearrange("p (i e) -> p i e", i=TT)
        dl = small[:, 64:96].rearrange("p (i e) -> p i e", i=TT)
        ex = small[:, 96:128].rearrange("p (i e) -> p i e", i=TT)
        m0 = small[:, 128:160].rearrange("p (i e) -> p i e", i=TT)
        m1 = small[:, 160:192].rearrange("p (i e) -> p i e", i=TT)
        mask = small[:, 192:224].rearrange("p (i e) -> p i e", i=TT)
        wsel = small[:, 224:256].rearrange("p (i e) -> p i e", i=TT)
        w9 = small[:, 256:256 + TT * (E + 1)].rearrange("p (i e) -> p i e", i=TT)
        idxf = small[:, 296:304].rearrange("p (i e) -> p i e", i=TT)
        rsum = small[:, 304:308]
        rinv = small[:, 308:312]
        h_sum, h_inv, h_max, h_nmx = [small[:, 400 + 8 * k:408 + 8 * k].rearrange("p (h i) -> p h i", h=2) for k in range(4)]
        idx8 = sb("idx8", [P, TT, 8], U32)
        rwh = sb("rwh", [P, 2, DC, E], F32R)
        rwl = sb("rwl", [P, 2, DC, E], F32R)
        rgp = sb("rgp", [P, DC, 16])
        lin_cols = sb("lin_cols", [P, 8])
        lin_bout = sb("lin_bout", [P, D])
        att_cols = sb("att_cols", [P, 4])
        att_bo = sb("att_bo", [P, D])
        d_desti = sb("d_desti", [P, 16], U32)

        ffn_hh, ffn_hl, wth_, wtl_, ffn_s, ffn_hf = sublayer_tensors(
            ffn_hh=([P, 2, T], F32R), ffn_hl=([P, 2, T], F32R), ffn_wth=([E + 1, T], F32R), ffn_wtl=([E + 1, T], F32R),
            ffn_s=([P, 2, T], F32), ffn_hf=([P, 2, T], F32))
        wth, wtl = wth_[:, :], wtl_[:, :]
        rg_xp, rg_xc, rg_gy, rg_ga, rg_a, rg_ch, rg_cl, rg_gh, rg_gl = sublayer_tensors(
            rg_xp=([P, DC, T + 4], F32), rg_xc=([P, DC, T], F32), rg_gy=([P, DC, T], F32), rg_ga=([P, DC, T], F32),
            rg_a=([P, DC, T], F32), rg_ch=([P, DC, T], F32R), rg_cl=([P, DC, T], F32R), rg_gh=([P, DC, T], F32R),
            rg_gl=([P, DC, T], F32R))
        rg_gx = rg_xp[:, :, 4:T + 4]
        rg_th = rg_ga
        (lin_tok, lin_feat, lin_bkv, lin_xn, lin_tmp, lin_kv, lin_kr, lin_ks, lin_qa, lin_qb, lin_qf, lin_hh, lin_hl,
         lin_qh, lin_ql) = sublayer_tensors(
            lin_tok=([P, 2, TT, P], F32),
            lin_feat=([P, 2, T], F32),
            lin_bkv=([P, 2 * D], F32), lin_xn=([P, TT, D], F32), lin_tmp=([P, DC, T], F32), lin_kv=([P, TT, 2 * D], F32),
            lin_kr=([P, TT, P], F32), lin_ks=([P, TT, P], F32), lin_qa=([P, T], F32), lin_qb=([P, T], F32),
            lin_qf=([P, DC, T], F32), lin_hh=([P, DC, T], F32R), lin_hl=([P, DC, T], F32R),
            lin_qh=([P, DC, T], F32R), lin_ql=([P, DC, T], F32R))
        lin_prod = lin_xn
        VS = P + HD2
        (a2_qh, a2_ql, a2_kh, a2_kl, a2_mh, a2_ml, a2_vh, a2_vl, a2_pth, a2_ptl, a2_p, a2_vf, a2_bv) = sublayer_tensors(
            a2_qh=([P, DC, T], F32R), a2_ql=([P, DC, T], F32R), a2_kh=([P, DC, T], F32R), a2_kl=([P, DC, T], F32R),
            a2_mh=([P, 2, T], F32R), a2_ml=([P, 2, T], F32R), a2_vh=([P, TT, 8, VS], F32R), a2_vl=([P, TT, 8, VS], F32R),
            a2_pth=([P, PT_AT[TT]], F32R), a2_ptl=([P, PT_AT[TT]], F32R), a2_p=([P, 2, P_AT[TT]], F32),
            a2_vf=([P, TT, D], F32), a2_bv=([P, D], F32))
        (a3_qh, a3_ql, a3_kh, a3_kl, a3_vh, a3_vl, a3_pth, a3_ptl, a3_zh, a3_zl, a3_p) = sublayer_tensors(
            a3_qh=([P, T], F32R), a3_ql=([P, T], F32R), a3_kh=([P, T], F32R), a3_kl=([P, T], F32R),
            a3_vh=([P, TT, 2 * HD3], F32R), a3_vl=([P, TT, 2 * HD3], F32R), a3_pth=([P, PT_AT[TT]], F32R),
            a3_ptl=([P, PT_AT[TT]], F32R), a3_zh=([P, T], F32R), a3_zl=([P, T], F32R), a3_p=([P, 2, P_AT[TT]], F32))
        (d_zero, d_back, d_rowi, d_row, d_eq, d_atoms, d_imp, d_col, d_work, d_wb, d_small, d_tri, d_q3, d_q3n, d_q3t) = sublayer_tensors(
            d_zero=([P, 1056], F32), d_back=([P, 2, NS], F32), d_rowi=([P, NS], I32), d_row=([P, NS], F32),
            d_eq=([P, 2, NS], BF16), d_atoms=([NA, NS], F32), d_imp=([P, P], F32), d_col=([P, 5, 16], I32),
            d_work=([P, 6, P], F32), d_wb=([P, 16, 25], BF16), d_small=([P, 256], F32), d_tri=([P, 2, P], BF16),
            d_q3=([P, DC, D], F32), d_q3n=([P, DC, D], F32), d_q3t=([P, DC, D], F32))

        def mm3(pe, o, l, r, start, stop):
            pe.matmul(o, l[0], r[0], start=start, stop=False, skip_group_check=True)
            pe.matmul(o, l[0], r[1], start=False, stop=False, skip_group_check=True)
            return pe.matmul(o, l[1], r[0], start=False, stop=stop, skip_group_check=True)

        def mm3c(pe, o, ls, rs):
            for c in range(len(ls)):
                last = mm3(pe, o, ls[c], rs[c], c == 0, c == len(ls) - 1)
            return last

        def acc(t):
            return ps[:, 6 + t // 2, (t % 2) * D:(t % 2 + 1) * D]

        def xT(b, c):
            return xh[:, b, c, :], xl[:, b, c, :]

        def xTt(b, c, t):
            return xh[:, b, c, t * P:(t + 1) * P], xl[:, b, c, t * P:(t + 1) * P]

        def rc(at, n, k=P):
            return rch[0:k, at:at + n], rcl[0:k, at:at + n]

        def dr(at, n):
            return drh[:, at:at + n], drl[:, at:at + n]

        def dve_stats(v, u):
            if u >= stop:
                return
            b = u % 2
            if u < 2:
                v.wait_ge(sem(f"x_in{b}"), 16)
            else:
                v.wait_ge(sem("x_res"), 4 * (u - 1))
            for i in range(TT):
                v.bn_stats(stats[:, b, i, :], x[:, TT * b + i, :]).then_inc(sem("ln_stats"), 1)
            for i in range(TT):
                v.wait_ge(sem("ln_stats"), TT * u + i + 1)
                v.bn_aggr(mv[:, b, i, :], stats[:, b, i, :]).then_inc(sem("ln_aggr"), 1)

        def dve_norm(v, u):
            if u >= stop:
                return
            b = u % 2
            v.wait_ge(sem("ln_rstd"), u + 1)
            if positive(2 * (u - 1)):
                v.wait_ge(sem("ln_T"), 2 * (u - 1))
            for i in range(TT):
                v.tensor_scalar(xn[:, b, i, :], x[:, TT * b + i, :], mv[:, b, i, 0:1], rstd[:, b, i:i + 1],
                                ALU.subtract, ALU.mult).then_inc(sem("ln_xn"), 1)

        def dve_ln(v, u):
            dve_stats(v, u)
            dve_norm(v, u)

        def pool_ln(g, u):
            if u >= stop:
                return
            b = u % 2
            g.wait_ge(sem("const_set"), 1)
            g.wait_ge(sem("ln_aggr"), TT * (u + 1))
            g.tensor_scalar(veps[:, b, :], mv[:, b, :, 1], EPS, 1.0, ALU.add, ALU.mult).then_inc(sem("ln_veps"), 1)
            g.wait_ge(sem("ln_veps"), u + 1)
            g.tensor_tensor(rstd[:, b, :], veps[:, b, :], nhalf[:, :], ALU.pow).then_inc(sem("ln_rstd"), 1)

        def pe_T(pe, u):
            if u >= stop:
                return
            b = u % 2
            pe.wait_ge(sem("const_ident"), 1)
            pe.wait_ge(sem("ln_xn"), TT * (u + 1))
            if positive(2 * u):
                pe.wait_ge(sem("ln_lo"), 2 * u)
            for c in range(DC):
                for i in range(TT):
                    last = pe.transpose(ps[:, c, i * P:(i + 1) * P], xn[:, b, i, c * P:(c + 1) * P], ident[:, :])
                last.then_inc(sem("ln_T"), 1)

        def act_T(s, u):
            if u >= stop:
                return
            b = u % 2
            for c in range(DC):
                s.wait_ge(sem("ln_T"), 2 * u + c + 1)
                s.activation(xh[:, b, c, :], ps[:, c, :], ACT.Copy).then_inc(sem("ln_hi"), 1)

        def dve_T(v, u):
            if u >= stop:
                return
            b = u % 2
            for c in range(DC):
                v.wait_ge(sem("ln_hi"), 2 * u + c + 1)
                v.tensor_tensor(xl[:, b, c, :], ps[:, c, :], f32(xh[:, b, c, :]), ALU.subtract)\
                    .then_inc(sem("ln_lo"), 1)

        def pe_ready(pe, u):
            pe.wait_ge(sem("ln_lo"), 2 * (u + 1))

        def dve_residual(v, u, scale, ready):
            b = u % 2
            for t in range(TT):
                if t % 2 == 0:
                    name, value = ready[t // 2]
                    v.wait_ge(sem(name), value)
                if KIND[u] == MOE1:
                    v.wait_ge(sem("moe_acc"), 2 * TT * (E // 2) * (MOE_AT[u] + 1))
                xt = x[:, TT * b + t, :]
                v.scalar_tensor_tensor(out=xt, in0=acc(t), scalar=scale, in1=xt, op0=ALU.mult, op1=ALU.add)\
                    .then_inc(sem("x_res"), 1)

        def sp_chunk(sp, r, p, src, cols):
            if positive(r - 1):
                sp.wait_ge(sem("w_split"), r - 1)
            sp.dma_start(raw[:, p, 0:cols], src).then_inc(sem(f"w_raw{p}"), 16)

        def pool_split(g, r, half, p, n, oh, ol, at=0):
            if half is not None:
                g.wait_ge(sem(f"w_raw{p}"), half * 16 + 16)
            if not isinstance(r, int):
                g.sem_inc(sem("pool_turn"), 1)
            g.tensor_scalar(oh, raw[:, p, at:n], 1.0, 1.0, ALU.mult, ALU.mult).then_inc(sem("w_hi"), 1)
            g.wait_ge(sem("w_hi"), r + 1)
            g.tensor_tensor(ol, raw[:, p, at:n], f32(oh), ALU.subtract).then_inc(sem("w_split"), 1)

        def chunk_cols(u, p):
            return PAIR_COLS[p] if KIND[u] == ATT3 else (W_DOWN + D if KIND[u] == FFN0 else W_IND + P)

        def sp_chunks(sp, u, i, p):
            r = RAW0[u] + p + i * 2
            n = chunk_cols(u, p)
            if KIND[u] == ATT3:
                src = a["qk3" if p == 0 else "v3"]
                k = i
            else:
                src = a["w0" if KIND[u] == FFN0 else "w2"]
                k = i * 2 + p
            sp_chunk(sp, r, p, src[bass.ds(k, 1)].rearrange("a p n -> p (a n)"), n)

        def pool_chunks(g, u, i, p):
            r, ring = RAW0[u] + p + i * 2, RING0[u] + p + i * 2
            n = chunk_cols(u, p)
            if KIND[u] != ATT3:
                g.wait_ge(sem(f"w_raw{p}"), i * 16 + 8 * RAW0[u] + 16)
                done = FFN_AT[u] + p + i * 2 - 1
                if positive(done):
                    g.wait_ge(sem("ffn_up"), done)
                if not isinstance(i, int):
                    g.sem_inc(sem("pool_turn"), 1)
                g.tensor_scalar(wh[:, p, 0:W_DOWN], raw[:, p, 0:W_DOWN], 1.0, 1.0, ALU.mult, ALU.mult)\
                    .then_inc(sem("w_gu_hi"), 1)
                g.wait_ge(sem("w_gu_hi"), done + 2)
                g.tensor_tensor(wl[:, p, 0:W_DOWN], raw[:, p, 0:W_DOWN], f32(wh[:, p, 0:W_DOWN]), ALU.subtract)\
                    .then_inc(sem("w_gu"), 1)
                if positive(ring - 1):
                    g.wait_ge(sem("w_used"), ring - 1)
                pool_split(g, r, None, p, n, wh[:, p, W_DOWN:n], wl[:, p, W_DOWN:n], W_DOWN)
                return
            if not (isinstance(i, int) and i == 0):
                g.wait_ge(sem("at_fill"), A3_FILL[u] + 2 + (4, 2)[p] - BODY + i * BODY)
            elif u == 21:
                g.wait_ge(sem("at_fill"), A3_FILL[20] + 2 + (4, 2)[p] + 7 * BODY)
            else:
                if positive(ring - 1):
                    g.wait_ge(sem("w_used"), ring - 1)
            pool_split(g, r, i + RAW0[u] // 2, p, n, wh[:, p, 0:n], wl[:, p, 0:n])

        def sp_resident(sp, name):
            cols, k = RES[name]
            n = cols // k
            for j in range(k):
                sp_chunk(sp, RAW0[name] + j, j % 2, a[name][:, j * n:(j + 1) * n], n)

        def pool_resident(g, name, done_unit=None):
            cols, k = RES[name]
            n, at = cols // k, RES_AT[name]
            dh, dlo = (drh, drl) if name in ("wt", "wo3") else (rch, rcl)
            if done_unit is not None:
                g.wait_ge(sem("x_res"), 4 * (done_unit + 1))
            for j in range(k):
                pool_split(g, RAW0[name] + j, (RAW0[name] + j) // 2, j % 2, n,
                           dh[:, at + j * n:at + (j + 1) * n], dlo[:, at + j * n:at + (j + 1) * n])

        def w(p, at, n=P):
            return wh[:, p, at:at + n], wl[:, p, at:at + n]

        ROUTED = [u for u in range(N_UNITS) if KIND[u] in (MOE1, MOE2)]
        MOE_AT = {u: n for n, u in enumerate(v for v in range(N_UNITS) if KIND[v] == MOE1)}
        MOE2_AT = {u: n for n, u in enumerate(v for v in range(N_UNITS) if KIND[v] == MOE2)}
        R_OPS = 18

        def rep(ap, n=E):
            return ap.to_broadcast([P, TT, n])

        def pe_logits(pe, u, bank):
            b, layer = u % 2, 0 if KIND[u] == MOE1 else 1
            pe.wait_ge(sem("const_router"), 1)
            for t in range(TT):
                for c in range(DC):
                    rh, rl = rwh[:, layer, c, :], rwl[:, layer, c, :]
                    last = mm3(pe, ps[:, bank, t * E:(t + 1) * E], xTt(b, c, t), (rh, rl), c == 0, c == DC - 1)
            last.then_inc(sem("rt_logits"), 1)

        def dve_router(v, u, bank):
            n = ROUTED.index(u)
            base = R_OPS * n
            count = [base]

            def then(ins):
                ins.then_inc(sem("rt_step"), 1)
                count[0] += 1

            def settled():
                v.wait_ge(sem("rt_step"), count[0])

            v.wait_ge(sem("rt_logits"), n + 1)
            pl = ps[:, bank, 0:TT * E].rearrange("p (i e) -> p i e", i=TT)
            if KIND[u] == MOE1:
                then(v.tensor_scalar(lg, pl, 50.0, -50.0, ALU.min, ALU.max))
            else:
                then(v.tensor_copy(lg, pl))
            settled()
            for i in range(TT):
                then(v.max(top8[:, i, :], lg[:, i, :]))
            settled()
            then(v.tensor_tensor(dl, lg, rep(top8[:, :, 0:1]), ALU.subtract))
            for i in range(TT):
                then(v.max_index(idx8[:, i, :], top8[:, i, :], lg[:, i, :]))
            settled()
            then(v.tensor_copy(idxf, idx8[:, :, 0:2]))
            settled()
            v.wait_ge(sem("const_iota"), 1)
            then(v.tensor_tensor(m0, iota8[:, :, :], rep(idxf[:, :, 0:1]), ALU.is_equal))
            then(v.tensor_tensor(m1, iota8[:, :, :], rep(idxf[:, :, 1:2]), ALU.is_equal))
            settled()
            then(v.tensor_tensor(mask, m0, m1, ALU.add))
            v.wait_ge(sem("rt_exp"), n + 1)
            settled()
            if KIND[u] == MOE1:
                then(v.tensor_tensor(wsel, ex, mask, ALU.mult))
                settled()
                then(v.tensor_reduce(rsum, wsel, AX_X, ALU.add))
                settled()
                then(v.reciprocal(rinv, rsum))
                settled()
                then(v.scalar_tensor_tensor(out=w9[:, :, 0:E], in0=wsel, scalar=0.5,
                                            in1=rep(rinv.rearrange("p (i o) -> p i o", o=1)),
                                            op0=ALU.mult, op1=ALU.mult))
            else:
                then(v.tensor_reduce(rsum, ex, AX_X, ALU.add))
                then(v.tensor_tensor(wsel, ex, mask, ALU.mult))
                settled()
                then(v.reciprocal(rinv, rsum))
                settled()
                then(v.tensor_tensor(w9[:, :, 0:E], wsel, rep(rinv.rearrange("p (i o) -> p i o", o=1)), ALU.mult))
            settled()
            assert count[0] == base + R_OPS

        def act_router(s, u):
            n = ROUTED.index(u)
            s.wait_ge(sem("rt_step"), R_OPS * n + 6)
            s.activation(ex, dl, ACT.Exp).then_inc(sem("rt_exp"), 1)


        def ffn_loop(eng, u, step, first, last):
            n = CHUNKS[KIND[u]]
            first()
            with eng.Fori(0, (n - 4) // 2) as i:
                for p in range(2):
                    step(i * 2 + (2 + p), p)
            last(n)

        def pe_ffn(pe, u):
            b, f0, r0 = u % 2, FFN_AT[u], RAW0[u]
            moe = KIND[u] == MOE2

            def gate_up(j, p, early=False):
                pe.wait_ge(sem("w_gu"), f0 + 1 + j)
                if not early:
                    pe.wait_ge(sem("ffn_silu"), f0 - 1 + j)
                    pe.wait_ge(sem("ffn_h"), f0 - 1 + j)
                mm3c(pe, ps[:, 2 + p, :], [w(p, W_GATE + c * P) for c in range(DC)], [xT(b, c) for c in range(DC)])\
                    .then_inc(sem("ffn_gate"), 1)
                mm3c(pe, ps[:, 4 + p, :], [w(p, W_UP + c * P) for c in range(DC)], [xT(b, c) for c in range(DC)])\
                    .then_inc(sem("ffn_up"), 1)

            def spread(j, p):
                pe.wait_ge(sem("w_split"), r0 + 1 + j)
                lhs = wh[0:E + 1, p, W_IND:W_IND + P]
                pe.matmul(ps[:, p, :], lhs, wth, start=True, stop=False)
                pe.matmul(ps[:, p, :], lhs, wtl, start=False, stop=True).then_inc(sem("ffn_wbc"), 1)

            def down(j, p, first=False, final=False):
                pe.wait_ge(sem("ffn_lo"), f0 + 1 + j)
                if not moe:
                    pe.wait_ge(sem("w_split"), r0 + 1 + j)
                if first:
                    if positive(4 * u):
                        pe.wait_ge(sem("x_res"), 4 * u)
                for t in range(TT):
                    last = mm3(pe, acc(t), (ffn_hh[:, p, t * P:(t + 1) * P], ffn_hl[:, p, t * P:(t + 1) * P]),
                               w(p, W_DOWN, D), first and t % 2 == 0, final)
                    if final and t == 1:
                        last.then_inc(sem("ffn_half"), 1)
                last.then_inc(sem("w_used"), 1)

            def first():
                pe_ready(pe, u)
                if moe:
                    pe.wait_ge(sem("x_res"), 4 * u)
                    pe_logits(pe, u, 6)
                gate_up(0, 0, early=True)
                gate_up(1, 1, early=True)
                if moe:
                    m = MOE2_AT[u]
                    pe.wait_ge(sem("rt_step"), R_OPS * (ROUTED.index(u) + 1))
                    for i in range(TT):
                        last = pe.transpose(ps[0:E + 1, 7, i * P:(i + 1) * P], w9[:, i, :], ident[:, :])
                    last.then_inc(sem("wt_T"), 1)
                    pe.wait_ge(sem("wt_lo"), m + 1)
                    spread(0, 0)
                    spread(1, 1)
                down(0, 0, first=True)

            def step(j, p):
                gate_up(j, p)
                if moe:
                    spread(j, p)
                down(j - 1, 1 - p)

            def last(n):
                step(n - 2, 0)
                step(n - 1, 1)
                if moe:
                    pe.wait_ge(sem("ffn_h"), f0 + n)
                pe_T(pe, u + 1)
                down(n - 1, 1, final=True)

            ffn_loop(pe, u, step, first, last)

        def act_ffn(s, u):
            f0, g0 = FFN_AT[u], RING0[u]

            def step(j, p):
                s.wait_ge(sem("ffn_gate"), f0 + 1 + j)
                if positive(f0 - 1 + j):
                    s.wait_ge(sem("ffn_h"), f0 - 1 + j)
                s.activation(ffn_s[:, p, :], ps[:, 2 + p, :], ACT.Silu).then_inc(sem("ffn_silu"), 1)
                s.wait_ge(sem("ffn_h"), f0 + 1 + j)
                if positive(g0 - 1 + j):
                    s.wait_ge(sem("w_used"), g0 - 1 + j)
                s.activation(ffn_hh[:, p, :], ffn_hf[:, p, :], ACT.Copy).then_inc(sem("ffn_hi"), 1)

            def first():
                if KIND[u] == MOE2:
                    act_router(s, u)
                    for j in range(2):
                        s.wait_ge(sem("ffn_gate"), f0 + 1 + j)
                        s.wait_ge(sem("ffn_h"), f0 - 1 + j)
                        s.activation(ffn_s[:, j, :], ps[:, 2 + j, :], ACT.Silu).then_inc(sem("ffn_silu"), 1)
                    s.wait_ge(sem("wt_T"), MOE2_AT[u] + 1)
                    s.activation(wth, ps[0:E + 1, 7, :], ACT.Copy).then_inc(sem("wt_hi"), 1)
                    for j in range(2):
                        s.wait_ge(sem("ffn_h"), f0 + 1 + j)
                        s.wait_ge(sem("w_used"), g0 - 1 + j)
                        s.activation(ffn_hh[:, j, :], ffn_hf[:, j, :], ACT.Copy).then_inc(sem("ffn_hi"), 1)
                else:
                    if u == 1:
                        act_softplus(s)
                    step(0, 0)
                    step(1, 1)

            def last(n):
                step(n - 2, 0)
                step(n - 1, 1)
                act_T(s, u + 1)

            ffn_loop(s, u, step, first, last)

        def dve_ffn(v, u):
            f0, g0 = FFN_AT[u], RING0[u]
            moe = KIND[u] == MOE2

            def step(j, p):
                v.wait_ge(sem("ffn_silu"), f0 + 1 + j)
                v.wait_ge(sem("ffn_up"), f0 + 1 + j)
                if positive(f0 - 1 + j):
                    v.wait_ge(sem("ffn_lo"), f0 - 1 + j)
                hf = ffn_hf[:, p, :]
                if moe:
                    k0 = f0 - MOE_F0
                    v.tensor_tensor(hf, ffn_s[:, p, :], ps[:, 4 + p, :], ALU.mult).then_inc(sem("ffn_h0"), 1)
                    v.wait_ge(sem("ffn_h0"), k0 + 1 + j)
                    v.wait_ge(sem("ffn_wbc"), k0 + 1 + j)
                    v.tensor_tensor(hf, hf, ps[:, p, :], ALU.mult).then_inc(sem("ffn_h"), 1)
                else:
                    v.tensor_tensor(hf, ffn_s[:, p, :], ps[:, 4 + p, :], ALU.mult).then_inc(sem("ffn_h"), 1)
                v.wait_ge(sem("ffn_hi"), f0 + 1 + j)
                if positive(g0 - 1 + j):
                    v.wait_ge(sem("w_used"), g0 - 1 + j)
                v.tensor_tensor(ffn_hl[:, p, :], hf, f32(ffn_hh[:, p, :]), ALU.subtract).then_inc(sem("ffn_lo"), 1)

            def first():
                if u == 1:
                    dve_consts(v)
                if moe:
                    dve_router(v, u, 6)
                    v.wait_ge(sem("wt_hi"), MOE2_AT[u] + 1)
                    v.tensor_tensor(wtl, ps[0:E + 1, 7, :], f32(wth), ALU.subtract).then_inc(sem("wt_lo"), 1)
                step(0, 0)
                step(1, 1)
                dve_stats(v, u + 1)

            def last(n):
                dve_norm(v, u + 1)
                step(n - 2, 0)
                step(n - 1, 1)
                dve_T(v, u + 1)
                dve_residual(v, u, 0.5, [("ffn_half", FFN_UNITS.index(u) + 1), ("w_used", g0 + n)])

            ffn_loop(v, u, step, first, last)

        FFN_UNITS = [u for u in range(N_UNITS) if KIND[u] in (FFN0, MOE2)]
        MOE_F0 = FFN_AT[12]

        RG_IG, RG_AG, RG_WR = 1024, 1280, 1536
        def pe_rglru(pe, u):
            b = u % 2
            pe.wait_ge(sem("w_split"), RAW0["rglru"] + 2)
            pe_ready(pe, u)
            for m in range(4):
                mm3c(pe, ps[:, 2 + m, :], [rc(c * 512 + m * P, P) for c in range(DC)], [xT(b, c) for c in range(DC)])\
                    .then_inc(sem("rg_xy"), 1)
            for c in range(DC):
                pe.wait_ge(sem("rg_clo"), DC * b + c + 1)
                mm3(pe, ps[:, c, :], rc(RG_IG + c * P, P), (rg_ch[:, c, :], rg_cl[:, c, :]), True, True)\
                    .then_inc(sem("rg_gates"), 1)
                mm3(pe, ps[:, 2 + c, :], rc(RG_AG + c * P, P), (rg_ch[:, c, :], rg_cl[:, c, :]), True, True)\
                    .then_inc(sem("rg_gates"), 1)
            pe.wait_ge(sem("rg_sigm"), 4 * (b + 1))
            pe_T(pe, u + 1)
            pe.wait_ge(sem("rg_glo"), DC * (b + 1))
            pe.wait_ge(sem("x_res"), 4 * u)
            for t in range(TT):
                last = mm3c(pe, acc(t), [(rg_gh[:, c, t * P:(t + 1) * P], rg_gl[:, c, t * P:(t + 1) * P])
                                         for c in range(DC)], [rc(RG_WR + c * D, D) for c in range(DC)])
                if t % 2:
                    last.then_inc(sem("rg_out"), 1)

        def act_rglru(s, u):
            b = u % 2
            s.wait_ge(sem("const_rgp"), 1)
            for c in range(DC):
                s.wait_ge(sem("rg_xy"), 4 * b + c + 1)
                s.wait_ge(sem("rg_pad"), 1)
                s.activation(rg_xp[:, c, 3:3 + T], ps[:, 2 + c, :], ACT.Copy).then_inc(sem("rg_x"), 1)
            for c in range(DC):
                s.wait_ge(sem("rg_xy"), 4 * b + DC + c + 1)
                s.activation(rg_gy[:, c, :], ps[:, 4 + c, :], ACT.Gelu).then_inc(sem("rg_gelu"), 1)
            for c in range(DC):
                s.wait_ge(sem("rg_conv"), 8 * b + 4 * c + 4)
                s.activation(rg_ch[:, c, :], rg_xc[:, c, :], ACT.Copy).then_inc(sem("rg_chi"), 1)
            for c in range(DC):
                s.wait_ge(sem("rg_gates"), 4 * b + 2 * c + 1)
                s.activation(rg_gx[:, c, :], ps[:, c, :], ACT.Sigmoid, bias=rgp[:, c, 5:6])\
                    .then_inc(sem("rg_sigm"), 1)
                s.wait_ge(sem("rg_gates"), 4 * b + 2 * c + 2)
                s.activation(rg_ga[:, c, :], ps[:, 2 + c, :], ACT.Sigmoid, bias=rgp[:, c, 6:7])\
                    .then_inc(sem("rg_sigm"), 1)
            for c in range(DC):
                s.wait_ge(sem("rg_sigm"), 4 * b + 2 * c + 2)
                s.activation(rg_a[:, c, :], rg_ga[:, c, :], ACT.Exp, scale=rgp[:, c, 10:11])\
                    .then_inc(sem("rg_a"), 1)
                s.activation(rg_th[:, c, :], rg_ga[:, c, :], ACT.Tanh, scale=rgp[:, c, 10:11])\
                    .then_inc(sem("rg_th"), 1)
            for c in range(DC):
                s.wait_ge(sem("rg_m2"), DC * b + c + 1)
                s.activation(rg_th[:, c, :], rg_th[:, c, :], ACT.Sqrt, scale=-1.0).then_inc(sem("rg_sqrt"), 1)
            act_T(s, u + 1)
            for c in range(DC):
                s.wait_ge(sem("rg_g"), DC * b + c + 1)
                s.activation(rg_gh[:, c, :], rg_gy[:, c, :], ACT.Copy).then_inc(sem("rg_ghi"), 1)

        def dve_rglru(v, u):
            b = u % 2
            v.wait_ge(sem("const_rgp"), 1)
            if b == 0:
                v.memset(rg_xp[:, :, 0:3], 0.0).then_inc(sem("rg_pad"), 1)
                v.wait_ge(sem("rg_pad"), 1)
            for c in range(DC):
                v.wait_ge(sem("rg_x"), DC * b + c + 1)
                v.tensor_scalar(rg_xc[:, c, :], rg_xp[:, c, 0:T], rgp[:, c, 0:1], rgp[:, c, 4:5], ALU.mult, ALU.add)\
                    .then_inc(sem("rg_conv"), 1)
                for k in range(1, 4):
                    v.wait_ge(sem("rg_conv"), 8 * b + 4 * c + k)
                    v.scalar_tensor_tensor(out=rg_xc[:, c, :], in0=rg_xp[:, c, k:k + T], scalar=rgp[:, c, k:k + 1],
                                           in1=rg_xc[:, c, :], op0=ALU.mult, op1=ALU.add).then_inc(sem("rg_conv"), 1)
                v.wait_ge(sem("rg_chi"), DC * b + c + 1)
                v.tensor_tensor(rg_cl[:, c, :], rg_xc[:, c, :], f32(rg_ch[:, c, :]), ALU.subtract)\
                    .then_inc(sem("rg_clo"), 1)
            dve_ln(v, u + 1)
            for c in range(DC):
                v.wait_ge(sem("rg_sigm"), 4 * b + 2 * c + 1)
                v.tensor_tensor(rg_xc[:, c, :], rg_gx[:, c, :], rg_xc[:, c, :], ALU.mult).then_inc(sem("rg_n"), 1)
            for c in range(DC):
                v.wait_ge(sem("rg_a"), DC * b + c + 1)
                v.wait_ge(sem("rg_n"), 2 * DC * b + c + 1)
                v.tensor_tensor(rg_gx[:, c, :], rg_a[:, c, :], rg_a[:, c, :], ALU.mult).then_inc(sem("rg_a2"), 1)
                v.wait_ge(sem("rg_a2"), DC * b + c + 1)
                v.wait_ge(sem("rg_th"), DC * b + c + 1)
                v.scalar_tensor_tensor(out=rg_th[:, c, :], in0=rg_gx[:, c, :], scalar=1.0, in1=rg_th[:, c, :],
                                       op0=ALU.add, op1=ALU.mult).then_inc(sem("rg_m2"), 1)
            for c in range(DC):
                v.wait_ge(sem("rg_sqrt"), DC * b + c + 1)
                v.tensor_tensor(rg_xc[:, c, :], rg_xc[:, c, :], rg_th[:, c, :], ALU.mult).then_inc(sem("rg_n"), 1)
            for c in range(DC):
                v.wait_ge(sem("rg_n"), 2 * DC * b + DC + c + 1)
                v.tensor_tensor_scan(rg_xc[:, c, :], rg_a[:, c, :], rg_xc[:, c, :], 0.0, ALU.mult, ALU.add)\
                    .then_inc(sem("rg_scan"), 1)
            for c in range(DC):
                v.wait_ge(sem("rg_scan"), DC * b + c + 1)
                v.wait_ge(sem("rg_gelu"), DC * b + c + 1)
                v.tensor_tensor(rg_gy[:, c, :], rg_gy[:, c, :], rg_xc[:, c, :], ALU.mult).then_inc(sem("rg_g"), 1)
            dve_T(v, u + 1)
            for c in range(DC):
                v.wait_ge(sem("rg_ghi"), DC * b + c + 1)
                v.tensor_tensor(rg_gl[:, c, :], rg_gy[:, c, :], f32(rg_gh[:, c, :]), ALU.subtract)\
                    .then_inc(sem("rg_glo"), 1)
            dve_residual(v, u, 1.0, [("rg_out", 2 * b + 1), ("rg_out", 2 * b + 2)])

        def pe_moe1(pe, u):
            b, m = u % 2, MOE_AT[u]
            pairs = E // 2
            pe_ready(pe, u)
            pe_logits(pe, u, 0)
            pe.wait_ge(sem("delta_lo"), 4)
            pe.wait_ge(sem("w_split"), RAW0["wt"] + 2)

            def pair(k):
                for t in range(TT):
                    if not isinstance(k, int) or k > 0:
                        pe.wait_ge(sem("moe_acc"), 2 * TT * pairs * m - 2 * TT + 2 * t + 2 + k * 2 * TT)
                    for c in range(DC):
                        at = (c * E + k * 2) * D
                        r = drh[:, bass.ds(at, 2 * D)], drl[:, bass.ds(at, 2 * D)]
                        last = mm3(pe, ps[:, 2 + t, :], xTt(b, c, t), r, c == 0, c == DC - 1)
                    last.then_inc(sem("moe_mm"), 1)

            pair(0)
            with pe.Fori(1, pairs) as k:
                pair(k)
            pe.wait_ge(sem("rt_step"), R_OPS * ROUTED.index(u) + 1)
            pe_T(pe, u + 1)
            pe.wait_ge(sem("x_res"), 4 * u)
            for t in range(TT):
                last = mm3c(pe, acc(t), [xTt(b, c, t) for c in range(DC)],
                            [dr(RES_AT["wt"] + c * D, D) for c in range(DC)])
                if t % 2:
                    last.then_inc(sem("moe_w"), 1)

        def act_moe1(s, u):
            act_router(s, u)
            act_T(s, u + 1)

        def dve_moe1(v, u):
            b, m = u % 2, MOE_AT[u]
            pairs = E // 2
            dve_router(v, u, 0)
            for k in range(pairs):
                for t in range(TT):
                    v.wait_ge(sem("moe_mm"), TT * pairs * m + TT * k + t + 1)
                    for e in range(2):
                        n = 2 * TT * pairs * m + 2 * (TT * k + t) + e
                        if positive(n):
                            v.wait_ge(sem("moe_acc"), n)
                        xt = x[:, TT * b + t, :]
                        v.scalar_tensor_tensor(out=xt, in0=ps[:, 2 + t, e * D:(e + 1) * D],
                                               scalar=w9[:, t, 2 * k + e:2 * k + e + 1], in1=xt,
                                               op0=ALU.mult, op1=ALU.add).then_inc(sem("moe_acc"), 1)
                if k == 0:
                    dve_ln(v, u + 1)
            dve_T(v, u + 1)
            dve_residual(v, u, 0.5, [("moe_w", 2 * m + 1), ("moe_w", 2 * m + 2)])

        def act_T_next(s, u):
            act_T(s, u + 1)

        def pe_ffn3(pe, u):
            b, m = u % 2, F3_AT[u]
            pe_ready(pe, u)
            pe.wait_ge(sem("q3_ready"), 2)
            pe.wait_ge(sem("x_res"), 4 * u)
            for t in range(TT):
                n = 0
                for c in range(DC):
                    for half in xTt(b, c, t):
                        last = pe.matmul(acc(t), half, qt[:, c, :], start=(n == 0), stop=(n == 3))
                        n += 1
                if t % 2:
                    last.then_inc(sem("f3_out"), 1)
            pe_T(pe, u + 1)

        def dve_ffn3(v, u):
            b, m = u % 2, F3_AT[u]
            dve_ln(v, u + 1)
            v.wait_ge(sem("const_in"), 16 * CONSTS)
            for t in range(TT):
                xt = x[:, TT * b + t, :]
                v.scalar_tensor_tensor(out=xt, in0=bias3[:, :], scalar=0.5, in1=xt, op0=ALU.mult, op1=ALU.add)\
                    .then_inc(sem("f3_bias"), 1)
            v.wait_ge(sem("f3_bias"), 4 * (m + 1))
            dve_residual(v, u, 0.5, [("f3_out", 2 * m + 1), ("f3_out", 2 * m + 2)])
            dve_T(v, u + 1)

        F3_AT = {u: n for n, u in enumerate(v for v in range(N_UNITS) if KIND[v] == FFN3)}


        L_Q, L_WO = 1024, 1792

        def pool_rsqrt(g, dst, src, n, name, eps=None):
            g.tensor_tensor(dst, src, nhalf[:, 0:n], ALU.pow).then_inc(sem(name), 1)

        def pe_lin1(pe, u):
            b = u % 2
            pe.wait_ge(sem("w_split"), RAW0["lin1"] + 4)
            pe_ready(pe, u)
            pe.wait_ge(sem("l_xn"), TT * (b + 1))
            for c in range(DC):
                for i in range(TT):
                    last = pe.transpose(ps[:, c, i * P:(i + 1) * P], lin_xn[:, i, c * P:(c + 1) * P], ident[:, :])
                last.then_inc(sem("l_T"), 1)
            pe.wait_ge(sem("l_hlo"), DC * (b + 1))
            for t in range(TT):
                mm3c(pe, ps[:, 2 + t, :], [(lin_hh[:, c, t * P:(t + 1) * P], lin_hl[:, c, t * P:(t + 1) * P])
                                           for c in range(DC)], [rc(c * 2 * D, 2 * D) for c in range(DC)])\
                    .then_inc(sem("l_kvmm"), 1)
            for k in range(3):
                if k == 0:
                    pe.wait_ge(sem("l_kv"), TT * b + 3)
                mm3c(pe, ps[:, 2 + k, :], [rc(L_Q + (c * 3 + k) * P, P) for c in range(DC)],
                     [(lin_hh[:, c, :], lin_hl[:, c, :]) for c in range(DC)]).then_inc(sem("l_qmm"), 1)
            pe.wait_ge(sem("x_res"), 4 * u)
            pe.wait_ge(sem("l_prod"), TT * (b + 1))
            for c in range(DC):
                for t in range(TT):
                    last = pe.matmul(ps[:, 6, c:c + 1], lin_prod[:, t, c * P:(c + 1) * P], ones[:, 0:1],
                                     start=(t == 0), stop=(t == TT - 1))
            last.then_inc(sem("l_sum"), 1)
            pe_T(pe, u + 1)
            pe.wait_ge(sem("l_qlo"), DC * (b + 1))
            for t in range(TT):
                last = mm3c(pe, acc(t), [(lin_qh[:, c, t * P:(t + 1) * P], lin_ql[:, c, t * P:(t + 1) * P])
                                         for c in range(DC)], [rc(L_WO + c * D, D) for c in range(DC)])
                if t % 2:
                    last.then_inc(sem("l_out"), 1)

        def act_lin1(s, u):
            b = u % 2
            s.wait_ge(sem("const_in"), 16 * CONSTS)
            for c in range(DC):
                s.wait_ge(sem("l_T"), DC * b + c + 1)
                s.activation(lin_hh[:, c, :], ps[:, c, :], ACT.Identity, bias=lin_cols[:, 2 + c:3 + c],
                             scale=lin_cols[:, c:c + 1]).then_inc(sem("l_hhi"), 1)
            for t in range(TT):
                s.wait_ge(sem("l_rope"), 4 * (TT * b + t + 1))
                s.activation(lin_sq[:, t, :], lin_kv[:, t, 0:D], ACT.Square, accum_out=lin_ss[:, t:t + 1])\
                    .then_inc(sem("l_ss"), 1)
            for c in range(DC):
                s.wait_ge(sem("l_qf"), 4 * b + 3 + c)
                s.activation(lin_qh[:, c, :], lin_qf[:, c, :], ACT.Copy).then_inc(sem("l_qhi"), 1)
            act_T(s, u + 1)

        lin_sq = lin_qf[:, :, :].rearrange("p c (a n) -> p (c a) n", a=2)
        lin_ss, lin_rn, lin_a = small[:, 320:324], small[:, 324:328], small[:, 328:330]
        l_mv, l_st, l_ve, l_rs = small[:, 336:344], small[:, 344:368], small[:, 368:372], small[:, 372:376]

        def pool_lin1(g, u):
            b = u % 2
            g.wait_ge(sem("l_aggr"), TT * (b + 1))
            g.tensor_scalar(l_ve, l_mv.rearrange("p (i k) -> p i k", k=2)[:, :, 1], EPS, 1.0, ALU.add, ALU.mult)\
                .then_inc(sem("l_ve"), 1)
            g.wait_ge(sem("l_ve"), b + 1)
            pool_rsqrt(g, l_rs, l_ve, TT, "l_rs")
            pool_ln(g, u + 1)
            for t in range(TT):
                g.wait_ge(sem("l_ss"), TT * b + t + 1)
                pool_rsqrt(g, lin_rn[:, t:t + 1], lin_ss[:, t:t + 1], 1, "l_rn")

        def dve_lin1(v, u):
            b = u % 2
            for i in range(TT):
                v.bn_stats(l_st[:, 6 * i:6 * i + 6], xn[:, b, i, :]).then_inc(sem("l_stats"), 1)
            for i in range(TT):
                v.wait_ge(sem("l_stats"), TT * b + i + 1)
                v.bn_aggr(l_mv[:, 2 * i:2 * i + 2], l_st[:, 6 * i:6 * i + 6]).then_inc(sem("l_aggr"), 1)
            v.wait_ge(sem("l_rs"), b + 1)
            for i in range(TT):
                v.tensor_scalar(lin_xn[:, i, :], xn[:, b, i, :], l_mv[:, 2 * i:2 * i + 1], l_rs[:, i:i + 1],
                                ALU.subtract, ALU.mult).then_inc(sem("l_xn"), 1)
            v.wait_ge(sem("const_in"), 16 * CONSTS)
            for c in range(DC):
                v.wait_ge(sem("l_hhi"), DC * b + c + 1)
                v.tensor_scalar(lin_tmp[:, c, :], ps[:, c, :], lin_cols[:, c:c + 1], lin_cols[:, 2 + c:3 + c],
                                ALU.mult, ALU.add).then_inc(sem("l_tmp"), 1)
            for c in range(DC):
                v.wait_ge(sem("l_tmp"), DC * b + c + 1)
                v.tensor_tensor(lin_hl[:, c, :], lin_tmp[:, c, :], f32(lin_hh[:, c, :]), ALU.subtract)\
                    .then_inc(sem("l_hlo"), 1)
            v.wait_ge(sem("lin_in"), 48)
            for i in range(TT):
                xt = x[:, TT * b + i, :]
                v.tensor_tensor(xt, xt, xn[:, b, i, :], ALU.add).then_inc(sem("l_xa"), 1)
            v.wait_ge(sem("l_xa"), TT * (b + 1))
            v.wait_ge(sem("const_in"), 16 * CONSTS)
            for i in range(TT):
                xt = x[:, TT * b + i, :]
                v.tensor_tensor(xt, xt, lin_bout[:, :], ALU.add).then_inc(sem("l_xb"), 1)
            for t in range(TT):
                v.wait_ge(sem("l_kvmm"), TT * b + t + 1)
                v.tensor_tensor(lin_kv[:, t, :], ps[:, 2 + t, :], lin_bkv[:, :], ALU.add).then_inc(sem("l_kv"), 1)
            dve_ln(v, u + 1)
            for t in range(TT):
                v.wait_ge(sem("l_kv"), TT * b + t + 1)
                n = 4 * (TT * b + t)
                kk = lin_kv[:, t, 0:P].rearrange("p (n k) -> p n k", k=2)
                ks = lin_ks[:, t, :].rearrange("p (n k) -> p n k", k=2)
                sn = lin_tok[:, 1, t, :].rearrange("p (n k) -> p n k", k=2)
                v.tensor_tensor(lin_kr[:, t, :], lin_kv[:, t, 0:P], lin_tok[:, 0, t, :], ALU.mult).then_inc(sem("l_rope"), 1)
                v.tensor_tensor(ks[:, :, 0], kk[:, :, 1], sn[:, :, 0], ALU.mult).then_inc(sem("l_rope"), 1)
                v.tensor_tensor(ks[:, :, 1], kk[:, :, 0], sn[:, :, 1], ALU.mult).then_inc(sem("l_rope"), 1)
                v.wait_ge(sem("l_rope"), n + 3)
                v.tensor_tensor(lin_kv[:, t, 0:P], lin_kr[:, t, :], lin_ks[:, t, :], ALU.add).then_inc(sem("l_rope"), 1)
            v.wait_ge(sem("l_T"), DC * (b + 1))
            for t in range(TT):
                v.wait_ge(sem("l_rn"), TT * b + t + 1)
                v.scalar_tensor_tensor(out=lin_prod[:, t, :], in0=lin_kv[:, t, 0:D], scalar=lin_rn[:, t:t + 1],
                                       in1=lin_kv[:, t, D:2 * D], op0=ALU.mult, op1=ALU.mult).then_inc(sem("l_prod"), 1)
            v.wait_ge(sem("l_qmm"), 3 * b + 1)
            v.scalar_tensor_tensor(out=lin_qa[:, :], in0=ps[:, 2, :], scalar=lin_cols[:, 4:5], in1=lin_feat[:, 0, :],
                                   op0=ALU.add, op1=ALU.mult).then_inc(sem("l_qf"), 1)
            v.wait_ge(sem("l_qmm"), 3 * b + 2)
            v.scalar_tensor_tensor(out=lin_qb[:, :], in0=ps[:, 3, :], scalar=lin_cols[:, 5:6], in1=lin_feat[:, 1, :],
                                   op0=ALU.add, op1=ALU.mult).then_inc(sem("l_qb"), 1)
            v.wait_ge(sem("l_qf"), 4 * b + 1)
            v.wait_ge(sem("l_qb"), b + 1)
            v.tensor_tensor(lin_qa[:, :], lin_qa[:, :], lin_qb[:, :], ALU.add).then_inc(sem("l_qf"), 1)
            v.wait_ge(sem("l_sum"), b + 1)
            v.tensor_copy(lin_a, ps[:, 6, 0:DC]).then_inc(sem("l_a"), 1)
            v.wait_ge(sem("l_a"), b + 1)
            v.wait_ge(sem("l_qf"), 4 * b + 2)
            v.tensor_scalar(lin_qf[:, 0, :], lin_qa[:, :], lin_a[:, 0:1], None, ALU.mult).then_inc(sem("l_qf"), 1)
            v.wait_ge(sem("l_qmm"), 3 * b + 3)
            v.tensor_scalar(lin_qf[:, 1, :], ps[:, 4, :], lin_cols[:, 6:7], lin_a[:, 1:2], ALU.add, ALU.mult)\
                .then_inc(sem("l_qf"), 1)
            for c in range(DC):
                v.wait_ge(sem("l_qhi"), DC * b + c + 1)
                v.tensor_tensor(lin_ql[:, c, :], lin_qf[:, c, :], f32(lin_qh[:, c, :]), ALU.subtract)\
                    .then_inc(sem("l_qlo"), 1)
            dve_T(v, u + 1)
            v.wait_ge(sem("l_xb"), TT * (b + 1))
            dve_residual(v, u, 1.0, [("l_out", 2 * b + 1), ("l_out", 2 * b + 2)])

        A2_HEADS = {14: 0, 15: H}
        A3_HEADS = {20: 2 * H, 21: 3 * H}
        A2_FILL = {14: 0, 15: 4 + 3 * H}
        A3_FILL = {20: 2 * (4 + 3 * H), 21: 2 * (4 + 3 * H) + 7 * H}

        def pe_scores(pe, n, q, k):
            for i in range(TT):
                if positive(n * TT - TT + max(i, 1) + 1):
                    pe.wait_ge(sem("at_exp"), n * TT - TT + max(i, 1) + 1)
                bank, at = S_AT[i]
                mm3(pe, ps[:, bank, at:at + S_COLS[i]], q(i), k(S_COLS[i]), True, False)
                pe.matmul(ps[:, bank, at + i * P:at + (i + 1) * P], identb[:, :], maskb[:, :], start=False, stop=True,
                          skip_group_check=True).then_inc(sem("at_s"), 1)

        def dve_max(v, n, par, scale):
            for tiles in ((0, 1), (2,), (3,)):
                v.wait_ge(sem("at_s"), tiles[-1] + 1 + n * TT)
                for i in tiles:
                    bank, at = S_AT[i]
                    v.tensor_reduce(h_max[:, par, i:i + 1], ps[:, bank, at:at + KEYS[i]], AX_X, ALU.max)\
                        .then_inc(sem("at_mx"), 1)
                v.wait_ge(sem("at_mx"), tiles[-1] + 1 + n * TT)
                sl = slice(tiles[0], tiles[-1] + 1)
                v.tensor_scalar(h_nmx[:, par, sl], h_max[:, par, sl], -scale, None, ALU.mult)\
                    .then_inc(sem("at_nmx"), len(tiles))

        def act_exp(s, n, par, scale, p):
            for i in range(TT):
                bank, at = S_AT[i]
                s.wait_ge(sem("at_nmx"), max(i, 1) + 1 + n * TT)
                s.activation(p[:, par, P_AT[i]:P_AT[i + 1]], ps[:, bank, at:at + KEYS[i]], ACT.Exp,
                             bias=h_nmx[:, par, i:i + 1], scale=scale, accum_out=h_sum[:, par, i:i + 1])\
                    .then_inc(sem("at_exp"), 1)

        def dve_rinv(v, n, par):
            v.wait_ge(sem("at_exp"), TT + n * TT)
            v.reciprocal(h_inv[:, par, :], h_sum[:, par, :]).then_inc(sem("at_rinv"), 1)

        def pool_norm(g, n, par, p):
            g.wait_ge(sem("at_rinv"), 1 + n)
            if not isinstance(n, int):
                g.sem_inc(sem("pool_turn"), 1)
            for i in range(TT):
                pp = p[:, par, P_AT[i]:P_AT[i + 1]]
                g.tensor_scalar(pp, pp, h_inv[:, par, i:i + 1], 1.0, ALU.mult, ALU.mult).then_inc(sem("at_norm"), 1)

        def pe_fill_start(pe, earlier):
            pe.wait_ge(sem("at_flo"), earlier)

        def pe_transpose_p(pe, n, par, p, banks, earlier):
            pe.wait_ge(sem("at_norm"), TT + n * TT)
            for f, blocks in enumerate(FILLS):
                pe_fill_start(pe, earlier[f])
                for kb in blocks:
                    for i in range(kb, TT):
                        at = PT_AT[kb] - PT_AT[blocks[0]] + (i - kb) * P
                        last = pe.transpose(ps[:, banks[f], at:at + P], p[:, par, P_AT[i] + kb * P:P_AT[i] + (kb + 1) * P],
                                            ident[:, :])
                last.then_inc(sem("at_fill"), 1)

        def pe_pv(pe, o, fill, v, pth, ptl, start, stop):
            for kb in range(TT):
                if kb < len(FILLS):
                    pe.wait_ge(sem("at_flo"), fill + kb + 1)
                r = slice(PT_AT[kb], PT_AT[kb + 1])
                last = mm3(pe, o[:, kb * P:T], v(kb), (pth[:, r], ptl[:, r]), start and kb == 0, stop and kb == TT - 1)
            return last

        def act_fill(s, fill, bank, dst, cols=T, **how):
            s.wait_ge(sem("at_fill"), fill + 1)
            func = ACT.Identity if how else ACT.Copy
            s.activation(dst, ps[:, bank, 0:cols], func, **how).then_inc(sem("at_fhi"), 1)

        def dve_fill(v, fill, bank, dst, hi, cols=T, bias=None):
            v.wait_ge(sem("at_fhi"), fill + 1)
            if bias is None:
                ins = v.tensor_tensor(dst, ps[:, bank, 0:cols], f32(hi), ALU.subtract)
            else:
                ins = v.scalar_tensor_tensor(out=dst, in0=ps[:, bank, 0:cols], scalar=bias, in1=f32(hi),
                                             op0=ALU.add, op1=ALU.subtract)
            ins.then_inc(sem("at_flo"), 1)

        def pt_cols(f):
            return PT_AT[FILLS[f][0]], PT_AT[FILLS[f][-1] + 1]

        def a2_v(g, kb, j):
            lo = slice(j * P, j * P + P)
            if g == 0:
                return (drh[:, kb * 8 * VS:(kb + 1) * 8 * VS][:, lo], drl[:, kb * 8 * VS:(kb + 1) * 8 * VS][:, lo])
            return (a2_vh[:, kb, :, :].rearrange("p h n -> p (h n)")[:, lo],
                    a2_vl[:, kb, :, :].rearrange("p h n -> p (h n)")[:, lo])

        def a2_vslot(g, hi, kb):
            t = (drh if hi else drl)[:, kb * 8 * VS:(kb + 1) * 8 * VS] if g == 0 else \
                (a2_vh if hi else a2_vl)[:, kb, :, :].rearrange("p h n -> p (h n)")
            return t.rearrange("p (h n) -> p h n", h=8)[:, :, 0:HD2]

        def pe_att2(pe, u):
            b, n0, f0 = u % 2, A2_HEADS[u], A2_FILL[u]
            pe.wait_ge(sem("w_split"), RAW0["att2"] + 2)
            pe_ready(pe, u)
            for f in range(4):
                if f == 3:
                    pe_fill_start(pe, f0 + 1)
                at = (f // 2) * 512 + (f % 2) * P
                mm3c(pe, ps[:, f % 3, :], [rc(at + c * D, P) for c in range(DC)], [xT(b, c) for c in range(DC)])\
                    .then_inc(sem("at_fill"), 1)
            pe.wait_ge(sem("x_res"), 4 * u)
            for t in range(TT):
                last = mm3c(pe, acc(t), [xTt(b, c, t) for c in range(DC)], [rc(1024 + c * D, D) for c in range(DC)])
                if t % 2:
                    last.then_inc(sem("a2_v"), 1)

            def scores(h):
                pe.wait_ge(sem("a2_mask"), 2 * (n0 + h) + 2)
                pe_scores(pe, n0 + h,
                          lambda i: (a2_mh[:, h % 2, i * P:(i + 1) * P], a2_ml[:, h % 2, i * P:(i + 1) * P]),
                          lambda n: (a2_kh[:, h // 8, 0:n], a2_kl[:, h // 8, 0:n]))

            pe.wait_ge(sem("at_flo"), f0 + 4)
            scores(0)
            pe.wait_ge(sem("a2_vlo"), 4 * (b + 1))
            def context(h):
                pe_pv(pe, ps[:, 6 + h // 8, :], f0 + 4 + 3 * h, lambda kb: a2_v(h // 8, kb, h % 8), a2_pth, a2_ptl,
                      h % 8 == 0, h % 8 == 7).then_inc(sem("a2_pv"), 1)

            for h in range(H):
                f = f0 + 4 + 3 * h
                if h + 1 < H:
                    scores(h + 1)
                if h > 0:
                    context(h - 1)
                pe_transpose_p(pe, n0 + h, h % 2, a2_p, [0, 1, 2], [f - 2, f - 1, f] if h else [f0 + 4, f0 + 2, f0 + 3])
            context(H - 1)
            pe.wait_ge(sem("at_flo"), f0 + 4 + 3 * H)
            pe_T(pe, u + 1)
            pe.wait_ge(sem("a2_zlo"), 2 * (b + 1))
            for t in range(TT):
                last = mm3c(pe, acc(t), [xTt(b, c, t) for c in range(DC)], [rc(1536 + c * D, D) for c in range(DC)])
                if t % 2:
                    last.then_inc(sem("a2_out"), 1)

        def act_att2(s, u):
            b, n0, f0 = u % 2, A2_HEADS[u], A2_FILL[u]
            s.wait_ge(sem("const_in"), 16 * CONSTS)
            for f in range(4):
                dst = (a2_qh if f < 2 else a2_kh)[:, f % 2, :]
                act_fill(s, f0 + f, f % 3, dst, bias=att_cols[:, f:f + 1], scale=1.0)
            s.wait_ge(sem("a2_vzero"), 2)
            for t in range(TT):
                s.wait_ge(sem("a2_vf"), 4 * b + t + 1)
                for g in range(2):
                    s.activation(a2_vslot(g, True, t), a2_vf[:, t, g * P:(g + 1) * P].rearrange("p (h n) -> p h n", h=8),
                                 ACT.Copy).then_inc(sem("a2_vhi"), 1)
            act_exp(s, n0, 0, SCALE2, a2_p)
            for h in range(H):
                if h + 1 < H:
                    act_exp(s, n0 + h + 1, (h + 1) % 2, SCALE2, a2_p)
                if h == 8:
                    act_z(s, b, 0)
                for f in range(3):
                    lo, hi = pt_cols(f)
                    act_fill(s, f0 + 4 + 3 * h + f, f, a2_pth[:, lo:hi], hi - lo)
            act_z(s, b, 1)
            act_T(s, u + 1)

        def act_z(s, b, g):
            s.wait_ge(sem("a2_pv"), H * b + 8 * (g + 1))
            s.activation(xh[:, b, g, :], ps[:, 6 + g, :], ACT.Copy).then_inc(sem("a2_zhi"), 1)

        def dve_z(v, b, g):
            v.wait_ge(sem("a2_zhi"), 2 * b + g + 1)
            v.tensor_tensor(xl[:, b, g, :], ps[:, 6 + g, :], f32(xh[:, b, g, :]), ALU.subtract).then_inc(sem("a2_zlo"), 1)

        def dve_att2(v, u):
            b, n0, f0 = u % 2, A2_HEADS[u], A2_FILL[u]
            v.wait_ge(sem("const_in"), 16 * CONSTS)
            for f in range(4):
                dst, hi = (a2_ql, a2_qh) if f < 2 else (a2_kl, a2_kh)
                dve_fill(v, f0 + f, f % 3, dst[:, f % 2, :], hi[:, f % 2, :], bias=att_cols[:, f:f + 1])
            v.wait_ge(sem("a2_bv_in"), 16)
            for t in range(TT):
                v.wait_ge(sem("a2_v"), 2 * b + t // 2 + 1)
                v.tensor_tensor(a2_vf[:, t, :], acc(t), a2_bv[:, :], ALU.add).then_inc(sem("a2_vf"), 1)
            dve_max(v, n0, 0, SCALE2)
            v.wait_ge(sem("a2_vzero"), 4)
            for t in range(TT):
                for g in range(2):
                    v.wait_ge(sem("a2_vhi"), 8 * b + 2 * t + g + 1)
                    ins = v.tensor_tensor(a2_vslot(g, False, t),
                                          a2_vf[:, t, g * P:(g + 1) * P].rearrange("p (h n) -> p h n", h=8),
                                          f32(a2_vslot(g, True, t)), ALU.subtract)
                    if g == 1:
                        ins.then_inc(sem("a2_vlo"), 1)
            dve_rinv(v, n0, 0)
            for h in range(H):
                if h == 1:
                    dve_stats(v, u + 1)
                if h == 3:
                    dve_norm(v, u + 1)
                if h + 1 < H:
                    dve_max(v, n0 + h + 1, (h + 1) % 2, SCALE2)
                    dve_rinv(v, n0 + h + 1, (h + 1) % 2)
                if h == 8:
                    dve_z(v, b, 0)
                for f in range(3):
                    lo, hi = pt_cols(f)
                    dve_fill(v, f0 + 4 + 3 * h + f, f, a2_ptl[:, lo:hi], a2_pth[:, lo:hi], hi - lo)
            dve_z(v, b, 1)
            dve_T(v, u + 1)
            v.wait_ge(sem("const_in"), 16 * CONSTS)
            for t in range(TT):
                xt = x[:, TT * b + t, :]
                v.tensor_tensor(xt, xt, att_bo[:, :], ALU.add).then_inc(sem("a2_xb"), 1)
            v.wait_ge(sem("a2_xb"), TT * (b + 1))
            dve_residual(v, u, 1.0, [("a2_out", 2 * b + 1), ("a2_out", 2 * b + 2)])

        def pool_att2(g, u):
            b, n0, f0 = u % 2, A2_HEADS[u], A2_FILL[u]
            if b == 0:
                g.wait_ge(sem("x_res"), 4 * 14)
                g.memset(f32(drh[:, :]), 0.0).then_inc(sem("a2_vzero"), 1)
                g.memset(f32(a2_vh[:, :, :, :]), 0.0).then_inc(sem("a2_vzero"), 1)
                g.memset(f32(drl[:, :]), 0.0).then_inc(sem("a2_vzero"), 1)
                g.memset(f32(a2_vl[:, :, :, :]), 0.0).then_inc(sem("a2_vzero"), 1)

            def mask(h):
                if h == 0:
                    g.wait_ge(sem("at_flo"), f0 + 2)
                if h >= 2:
                    g.wait_ge(sem("at_s"), TT * (n0 + h - 1))
                elif b == 1:
                    g.wait_ge(sem("at_s"), TT * n0)
                for dst, src in ((a2_mh, a2_qh), (a2_ml, a2_ql)):
                    g.tensor_scalar(dst[:, h % 2, :], f32(src[:, h // 8, :]), headmask[:, h % 8:h % 8 + 1], 1.0,
                                    ALU.mult, ALU.mult).then_inc(sem("a2_mask"), 1)

            mask(0)
            mask(1)
            for h in range(H):
                pool_norm(g, n0 + h, h % 2, a2_p)
                if h + 2 < H:
                    mask(h + 2)
                if h == 1:
                    pool_ln(g, u + 1)

        V_FILLS, BODY = 2, 14

        def pair_fills(last):
            names = [("v", 0, 0), ("v", 0, 1)]
            for hh in range(2):
                if not (last and hh == 1):
                    names += [("q", hh, 0), ("k", hh, 0)]
                names += [("p", hh, f) for f in range(3)] + [("z", hh, 0)]
            seen = {2: -2, 0: -1, 1: -3}
            out_, bank = {}, 2
            for place, name in enumerate(names):
                out_[name] = (place, bank, seen[bank])
                seen[bank] = place
                bank = (bank + 1) % 3
            if last:
                out_["z", 1, 0] = (out_["z", 1, 0][0], 2, out_["p", 1, 1][0])
            return out_

        def pe_att3(pe, u):
            b, n0, f0, r0 = u % 2, A3_HEADS[u], A3_FILL[u], RAW0[u]

            def fill(base, place, bank, earlier):
                pe_fill_start(pe, base + earlier + 1)

            def qk(hh, banks, starts):
                for k in range(2):
                    pe_fill_start(pe, starts[k])
                    at = k * 2 * D + hh * P
                    mm3c(pe, ps[:, banks[k], :], [w(0, at + c * 2 * P) for c in range(DC)],
                         [xT(b, c) for c in range(DC)]).then_inc(sem("at_fill"), 1)

            def scores(n, fill_done):
                pe.wait_ge(sem("at_flo"), fill_done)
                pe_scores(pe, n, lambda i: (a3_qh[:, i * P:(i + 1) * P], a3_ql[:, i * P:(i + 1) * P]),
                          lambda k: (a3_kh[:, 0:k], a3_kl[:, 0:k]))

            def out_head(h, done, start=False, final=False):
                pe.wait_ge(sem("at_flo"), done)
                r = drh[:, bass.ds(h * D, D)], drl[:, bass.ds(h * D, D)]
                for t in range(TT):
                    last = mm3(pe, acc(t), (a3_zh[:, t * P:(t + 1) * P], a3_zl[:, t * P:(t + 1) * P]), r,
                               start and t % 2 == 0, final)
                    if final and t % 2:
                        last.then_inc(sem("a3_out"), 1)

            def pair(r, first=False, last=False):
                fills = pair_fills(last)
                base = f0 + 2 + r * BODY
                n = r * 2 + n0
                at = {k: base + v[0] for k, v in fills.items()}
                starts = {k: base + v[2] + 1 for k, v in fills.items()}
                bank = {k: v[1] for k, v in fills.items()}
                pe.wait_ge(sem("w_split"), r0 + 2 + r * 2)
                for f in range(2):
                    pe_fill_start(pe, starts["v", 0, f])
                    for t in (2 * f, 2 * f + 1):
                        m = mm3c(pe, ps[:, bank["v", 0, f], (t % 2) * D:(t % 2 + 1) * D], [xTt(b, c, t) for c in range(DC)],
                                 [w(1, c * 2 * P, 2 * P) for c in range(DC)])
                    m.then_inc(sem("at_fill"), 1)
                for hh in range(2):
                    done = last and hh == 1
                    if not done:
                        if hh == 1:
                            pe.wait_ge(sem("w_split"), r0 + 3 + r * 2)
                        qk(1 - hh, [bank["q", hh, 0], bank["k", hh, 0]], [starts["q", hh, 0], starts["k", hh, 0]])
                    if first and hh == 0:
                        pe.wait_ge(sem("x_res"), 4 * u)
                    else:
                        out_head(r * 2 + (hh - 1), (base if hh == 0 else at["z", 0, 0] + 1), start=first)
                    pe_transpose_p(pe, n + hh, hh, a3_p, [bank["p", hh, f] for f in range(3)],
                                   [starts["p", hh, f] for f in range(3)])
                    if not done:
                        scores(n + (hh + 1), at["k", hh, 0] + 1)
                    pe_fill_start(pe, starts["z", hh, 0])
                    pe_pv(pe, ps[:, bank["z", hh, 0], :], at["p", hh, 0],
                          lambda kb: (a3_vh[:, kb, hh * P:(hh + 1) * P], a3_vl[:, kb, hh * P:(hh + 1) * P]),
                          a3_pth, a3_ptl, True, True).then_inc(sem("at_fill"), 1)
                return at

            pe_ready(pe, u)
            pe.wait_ge(sem("w_split"), r0 + 1)
            pe.wait_ge(sem("w_split"), RAW0["wo3"] + 4)
            qk(0, [2, 0], [f0 - 1, f0])
            scores(n0, f0 + 2)
            pair(0, first=True)
            with pe.Fori(1, H // 2 - 1) as r:
                pair(r)
            at = pair(H // 2 - 1, last=True)
            pe.wait_ge(sem("at_flo"), f0 + 7 * H - 1)
            pe_T(pe, u + 1)
            out_head(H - 1, at["z", 1, 0] + 1, final=True)


        def act_att3(s, u):
            b, n0, f0 = u % 2, A3_HEADS[u], A3_FILL[u]

            def pair(r, last=False):
                fills = pair_fills(last)
                base, n = f0 + 2 + r * BODY, r * 2 + n0

                def one(key, dst, cols=T):
                    act_fill(s, base + fills[key][0], fills[key][1], dst, cols)

                for f in range(2):
                    one(("v", 0, f), a3_vh[:, 2 * f:2 * f + 2, :].rearrange("p t n -> p (t n)"))
                for hh in range(2):
                    done = last and hh == 1
                    if not done:
                        one(("q", hh, 0), a3_qh[:, :])
                        one(("k", hh, 0), a3_kh[:, :])
                    for f in range(3):
                        lo, hi = pt_cols(f)
                        one(("p", hh, f), a3_pth[:, lo:hi], hi - lo)
                    if not done:
                        act_exp(s, n + (hh + 1), 1 - hh, SCALE3, a3_p)
                    one(("z", hh, 0), a3_zh[:, :])

            act_fill(s, f0, 2, a3_qh[:, :])
            act_fill(s, f0 + 1, 0, a3_kh[:, :])
            act_exp(s, n0, 0, SCALE3, a3_p)
            pair(0)
            with s.Fori(1, H // 2 - 1) as r:
                pair(r)
            pair(H // 2 - 1, last=True)
            act_T(s, u + 1)

        def dve_att3(v, u):
            b, n0, f0 = u % 2, A3_HEADS[u], A3_FILL[u]

            def pair(r, last=False, first=False):
                fills = pair_fills(last)
                base, n = f0 + 2 + r * BODY, r * 2 + n0

                def one(key, dst, src, cols=T):
                    dve_fill(v, base + fills[key][0], fills[key][1], dst, src, cols)

                for f in range(2):
                    one(("v", 0, f), a3_vl[:, 2 * f:2 * f + 2, :].rearrange("p t n -> p (t n)"),
                        a3_vh[:, 2 * f:2 * f + 2, :].rearrange("p t n -> p (t n)"))
                for hh in range(2):
                    done = last and hh == 1
                    if not done:
                        one(("q", hh, 0), a3_ql[:, :], a3_qh[:, :])
                        one(("k", hh, 0), a3_kl[:, :], a3_kh[:, :])
                    for f in range(3):
                        lo, hi = pt_cols(f)
                        one(("p", hh, f), a3_ptl[:, lo:hi], a3_pth[:, lo:hi], hi - lo)
                    if not done:
                        dve_max(v, n + (hh + 1), 1 - hh, SCALE3)
                        dve_rinv(v, n + (hh + 1), 1 - hh)
                    one(("z", hh, 0), a3_zl[:, :], a3_zh[:, :])
                    if first and hh == 0:
                        dve_stats(v, u + 1)

            dve_fill(v, f0, 2, a3_ql[:, :], a3_qh[:, :])
            dve_fill(v, f0 + 1, 0, a3_kl[:, :], a3_kh[:, :])
            dve_max(v, n0, 0, SCALE3)
            dve_rinv(v, n0, 0)
            pair(0, first=True)
            with v.Fori(1, H // 2 - 1) as r:
                pair(r)
            dve_norm(v, u + 1)
            pair(H // 2 - 1, last=True)
            dve_T(v, u + 1)
            dve_residual(v, u, 1.0, [("a3_out", 2 * b + 1), ("a3_out", 2 * b + 2)])

        def pool_att3(g, u):
            n0 = A3_HEADS[u]

            def pair(r, last=False, first=False):
                for hh in range(2):
                    pool_norm(g, r * 2 + (n0 + hh), hh, a3_p)
                    if not last:
                        pool_chunks(g, u, r + 1, hh)
                if first:
                    pool_ln(g, u + 1)

            pair(0, first=True)
            with g.Fori(1, H // 2 - 1) as r:
                pair(r)
            pair(H // 2 - 1, last=True)



        SPARE = D * D
        NK = NS // P
        table = nc.dram_tensor("delta_table", [SPARE + NS, E], F32, kind="Internal").ap()
        d_sm = d_small[0:E, 0:NA]
        d_smT = d_small[0:NA, 64:72]
        d_max, d_sum, d_ri = d_small[0:E, 72:73], d_small[0:E, 73:74], d_small[0:E, 74:75]
        d_ew = d_small[0:E, 80:144]
        d_colf = d_small[:, 144:160]
        d_dest = d_small[:, 160:176]
        d_pos = d_small[:, 176:192]
        d_dup = d_small[:, 192:208]
        d_thr = d_small[:, 208:216]
        d_sg, d_wt, d_r1, d_r2, d_cmb = [d_work[:, k, :] for k in range(5)]

        def sp_delta(sp):
            sp.wait_ge(sem("x_res"), 8)
            sp.dma_start(d_rowi[:, :], a["idx_row"].to_broadcast([P, NS])).then_inc(sem("d_in"), 16)
            sp.dma_start(d_col[:, 0, :], a["idx_col"]).then_inc(sem("d_in"), 16)
            sp.dma_start(d_pos, a["pos"]).then_inc(sem("d_in"), 16)
            sp.dma_start(d_atoms[:, :], a["atoms"]).then_inc(sem("d_in"), 16)
            sp.dma_start(d_ew, a["expert_atoms"]).then_inc(sem("d_in"), 16)
            sp.dma_start(d_imp[:, :], a["importance"]).then_inc(sem("d_in"), 16)
            sp.dma_start(d_q3[:, :, :], a["weight3"]).then_inc(sem("d_in_q3"), 16)
            sp.wait_ge(sem("d_zero"), 1)
            flat = table.rearrange("(p r) e -> p (r e)", p=P)
            for k in range(4):
                sp.dma_start(flat[:, k * 1056:(k + 1) * 1056], d_zero[:, :]).then_inc(sem("d_zeroed"), 16)
            sp.wait_ge(sem("d_scattered"), 16 * NK)
            for c in range(DC):
                sp.dma_start(d_back[:, c, :], table[c * P * D:(c + 1) * P * D, :].rearrange("(p r) e -> p (r e)", p=P))\
                    .then_inc(sem(f"d_back{c}"), 16)

        def pool_delta(g):
            g.wait_ge(sem("x_res"), 8)
            g.memset(d_zero[:, :], 0.0).then_inc(sem("d_zero"), 1)
            g.wait_ge(sem("d_dest"), 1)
            g.wait_ge(sem("d_cmb"), 3)
            g.wait_ge(sem("d_zeroed"), 64)
            for k in range(NK):
                g.indirect_dma_start(out=table[:, :], out_offset=bass.IndirectOffsetOnAxis(ap=d_desti[:, k:k + 1], axis=0),
                                     in_=d_cmb[:, k * E:(k + 1) * E], in_offset=None).then_inc(sem("d_scattered"), 16)

        def act_delta(s):
            s.wait_ge(sem("d_max"), 1)
            s.activation(d_sm, d_ew, ACT.Exp, bias=d_max, accum_out=d_sum).then_inc(sem("d_exp"), 1)
            s.wait_ge(sem("d_in"), 16 * 6)
            s.activation(d_sg, d_imp[:, :], ACT.Exp, scale=-1.0).then_inc(sem("d_exp"), 1)

        def pe_delta(pe):
            pe.wait_ge(sem("x_res"), 8)
            pe.wait_ge(sem("d_sm"), 1)
            pe.transpose(ps[0:NA, 0, 0:E], d_sm, ident[0:E, 0:E]).then_inc(sem("d_smt"), 1)
            pe.wait_ge(sem("d_smtc"), 1)
            pe.wait_ge(sem("d_in"), 16 * 6)
            for k in range(NK):
                last = pe.matmul(ps[:, 1, k * E:(k + 1) * E], d_atoms[:, k * P:(k + 1) * P], d_smT, start=True, stop=True)
            last.then_inc(sem("d_delta"), 1)
            o = ps[:, 2, 0:NK * 25].rearrange("p (m n) -> p m n", m=NK)
            pe.wait_ge(sem("d_wb"), 4)
            for k in range(NK):
                pe.wait_ge(sem("d_eqtri"), k + 1)
                for m in range(NK):
                    n = 25 if k < m else 24
                    pe.matmul(o[:, m, 0:n], d_eq[:, k % 2, m * P:(m + 1) * P], d_wb[:, k, 0:n],
                              start=(k == 0 and m == 0), stop=False, skip_group_check=True)
                pe.matmul(o[:, k, 24:25], d_tri[:, 1, :], d_wb[:, k, 24:25], start=False, stop=(k == NK - 1),
                          skip_group_check=True).then_inc(sem("d_comb"), 1)
            pe.wait_ge(sem("q_tern"), 1)
            for c in range(DC):
                for oc in range(DC):
                    last = pe.transpose(ps[:, 3, c * D + oc * P:c * D + (oc + 1) * P], d_q3t[:, oc, c * P:(c + 1) * P],
                                        ident[:, :])
            last.then_inc(sem("q_T"), 1)
            pe.wait_ge(sem("q3_ready"), 1)

        def dve_delta(v):
            count = [0]

            def then(ins):
                ins.then_inc(sem("d_step"), 1)
                count[0] += 1

            def settled():
                v.wait_ge(sem("d_step"), count[0])

            v.wait_ge(sem("x_res"), 8)
            v.wait_ge(sem("d_in"), 16 * 6)
            v.tensor_reduce(d_ri, d_ew, AX_X, ALU.max).then_inc(sem("d_mx0"), 1)
            v.wait_ge(sem("d_mx0"), 1)
            v.tensor_scalar(d_max, d_ri, -1.0, None, ALU.mult).then_inc(sem("d_max"), 1)
            v.wait_ge(sem("const_in"), 16 * CONSTS)
            then(v.tensor_copy(d_tri[:, 0, :], tri[:, :]))
            v.wait_ge(sem("d_in"), 16 * 6)
            then(v.tensor_copy(d_row[:, :], d_rowi[:, :]))
            v.wait_ge(sem("d_in"), 16 * 6)
            then(v.tensor_copy(d_colf, d_col[:, 0, :]))
            then(v.tensor_scalar(d_col[:, 1, :], d_col[:, 0, :], D - 1, 8, ALU.bitwise_and, ALU.logical_shift_left))
            then(v.tensor_scalar(d_col[:, 2, :], d_col[:, 0, :], 8, None, ALU.logical_shift_right))
            v.wait_ge(sem("d_exp"), 1)
            then(v.reciprocal(d_ri, d_sum))
            settled()
            then(v.tensor_tensor(d_col[:, 3, :], d_col[:, 1, :], d_col[:, 2, :], ALU.bitwise_or))
            v.tensor_scalar(d_sm, d_sm, d_ri, None, ALU.mult).then_inc(sem("d_sm"), 1)
            v.wait_ge(sem("d_exp"), 2)
            then(v.tensor_scalar(d_sg, d_sg, 1.0, None, ALU.add))
            settled()
            then(v.reciprocal(d_sg, d_sg))
            then(v.tensor_copy(d_dest, d_col[:, 3, :]))
            v.wait_ge(sem("d_smt"), 1)
            v.tensor_copy(d_smT, ps[0:NA, 0, 0:E]).then_inc(sem("d_smtc"), 1)
            v.wait_ge(sem("d_delta"), 1)
            settled()
            then(v.tensor_tensor(d_wt, ps[:, 1, 0:P], d_sg, ALU.mult))
            settled()
            wk = d_wt.rearrange("p (k e) -> p k e", e=E)
            v.memset(d_wb[:, :, 24:25], 1.0).then_inc(sem("d_wb"), 1)
            v.tensor_copy(d_wb[:, :, 0:8], wk).then_inc(sem("d_wb"), 1)
            v.wait_ge(sem("d_wb"), 2)
            then(v.tensor_tensor(d_r1.rearrange("p (k e) -> p k e", e=E), wk, d_wb[:, :, 0:8], ALU.subtract))
            settled()
            r1, r2 = [x_.rearrange("p (k e) -> p k e", e=E) for x_ in (d_r1, d_r2)]
            v.tensor_copy(d_wb[:, :, 8:16], r1).then_inc(sem("d_wb"), 1)
            v.wait_ge(sem("d_wb"), 3)
            then(v.tensor_tensor(r2, r1, d_wb[:, :, 8:16], ALU.subtract))
            settled()
            v.tensor_copy(d_wb[:, :, 16:24], r2).then_inc(sem("d_wb"), 1)
            for k in range(NK):
                if positive(k - 1):
                    v.wait_ge(sem("d_comb"), k - 1)
                then(v.tensor_scalar(d_eq[:, k % 2, :], d_row[:, :], d_colf[:, k:k + 1], None, ALU.is_equal))
                settled()
                if positive(k):
                    v.wait_ge(sem("d_comb"), k)
                v.tensor_tensor(d_tri[:, 1, :], d_eq[:, k % 2, k * P:(k + 1) * P], d_tri[:, 0, :], ALU.mult)\
                    .then_inc(sem("d_eqtri"), 1)
            v.wait_ge(sem("d_in_q3"), 16)
            then(v.tensor_scalar(d_q3n[:, :, :], d_q3[:, :, :], -1.0, None, ALU.mult))
            settled()
            then(v.tensor_tensor(d_q3t[:, :, :], d_q3[:, :, :], d_q3n[:, :, :], ALU.max))
            settled()
            then(v.tensor_reduce(d_thr[:, 0:2], d_q3t[:, :, :], AX_X, ALU.add))
            settled()
            then(v.tensor_scalar(d_thr[:, 2:4], d_thr[:, 0:2], 1.0 / D, 0.7, ALU.mult, ALU.mult))
            settled()
            for oc in range(DC):
                then(v.tensor_scalar(d_q3[:, oc, :], d_q3[:, oc, :], d_thr[:, 2 + oc:3 + oc], None, ALU.is_gt))
                then(v.tensor_scalar(d_q3n[:, oc, :], d_q3n[:, oc, :], d_thr[:, 2 + oc:3 + oc], None, ALU.is_gt))
            settled()
            v.tensor_tensor(d_q3t[:, :, :], d_q3[:, :, :], d_q3n[:, :, :], ALU.subtract).then_inc(sem("q_tern"), 1)
            v.wait_ge(sem("d_comb"), NK)
            o = ps[:, 2, 0:NK * 25].rearrange("p (m n) -> p m n", m=NK)
            cmb = d_cmb.rearrange("p (k e) -> p k e", e=E)
            v.tensor_copy(cmb, o[:, :, 0:8]).then_inc(sem("d_cmb"), 1)
            v.wait_ge(sem("d_cmb"), 1)
            v.tensor_tensor(cmb, cmb, o[:, :, 8:16], ALU.add).then_inc(sem("d_cmb"), 1)
            v.wait_ge(sem("d_cmb"), 2)
            v.tensor_tensor(cmb, cmb, o[:, :, 16:24], ALU.add).then_inc(sem("d_cmb"), 1)
            then(v.tensor_scalar(d_dup, o[:, :, 24], 1.0, None, ALU.min))
            v.wait_ge(sem("d_in"), 16 * 6)
            then(v.tensor_tensor(d_pos, d_pos, d_dest, ALU.subtract))
            settled()
            then(v.tensor_tensor(d_pos, d_pos, d_dup, ALU.mult))
            settled()
            then(v.tensor_tensor(d_dest, d_dest, d_pos, ALU.add))
            settled()
            v.tensor_copy(d_desti[:, :], d_dest).then_inc(sem("d_dest"), 1)
            v.wait_ge(sem("q_T"), 1)
            v.tensor_copy(qt[:, :, :].rearrange("p c n -> p (c n)"), ps[:, 3, :]).then_inc(sem("q3_ready"), 2)
            for c in range(DC):
                v.wait_ge(sem(f"d_back{c}"), 16)
                src = d_back[:, c, :].rearrange("p (r e) -> p e r", e=E)
                for h in range(2):
                    at = (c * E + 4 * h) * D
                    hi = drh[:, at:at + 4 * D].rearrange("p (e r) -> p e r", e=4)
                    lo = drl[:, at:at + 4 * D].rearrange("p (e r) -> p e r", e=4)
                    v.tensor_copy(hi, src[:, 4 * h:4 * h + 4, :]).then_inc(sem("delta_hi"), 1)
                    v.wait_ge(sem("delta_hi"), 2 * c + h + 1)
                    v.tensor_tensor(lo, src[:, 4 * h:4 * h + 4, :], f32(hi), ALU.subtract).then_inc(sem("delta_lo"), 1)


        def sp_start(sp):
            for b in range(NB):
                sp.dma_start(x[:, TT * b:TT * (b + 1), :], a["x"][b].rearrange("(i p) d -> p i d", p=P))\
                    .then_inc(sem(f"x_in{b}"), 16)
            sp_chunks(sp, 0, 0, 0)
            sp_chunks(sp, 0, 0, 1)

        CONSTS = 11

        def act_start(s):
            for dst, name, signal in ((ident, "ident", "ident_in"), (maskcol, "mask", "const_in"), (tri, "tri", "const_in"),
                                      (iota8, "iota8", "const_in"), (headmask, "headmask", "const_in"),
                                      (router_w, "router", "const_in"), (rgp, "rg_params", "const_in"),
                                      (lin_cols, "lin_cols", "const_in"), (att_cols, "att_cols", "const_in")):
                full = dst[tuple(slice(None) for _ in dst.shape)]
                s.dma_start(full, a[name]).then_inc(sem(signal), 16)
            s.dma_start(bias3[:, :], a["bias3"].to_broadcast([P, D])).then_inc(sem("const_in"), 16)
            s.dma_start(lin_bout[:, :], a["lin_bout"].to_broadcast([P, D])).then_inc(sem("const_in"), 16)
            s.dma_start(att_bo[:, :], a["att_bo"].to_broadcast([P, D])).then_inc(sem("const_in"), 16)

        def act_softplus(s):
            s.wait_ge(sem("sp_abs"), 1)
            s.activation(sp_y, sp_abs, ACT.Exp, scale=-1.0).then_inc(sem("sp_y"), 1)
            s.wait_ge(sem("sp_u"), 1)
            s.activation(sp_ln, sp_u, ACT.Ln).then_inc(sem("sp_ln"), 1)

        sp_abs, sp_y, sp_u, sp_v, sp_ln, sp_z, sp_m, sp_t = [small[:, 380 + 2 * k:382 + 2 * k] for k in range(8)]

        def pool_start(g):
            g.memset(nhalf[:, :], -0.5).then_inc(sem("const_set"), 1)
            g.memset(ones[:, :], 1.0).then_inc(sem("const_set"), 1)
            g.memset(w9, 1.0).then_inc(sem("const_set"), 1)

        def dve_start(v):
            v.wait_ge(sem("ident_in"), 16)
            v.tensor_copy(identb[:, :], ident[:, :]).then_inc(sem("const_ident"), 1)
            dve_ln(v, 0)
            dve_T(v, 0)

        def dve_consts(v):
            v.wait_ge(sem("const_in"), 16 * CONSTS)
            v.tensor_copy(maskb[:, :], maskcol[:, :]).then_inc(sem("const_mask"), 1)
            v.wait_ge(sem("const_in"), 16 * CONSTS)
            v.tensor_copy(rwh[:, :, :, :], router_w[:, :, :, :]).then_inc(sem("rw_hi"), 1)
            v.wait_ge(sem("rw_hi"), 1)
            v.tensor_tensor(rwl[:, :, :, :], router_w[:, :, :, :], f32(rwh[:, :, :, :]), ALU.subtract)\
                .then_inc(sem("const_router"), 1)
            v.wait_ge(sem("const_in"), 16 * CONSTS)
            v.wait_ge(sem("const_set"), 3)
            v.tensor_scalar(iota8[:, :, :], iota8[:, :, :], 1.0, None, ALU.mult).then_inc(sem("const_iota"), 1)
            v.wait_ge(sem("const_in"), 16 * CONSTS)
            p = rgp[:, :, 7]
            v.tensor_scalar(sp_t, p, -1.0, None, ALU.mult).then_inc(sem("sp_1"), 1)
            v.wait_ge(sem("sp_1"), 1)
            v.tensor_tensor(sp_abs, p, sp_t, ALU.max).then_inc(sem("sp_abs"), 1)
            v.wait_ge(sem("sp_y"), 1)
            v.tensor_scalar(sp_u, sp_y, 1.0, None, ALU.add).then_inc(sem("sp_u"), 1)
            v.wait_ge(sem("sp_u"), 1)
            v.tensor_scalar(sp_v, sp_u, 1.0, None, ALU.subtract).then_inc(sem("sp_2"), 1)
            v.wait_ge(sem("sp_2"), 1)
            v.tensor_scalar(sp_z, sp_v, 0.0, None, ALU.is_equal).then_inc(sem("sp_2"), 1)
            v.wait_ge(sem("sp_2"), 2)
            v.tensor_tensor(sp_v, sp_v, sp_z, ALU.add).then_inc(sem("sp_2"), 1)
            v.wait_ge(sem("sp_2"), 3)
            v.reciprocal(sp_v, sp_v).then_inc(sem("sp_2"), 1)
            v.wait_ge(sem("sp_2"), 4)
            v.wait_ge(sem("sp_ln"), 1)
            v.tensor_tensor(sp_ln, sp_ln, sp_v, ALU.mult).then_inc(sem("sp_2"), 1)
            v.wait_ge(sem("sp_2"), 5)
            v.tensor_tensor(sp_ln, sp_ln, sp_z, ALU.add).then_inc(sem("sp_2"), 1)
            v.wait_ge(sem("sp_2"), 6)
            v.tensor_tensor(sp_ln, sp_ln, sp_y, ALU.mult).then_inc(sem("sp_2"), 1)
            v.tensor_scalar(sp_m, p, 0.0, None, ALU.max).then_inc(sem("sp_2"), 1)
            v.wait_ge(sem("sp_2"), 8)
            v.tensor_tensor(sp_ln, sp_ln, sp_m, ALU.add).then_inc(sem("sp_2"), 1)
            v.wait_ge(sem("sp_2"), 9)
            v.tensor_scalar(rgp[:, :, 10], sp_ln, -8.0, None, ALU.mult).then_inc(sem("const_rgp"), 1)

        PE_OF = {FFN0: pe_ffn, RGLRU: pe_rglru, MOE1: pe_moe1, LIN1: pe_lin1, MOE2: pe_ffn, ATT2: pe_att2, FFN3: pe_ffn3,
                 ATT3: pe_att3}
        ACT_OF = {FFN0: act_ffn, RGLRU: act_rglru, MOE1: act_moe1, LIN1: act_lin1, MOE2: act_ffn, ATT2: act_att2,
                  FFN3: act_T_next, ATT3: act_att3}
        DVE_OF = {FFN0: dve_ffn, RGLRU: dve_rglru, MOE1: dve_moe1, LIN1: dve_lin1, MOE2: dve_ffn, ATT2: dve_att2,
                  FFN3: dve_ffn3, ATT3: dve_att3}
        RES_STOP = dict(rglru=2, wt=2, lin1=4, att2=12, wo3=17)
        DELTA_BEFORE = 2

        @block.sync
        def _(sp):
            sp_start(sp)
            for kind, what in ORDER:
                if kind == "r":
                    if stop > RES_STOP[what]:
                        sp_resident(sp, what)
                elif what < stop:
                    n = CHUNKS[KIND[what]] // 2
                    with sp.Fori(1 if what == 0 else 0, n) as i:
                        for p in range(2):
                            sp_chunks(sp, what, i, p)
                if what == "wt" and stop > 2:
                    sp_delta(sp)
                if what == "lin1" and stop > 8:
                    sp.wait_ge(sem("x_res"), 4 * 8)
                    sp.dma_start(lin_tok[:, :, :, :], a["rope_tok"]).then_inc(sem("lin_in"), 16)
                    sp.dma_start(lin_feat[:, :, :], a["rope_feat"]).then_inc(sem("lin_in"), 16)
                    sp.dma_start(lin_bkv[:, :], a["lin_bkv"].to_broadcast([P, 2 * D])).then_inc(sem("lin_in"), 16)
                if what == "att2" and stop > 14:
                    sp.wait_ge(sem("x_res"), 4 * 14)
                    sp.dma_start(a2_bv[:, :], a["att_bv"].to_broadcast([P, D])).then_inc(sem("a2_bv_in"), 16)
            for b in range(NB):
                sp.wait_ge(sem("x_res"), 4 * (stop - 1 + b))
                sp.dma_start(out[b].rearrange("(i p) d -> p i d", p=P), x[:, TT * b:TT * (b + 1), :])\
                    .then_inc(sem("stored"), 16)
            sp.wait_ge(sem("stored"), 32)

        @block.gpsimd
        def _(g):
            pool_start(g)
            started = set()

            def pre(u):
                if u < stop:
                    pool_chunks(g, u, 0, 0)
                    pool_chunks(g, u, 0, 1)

            def rest(u):
                if u < stop:
                    for p in range(2):
                        pool_chunks(g, u, 1, p)
                    pool_ln(g, u + 1)
                    with g.Fori(2, CHUNKS[KIND[u]] // 2) as i:
                        for p in range(2):
                            pool_chunks(g, u, i, p)

            def some(u, f, *args):
                if u < stop:
                    f(*args)

            pool_ln(g, 0)
            pre(0)
            rest(0)
            pre(1)
            rest(1)
            some(2, pool_resident, g, "rglru")
            some(2, pool_resident, g, "wt")
            some(2, pool_delta, g)
            pool_ln(g, 3)
            pre(4)
            pool_ln(g, 4)
            rest(4)
            pre(5)
            rest(5)
            some(4, pool_resident, g, "lin1", 3)
            pool_ln(g, 7)
            pool_ln(g, 8)
            some(8, pool_lin1, g, 8)
            some(9, pool_lin1, g, 9)
            pre(12)
            pool_ln(g, 11)
            pool_ln(g, 12)
            rest(12)
            pre(13)
            rest(13)
            some(12, pool_resident, g, "att2", 9)
            some(14, pool_att2, g, 14)
            some(15, pool_att2, g, 15)
            pre(16)
            rest(16)
            pre(17)
            rest(17)
            some(17, pool_resident, g, "wo3", 15)
            pool_ln(g, 19)
            pool_ln(g, 20)
            pre(20)
            some(20, pool_att3, g, 20)
            pre(21)
            some(21, pool_att3, g, 21)
            pool_ln(g, 23)

        @block.tensor
        def _(pe):
            pe_T(pe, 0)
            for u in range(stop):
                if u == DELTA_BEFORE:
                    pe_delta(pe)
                PE_OF[KIND[u]](pe, u)

        @block.scalar
        def _(s):
            act_start(s)
            act_T(s, 0)
            for u in range(stop):
                if u == DELTA_BEFORE:
                    act_delta(s)
                ACT_OF[KIND[u]](s, u)

        @block.vector
        def _(v):
            dve_start(v)
            for u in range(stop):
                if u == DELTA_BEFORE:
                    dve_delta(v)
                DVE_OF[KIND[u]](v, u)


def layout(**t):
    f = {k: np.asarray(v) for k, v in t.items()}
    one = np.float32
    a = {"x": f["L0_attn_x"]}

    def ffn_chunks(gate, up, down, n, extra):
        rows = n * P

        def padded(m):
            return np.concatenate([m, np.zeros((rows - m.shape[0], m.shape[1]), m.dtype)]) if m.shape[0] < rows else m

        def cols(m):
            return padded(m).reshape(n, P, DC, P).transpose(0, 3, 2, 1).reshape(n, P, DC * P)

        parts = [cols(gate), cols(up), padded(down).reshape(n, P, D)] + extra
        return np.ascontiguousarray(np.concatenate(parts, axis=2))

    def rows_by_chunk(m):
        return m.reshape(DC, P, -1).transpose(1, 0, 2).reshape(P, -1)

    a["w0"] = ffn_chunks(f["L0_ffn_w_gate"], f["L0_ffn_w_up"], f["L0_ffn_w_down"].T, CH0, [])
    member = np.zeros((CH2 * P, P), one)
    member[:FS, E] = 1
    for e in range(E):
        member[FS + e * FE:FS + (e + 1) * FE, e] = 1
    a["w2"] = ffn_chunks(np.concatenate([f["L2_ffn_Wsg"], f["L2_ffn_Wg"].reshape(E * FE, D)]),
                         np.concatenate([f["L2_ffn_Wsu"], f["L2_ffn_Wu"].reshape(E * FE, D)]),
                         np.concatenate([f["L2_ffn_Wsd"].T, f["L2_ffn_Wd"].transpose(0, 2, 1).reshape(E * FE, D)]),
                         CH2, [member.reshape(CH2, P, P).transpose(0, 2, 1)])

    def block_diag(m):
        o = np.zeros((DC, P, P), one)
        for n in range(H):
            i = n % 8
            o[n // 8, 16 * i:16 * i + 16, 16 * i:16 * i + 16] = m[n]
        return o.transpose(1, 0, 2).reshape(P, DC * P)

    a["rglru"] = np.concatenate([rows_by_chunk(f["L0_attn_W_xy"].T), block_diag(f["L0_attn_ig_w"]),
                                 block_diag(f["L0_attn_ag_w"]), rows_by_chunk(f["L0_attn_W_resid"].T)], axis=1)
    cp = np.zeros((P, DC, 16), one)
    for k in range(4):
        cp[:, :, k] = f["L0_attn_conv_w"][k].reshape(DC, P).T
    for k, name in enumerate(("conv_b", "ig_b", "ag_b", "a_param")):
        cp[:, :, 4 + k] = f["L0_attn_" + name].reshape(DC, P).T
    a["rg_params"] = cp

    a["wt"] = rows_by_chunk(f["L1_ffn_W"].T)
    idx = f["L1_ffn_mask_idx"]
    a["idx_row"] = idx.reshape(1, NS)
    a["idx_col"] = np.ascontiguousarray(idx.reshape(NS // P, P).T)
    a["pos"] = np.ascontiguousarray((D * D + np.arange(NS, dtype=one)).reshape(NS // P, P).T)
    a["atoms"] = f["L1_ffn_atoms"]
    a["expert_atoms"] = f["L1_ffn_expert_atom_weights"]
    a["importance"] = np.ascontiguousarray(f["L1_ffn_importance"].T.reshape(NS // P, P, E).transpose(1, 0, 2).reshape(P, P))
    a["router"] = np.ascontiguousarray(np.stack([m.T.reshape(DC, P, E).transpose(1, 0, 2)
                                                 for m in (f["L1_ffn_gate_w"], f["L2_ffn_Wr"])], axis=1))
    w_in, b_in = f["L1_attn_W_in"], f["L1_attn_b_in"]
    swap = np.arange(P).reshape(-1, 2)[:, ::-1].reshape(-1)
    q = w_in[:, 0:D]
    qs = np.concatenate([q[:, 0:P], q[:, swap], q[:, P:D]], axis=1)
    a["lin1"] = np.concatenate([rows_by_chunk(w_in[:, D:3 * D]), rows_by_chunk(qs), rows_by_chunk(f["L1_attn_W_out"])], axis=1)
    cols = np.zeros((P, 8), one)
    cols[:, 0:2] = f["L1_attn_ln_w"].reshape(DC, P).T
    cols[:, 2:4] = f["L1_attn_ln_b"].reshape(DC, P).T
    cols[:, 4], cols[:, 5], cols[:, 6] = b_in[0:P], b_in[swap], b_in[P:D]
    a["lin_cols"] = cols
    a["lin_bkv"] = b_in[D:3 * D].reshape(1, 2 * D)
    a["lin_bout"] = f["L1_attn_b_out"].reshape(1, D)
    rot = D // 2
    inv = (one(1.0) / np.power(one(10000.0), (np.arange(0, rot, 2, dtype=one) / one(rot)))).astype(one)
    ang = np.repeat((np.arange(T, dtype=one)[:, None] * inv[None, :]).astype(one), 2, axis=1)
    sign = np.where(np.arange(rot) % 2 == 0, -1, 1).astype(one)
    tab = np.stack([np.cos(ang), np.sin(ang) * sign]).astype(one)
    a["rope_tok"] = np.ascontiguousarray(tab.reshape(2, TT, P, rot).transpose(2, 0, 1, 3))
    a["rope_feat"] = np.ascontiguousarray(tab.transpose(2, 0, 1))

    a["att2"] = np.concatenate([rows_by_chunk(f["L2_attn_W" + k].T) for k in "qkvo"], axis=1)
    a["att_cols"] = np.ascontiguousarray(np.concatenate([f["L2_attn_bq"].reshape(DC, P).T, f["L2_attn_bk"].reshape(DC, P).T], axis=1))
    a["att_bv"] = f["L2_attn_bv"].reshape(1, D)
    a["att_bo"] = f["L2_attn_bo"].reshape(1, D)

    def by_pair(m):
        return m.reshape(H // 2, 2, HD3, DC, P).transpose(0, 4, 3, 1, 2).reshape(H // 2, P, DC * 2 * HD3)

    a["qk3"] = np.ascontiguousarray(np.concatenate([by_pair(f["L3_attn_W_Q"]), by_pair(f["L3_attn_W_K"])], axis=2))
    a["v3"] = np.ascontiguousarray(by_pair(f["L3_attn_W_V"]))
    a["wo3"] = np.ascontiguousarray(f["L3_attn_W_O"].transpose(2, 0, 1).reshape(P, H * D))
    a["weight3"] = np.ascontiguousarray(f["L3_ffn_weight"].reshape(DC, P, D).transpose(1, 0, 2))
    a["bias3"] = f["L3_ffn_bias"].reshape(1, D)
    a["ident"] = np.eye(P, dtype=one)
    a["mask"] = np.where(np.arange(P)[None, :] > np.arange(P)[:, None], one(NEG), one(0))
    a["tri"] = (np.arange(P)[:, None] < np.arange(P)[None, :]).astype(one)
    a["iota8"] = np.ascontiguousarray(np.broadcast_to(np.arange(E, dtype=one), (P, TT, E)))
    a["headmask"] = (np.arange(P)[:, None] // HD2 == np.arange(8)[None, :]).astype(one)
    return {k: np.ascontiguousarray(v) for k, v in a.items()}


def kernel(**inputs):
    import concourse.bacc as bacc
    from concourse.bass_utils import run_bass_kernel_spmd

    arrays = layout(**inputs)
    nc = bacc.Bacc("TRN2", target_bir_lowering=False, num_devices=1)
    aps = {k: nc.dram_tensor(f"in_{k}", v.shape, mybir.dt.from_np(v.dtype), kind="ExternalInput").ap()
           for k, v in arrays.items()}
    out = nc.dram_tensor("out", (NB, T, D), F32, kind="ExternalOutput").ap()
    build(nc, aps, out)
    r = run_bass_kernel_spmd(nc, [{f"in_{k}": v for k, v in arrays.items()}], core_ids=[0])
    return r.results[0]["out"]
```

```python
from contextlib import ExitStack

import numpy as np

import concourse.bass as bass
from concourse import mybir

ALU = mybir.AluOpType
ACT = mybir.ActivationFunctionType
AX_X = mybir.AxisListType.X
F32 = mybir.dt.float32
F32R = mybir.dt.float32r
BF16 = mybir.dt.bfloat16
I32 = mybir.dt.int32
U32 = mybir.dt.uint32

P = 128
NB = 2
T = 512
D = 256
TT = T // P
DC = D // P
EPS = 1e-5
NEG = -1e30

N_UNITS = 24
FFN0, RGLRU, MOE1, LIN1, MOE2, ATT2, FFN3, ATT3 = "ffn0", "rglru", "moe1", "lin1", "moe2", "att2", "ffn3", "att3"
SUBLAYERS = [FFN0, RGLRU, FFN0, MOE1, LIN1, MOE1, MOE2, ATT2, MOE2, FFN3, ATT3, FFN3]
KIND = [SUBLAYERS[u // 2] for u in range(N_UNITS)]

HID0 = 1024
E = 8
NS = 2048
NA = 64
FE, FS = 176, 352
CH0 = HID0 // P
PLAIN2 = FS // P
CH2 = -(-(E * FE + FS) // P)
H = 16
HD2 = D // H
HD3 = 128
SCALE2 = float(HD2) ** -0.5
SCALE3 = float(HD3) ** -0.5

W_LO = 32
SLOT = 1024
W_GATE, W_UP, W_DOWN, W_IND = 0, DC * P, 2 * DC * P, 2 * DC * P + D
PAIR_COLS = (2 * DC * 2 * P, DC * 2 * P)
RES = {"rglru": (2048, 2), "wt": (2 * D, 2), "lin1": (2304, 4), "att2": (2048, 2), "wo3": (H * D, 4)}
RES_AT = {"rglru": 0, "wt": E * 2 * D, "lin1": 0, "att2": 0, "wo3": 0}

ORDER = [("u", 0), ("u", 1), ("r", "rglru"), ("r", "wt"), ("u", 4), ("u", 5), ("r", "lin1"), ("u", 12), ("u", 13),
         ("r", "att2"), ("u", 16), ("u", 17), ("r", "wo3"), ("u", 20), ("u", 21)]
CHUNKS = {FFN0: CH0, MOE2: CH2, ATT3: H}
RAW0, RING0, FFN_AT = {}, {}, {}
_raw = _ring = _ffn = 0
for _kind, _what in ORDER:
    RAW0[_what] = _raw
    if _kind == "u":
        RING0[_what] = _ring
        _n = CHUNKS[KIND[_what]]
        _ring += _n
        if KIND[_what] != ATT3:
            FFN_AT[_what] = _ffn
            _ffn += _n
        _raw += _n
    else:
        _raw += RES[_what][1]

KEYS = [P * (i + 1) for i in range(TT)]
S_COLS = [max(2 * P, k) for k in KEYS]
S_AT = [(3, 0), (3, 256), (4, 0), (5, 0)]
P_AT = [sum(KEYS[:i]) for i in range(TT + 1)]
PT_N = [T - P * kb for kb in range(TT)]
PT_AT = [sum(PT_N[:i]) for i in range(TT + 1)]
FILLS = [[0], [1], [2, 3]]


def build(nc, a, out, stop=N_UNITS):
    with ExitStack() as ctx:
        def sb(name, shape, dt=F32):
            return ctx.enter_context(nc.sbuf_tensor(name, shape, dt))

        sems = {}

        def sem(name):
            if name not in sems:
                sems[name] = ctx.enter_context(nc.semaphore(name))
            return sems[name]

        def positive(count):
            return not isinstance(count, int) or count > 0

        ps = ctx.enter_context(nc.psum_tensor("ps", [P, 8, 512], F32))

        x = sb("x", [P, NB * TT, D])
        xn = sb("xn", [P, NB, TT, D])
        xh = sb("xh", [P, NB, DC, T], F32R)
        xl = sb("xl", [P, NB, DC, T], F32R)
        stats = sb("stats", [P, NB, TT, 6])
        mv = sb("mv", [P, NB, TT, 2])
        veps = sb("veps", [P, NB, TT])
        rstd = sb("rstd", [P, NB, TT])
        nhalf = sb("nhalf", [P, TT])
        raw = sb("raw", [P, 2, SLOT])
        wh = sb("wh", [P, 2, SLOT], F32R)
        wl = sb("wl", [P, 2, SLOT], F32R)
        rch = sb("rch", [P, 2304], F32R)
        rcl = sb("rcl", [P, 2304], F32R)
        drh = sb("drh", [P, E * 2 * D + 2 * D], F32R)
        drl = sb("drl", [P, E * 2 * D + 2 * D], F32R)
        qt = sb("qt", [P, DC, D], F32R)
        ident = sb("ident", [P, P])
        identb = sb("identb", [P, P], BF16)
        tri = sb("tri", [P, P])
        maskcol = sb("maskcol", [P, P])
        maskb = sb("maskb", [P, P], BF16)
        ones = sb("ones", [P, P])
        iota8 = sb("iota8", [P, TT, E])
        headmask = sb("headmask", [P, 8])
        router_w = sb("router_w", [P, 2, DC, E])
        bias3 = sb("bias3", [P, D])
        def f32(ap):
            return ap.bitcast(F32)

        block = ctx.enter_context(nc.Block())

        def sublayer_tensors(**shapes):
            with ExitStack() as own:
                return [own.enter_context(nc.sbuf_tensor(name, shape, dt)) for name, (shape, dt) in shapes.items()]

        small = sb("small", [P, 512])
        lg = small[:, 0:32].rearrange("p (i e) -> p i e", i=TT)
        top8 = small[:, 32:64].rearrange("p (i e) -> p i e", i=TT)
        dl = small[:, 64:96].rearrange("p (i e) -> p i e", i=TT)
        ex = small[:, 96:128].rearrange("p (i e) -> p i e", i=TT)
        m0 = small[:, 128:160].rearrange("p (i e) -> p i e", i=TT)
        m1 = small[:, 160:192].rearrange("p (i e) -> p i e", i=TT)
        mask = small[:, 192:224].rearrange("p (i e) -> p i e", i=TT)
        wsel = small[:, 224:256].rearrange("p (i e) -> p i e", i=TT)
        w_moe1 = small[:, 256:256 + TT * E].rearrange("p (i e) -> p i e", i=TT)
        idxf = small[:, 296:304].rearrange("p (i e) -> p i e", i=TT)
        rsum = small[:, 304:308]
        rinv = small[:, 308:312]
        h_sum, h_inv, h_max, h_nmx = [small[:, 400 + 8 * k:408 + 8 * k].rearrange("p (h i) -> p h i", h=2) for k in range(4)]
        idx8 = sb("idx8", [P, TT, 8], U32)
        rwh = sb("rwh", [P, 2, DC, E], F32R)
        rwl = sb("rwl", [P, 2, DC, E], F32R)
        rgp = sb("rgp", [P, DC, 16])
        lin_cols = sb("lin_cols", [P, 8])
        lin_bout = sb("lin_bout", [P, D])
        att_cols = sb("att_cols", [P, 4])
        att_bo = sb("att_bo", [P, D])
        d_desti = sb("d_desti", [P, 16], U32)

        ffn_hh, ffn_hl, ffn_w, ffn_wt, ffn_s, ffn_hf = sublayer_tensors(
            ffn_hh=([P, 2, T], F32R), ffn_hl=([P, 2, T], F32R), ffn_w=([P, TT, P], F32), ffn_wt=([P, T], F32R),
            ffn_s=([P, 2, T], F32), ffn_hf=([P, 2, T], F32))
        w_copies = ffn_w[:, :, :].rearrange("p i (g n) -> p i g n", n=W_LO)[:, :, 0:2, :]
        rg_xp, rg_xc, rg_gy, rg_ga, rg_a, rg_ch, rg_cl, rg_gh, rg_gl = sublayer_tensors(
            rg_xp=([P, DC, T + 4], F32), rg_xc=([P, DC, T], F32), rg_gy=([P, DC, T], F32), rg_ga=([P, DC, T], F32),
            rg_a=([P, DC, T], F32), rg_ch=([P, DC, T], F32R), rg_cl=([P, DC, T], F32R), rg_gh=([P, DC, T], F32R),
            rg_gl=([P, DC, T], F32R))
        rg_gx = rg_xp[:, :, 4:T + 4]
        rg_th = rg_ga
        (lin_tok, lin_feat, lin_bkv, lin_xn, lin_tmp, lin_kv, lin_kr, lin_ks, lin_qa, lin_qb, lin_qf, 
         lin_qh, lin_ql) = sublayer_tensors(
            lin_tok=([P, 2, TT, P], F32),
            lin_feat=([P, 2, T], F32),
            lin_bkv=([P, 2 * D], F32), lin_xn=([P, NB, TT, D], F32), lin_tmp=([P, DC, T], F32), lin_kv=([P, TT, 2 * D], F32),
            lin_kr=([P, TT, P], F32), lin_ks=([P, TT, P], F32), lin_qa=([P, T], F32), lin_qb=([P, T], F32),
            lin_qf=([P, DC, T], F32), 
            lin_qh=([P, DC, T], F32R), lin_ql=([P, DC, T], F32R))
        VS = P + HD2
        (a2_qh, a2_ql, a2_kh, a2_kl, a2_vf, a2_vh, a2_vl, a2_sq, a2_sk, a2_pth, a2_ptl, a2_p, a2_bv) = sublayer_tensors(
            a2_qh=([P, DC, T], F32R), a2_ql=([P, DC, T], F32R), a2_kh=([P, DC, T], F32R), a2_kl=([P, DC, T], F32R),
            a2_vf=([P, TT, D], F32), a2_vh=([P, TT, 8, VS], F32R), a2_vl=([P, TT, 8, VS], F32R),
            a2_sq=([P, 2, T], F32R), a2_sk=([P, 2, T], F32R), a2_pth=([P, PT_AT[TT]], F32R),
            a2_ptl=([P, PT_AT[TT]], F32R), a2_p=([P, 2, P_AT[TT]], F32), a2_bv=([P, D], F32))
        (a3_qh, a3_ql, a3_kh, a3_kl, a3_vh, a3_vl, a3_pth, a3_ptl, a3_zh, a3_zl, a3_p) = sublayer_tensors(
            a3_qh=([P, T], F32R), a3_ql=([P, T], F32R), a3_kh=([P, T], F32R), a3_kl=([P, T], F32R),
            a3_vh=([P, TT, 2 * HD3], F32R), a3_vl=([P, TT, 2 * HD3], F32R), a3_pth=([P, PT_AT[TT]], F32R),
            a3_ptl=([P, PT_AT[TT]], F32R), a3_zh=([P, T], F32R), a3_zl=([P, T], F32R), a3_p=([P, 2, P_AT[TT]], F32))
        (_ffn_pad, d_rowi, d_atoms, d_imp, d_back, d_row, d_eq, d_col, d_work, d_wb, d_small, d_tri, d_q3, d_q3n,
         d_q3t) = sublayer_tensors(
            _ffn_pad=([P, 10 * T], F32), d_rowi=([P, NS], I32), d_atoms=([NA, NS], F32), d_imp=([P, P], F32),
            d_back=([P, 2, NS], F32), d_row=([P, NS], F32), d_eq=([P, 3, NS], BF16), d_col=([P, 5, 16], I32),
            d_work=([P, 6, P], F32), d_wb=([P, 16, 25], BF16), d_small=([P, 256], F32), d_tri=([P, 3, P], BF16),
            d_q3=([P, DC, D], F32), d_q3n=([P, DC, D], F32), d_q3t=([P, DC, D], F32))
        d_zero = d_back[:, 0, 0:1056]

        def mm3(pe, o, l, r, start, stop):
            pe.matmul(o, l[0], r[0], start=start, stop=False, skip_group_check=True)
            pe.matmul(o, l[0], r[1], start=False, stop=False, skip_group_check=True)
            return pe.matmul(o, l[1], r[0], start=False, stop=stop, skip_group_check=True)

        def mm3c(pe, o, ls, rs):
            for c in range(len(ls)):
                last = mm3(pe, o, ls[c], rs[c], c == 0, c == len(ls) - 1)
            return last

        def acc(t):
            return ps[:, 6 + t // 2, (t % 2) * D:(t % 2 + 1) * D]

        def xT(b, c):
            return xh[:, b, c, :], xl[:, b, c, :]

        def xTt(b, c, t):
            return xh[:, b, c, t * P:(t + 1) * P], xl[:, b, c, t * P:(t + 1) * P]

        def rc(at, n, k=P):
            return rch[0:k, at:at + n], rcl[0:k, at:at + n]

        def dr(at, n):
            return drh[:, at:at + n], drl[:, at:at + n]

        def dve_stats(v, u):
            if u >= stop:
                return
            b = u % 2
            if u < 2:
                v.wait_ge(sem(f"x_in{b}"), 16)
            else:
                v.wait_ge(sem("x_res"), 4 * (u - 1))
            for i in range(TT):
                v.bn_stats(stats[:, b, i, :], x[:, TT * b + i, :]).then_inc(sem("ln_stats"), 1)
            for i in range(TT):
                v.wait_ge(sem("ln_stats"), TT * u + i + 1)
                v.bn_aggr(mv[:, b, i, :], stats[:, b, i, :]).then_inc(sem("ln_aggr"), 1)

        def dve_norm(v, u):
            if u >= stop:
                return
            b = u % 2
            v.wait_ge(sem("ln_rstd"), u + 1)
            if positive(2 * (u - 1)):
                v.wait_ge(sem("ln_T"), 2 * (u - 1))
            for i in range(TT):
                v.tensor_scalar(xn[:, b, i, :], x[:, TT * b + i, :], mv[:, b, i, 0:1], rstd[:, b, i:i + 1],
                                ALU.subtract, ALU.mult).then_inc(sem("ln_xn"), 1)
            if KIND[u] == LIN1:
                for i in range(TT):
                    v.wait_ge(sem("ln_xn"), TT * u + i + 1)
                    v.bn_stats(l_st[:, 6 * i:6 * i + 6], xn[:, b, i, :]).then_inc(sem("l_stats"), 1)
                for i in range(TT):
                    v.wait_ge(sem("l_stats"), TT * b + i + 1)
                    v.bn_aggr(l_mv[:, 2 * i:2 * i + 2], l_st[:, 6 * i:6 * i + 6]).then_inc(sem("l_aggr"), 1)

        def dve_norm2(v, u):
            if u >= stop:
                return
            b = u % 2
            v.wait_ge(sem("l_rs"), b + 1)
            for i in range(TT):
                v.tensor_scalar(lin_xn[:, b, i, :], xn[:, b, i, :], l_mv[:, 2 * i:2 * i + 1], l_rs[:, i:i + 1],
                                ALU.subtract, ALU.mult).then_inc(sem("l_xn"), 1)

        def dve_ln(v, u):
            dve_stats(v, u)
            dve_norm(v, u)

        def pool_ln(g, u):
            if u >= stop:
                return
            b = u % 2
            g.wait_ge(sem("const_set"), 1)
            g.wait_ge(sem("ln_aggr"), TT * (u + 1))
            g.tensor_scalar(veps[:, b, :], mv[:, b, :, 1], EPS, 1.0, ALU.add, ALU.mult).then_inc(sem("ln_veps"), 1)
            g.wait_ge(sem("ln_veps"), u + 1)
            g.tensor_tensor(rstd[:, b, :], veps[:, b, :], nhalf[:, :], ALU.pow).then_inc(sem("ln_rstd"), 1)

        def pe_T(pe, u):
            if u >= stop:
                return
            b = u % 2
            pe.wait_ge(sem("const_ident"), 1)
            pe.wait_ge(sem("ln_xn"), TT * (u + 1))
            if positive(2 * u):
                pe.wait_ge(sem("ln_lo"), 2 * u)
            src = xn
            if KIND[u] == LIN1:
                src = lin_xn
                pe.wait_ge(sem("l_xn"), TT * (b + 1))
            for c in range(DC):
                for i in range(TT):
                    last = pe.transpose(ps[:, c, i * P:(i + 1) * P], src[:, b, i, c * P:(c + 1) * P], ident[:, :])
                last.then_inc(sem("ln_T"), 1)

        def act_T(s, u):
            if u >= stop:
                return
            b = u % 2
            for c in range(DC):
                s.wait_ge(sem("ln_T"), 2 * u + c + 1)
                if KIND[u] == LIN1:
                    s.activation(xh[:, b, c, :], ps[:, c, :], ACT.Identity, bias=lin_cols[:, 2 + c:3 + c],
                                 scale=lin_cols[:, c:c + 1]).then_inc(sem("ln_hi"), 1)
                else:
                    s.activation(xh[:, b, c, :], ps[:, c, :], ACT.Copy).then_inc(sem("ln_hi"), 1)

        def dve_T(v, u):
            if u >= stop:
                return
            b = u % 2
            for c in range(DC):
                v.wait_ge(sem("ln_hi"), 2 * u + c + 1)
                src = ps[:, c, :]
                if KIND[u] == LIN1:
                    v.tensor_scalar(lin_tmp[:, c, :], src, lin_cols[:, c:c + 1], lin_cols[:, 2 + c:3 + c],
                                    ALU.mult, ALU.add).then_inc(sem("l_tmp"), 1)
                    v.wait_ge(sem("l_tmp"), DC * b + c + 1)
                    src = lin_tmp[:, c, :]
                v.tensor_tensor(xl[:, b, c, :], src, f32(xh[:, b, c, :]), ALU.subtract).then_inc(sem("ln_lo"), 1)

        def pe_ready(pe, u):
            pe.wait_ge(sem("ln_lo"), 2 * (u + 1))

        def dve_residual(v, u, scale, ready):
            b = u % 2
            for t in range(TT):
                if t % 2 == 0:
                    name, value = ready[t // 2]
                    v.wait_ge(sem(name), value)
                if KIND[u] == MOE1:
                    v.wait_ge(sem("moe_acc"), 2 * TT * (E // 2) * (MOE_AT[u] + 1))
                xt = x[:, TT * b + t, :]
                v.scalar_tensor_tensor(out=xt, in0=acc(t), scalar=scale, in1=xt, op0=ALU.mult, op1=ALU.add)\
                    .then_inc(sem("x_res"), 1)

        def sp_chunk(sp, r, p, src, cols):
            if positive(r - 1):
                sp.wait_ge(sem("w_split"), r - 1)
            sp.dma_start(raw[:, p, 0:cols], src).then_inc(sem(f"w_raw{p}"), 16)

        def pool_split(g, r, half, p, n, oh, ol, at=0):
            if half is not None:
                g.wait_ge(sem(f"w_raw{p}"), half * 16 + 16)
            if not isinstance(r, int):
                g.sem_inc(sem("pool_turn"), 1)
            g.tensor_scalar(oh, raw[:, p, at:n], 1.0, 1.0, ALU.mult, ALU.mult).then_inc(sem("w_hi"), 1)
            g.wait_ge(sem("w_hi"), r + 1)
            g.tensor_tensor(ol, raw[:, p, at:n], f32(oh), ALU.subtract).then_inc(sem("w_split"), 1)

        def chunk_cols(u, p):
            return PAIR_COLS[p] if KIND[u] == ATT3 else (W_DOWN + D if KIND[u] == FFN0 else W_IND + P)

        def sp_chunks(sp, u, i, p):
            r = RAW0[u] + p + i * 2
            n = chunk_cols(u, p)
            if KIND[u] == ATT3:
                src = a["qk3" if p == 0 else "v3"]
                k = i
            else:
                src = a["w0" if KIND[u] == FFN0 else "w2"]
                k = i * 2 + p
            sp_chunk(sp, r, p, src[bass.ds(k, 1)].rearrange("a p n -> p (a n)"), n)

        def pool_chunks(g, u, i, p):
            r, ring = RAW0[u] + p + i * 2, RING0[u] + p + i * 2
            n = chunk_cols(u, p)
            if KIND[u] != ATT3:
                g.wait_ge(sem(f"w_raw{p}"), i * 16 + 8 * RAW0[u] + 16)
                done = FFN_AT[u] + p + i * 2 - 1
                if positive(done):
                    g.wait_ge(sem("ffn_up"), done)
                if not isinstance(i, int):
                    g.sem_inc(sem("pool_turn"), 1)
                g.tensor_scalar(wh[:, p, 0:W_DOWN], raw[:, p, 0:W_DOWN], 1.0, 1.0, ALU.mult, ALU.mult)\
                    .then_inc(sem("w_gu_hi"), 1)
                g.wait_ge(sem("w_gu_hi"), done + 2)
                g.tensor_tensor(wl[:, p, 0:W_DOWN], raw[:, p, 0:W_DOWN], f32(wh[:, p, 0:W_DOWN]), ALU.subtract)\
                    .then_inc(sem("w_gu"), 1)
                if positive(ring - 1):
                    g.wait_ge(sem("w_used"), ring - 1)
                pool_split(g, r, None, p, n, wh[:, p, W_DOWN:n], wl[:, p, W_DOWN:n], W_DOWN)
                return
            if not (isinstance(i, int) and i == 0):
                g.wait_ge(sem("at_fill"), A3_FILL[u] + 2 + (4, 2)[p] - BODY + i * BODY)
            elif u == 21:
                g.wait_ge(sem("at_fill"), A3_FILL[20] + 2 + (4, 2)[p] + 7 * BODY)
            else:
                if positive(ring - 1):
                    g.wait_ge(sem("w_used"), ring - 1)
            pool_split(g, r, i + RAW0[u] // 2, p, n, wh[:, p, 0:n], wl[:, p, 0:n])

        def sp_resident(sp, name):
            cols, k = RES[name]
            n = cols // k
            for j in range(k):
                sp_chunk(sp, RAW0[name] + j, j % 2, a[name][:, j * n:(j + 1) * n], n)

        def pool_resident(g, name, done_unit=None, pieces=None):
            cols, k = RES[name]
            n, at = cols // k, RES_AT[name]
            dh, dlo = (drh, drl) if name in ("wt", "wo3") else (rch, rcl)
            if done_unit is not None:
                g.wait_ge(sem("x_res"), 4 * (done_unit + 1))
            for j in pieces or range(k):
                pool_split(g, RAW0[name] + j, (RAW0[name] + j) // 2, j % 2, n,
                           dh[:, at + j * n:at + (j + 1) * n], dlo[:, at + j * n:at + (j + 1) * n])

        def w(p, at, n=P):
            return wh[:, p, at:at + n], wl[:, p, at:at + n]

        ROUTED = [u for u in range(N_UNITS) if KIND[u] in (MOE1, MOE2)]
        MOE_AT = {u: n for n, u in enumerate(v for v in range(N_UNITS) if KIND[v] == MOE1)}
        MOE2_AT = {u: n for n, u in enumerate(v for v in range(N_UNITS) if KIND[v] == MOE2)}
        R_OPS = 18

        def rep(ap, n=E):
            return ap.to_broadcast([P, TT, n])

        def pe_logits(pe, u, bank):
            b, layer = u % 2, 0 if KIND[u] == MOE1 else 1
            pe.wait_ge(sem("const_router"), 1)
            for t in range(TT):
                for c in range(DC):
                    rh, rl = rwh[:, layer, c, :], rwl[:, layer, c, :]
                    last = mm3(pe, ps[:, bank, t * E:(t + 1) * E], xTt(b, c, t), (rh, rl), c == 0, c == DC - 1)
            last.then_inc(sem("rt_logits"), 1)

        def dve_router(v, u, bank):
            n = ROUTED.index(u)
            base = R_OPS * n
            count = [base]

            def then(ins):
                ins.then_inc(sem("rt_step"), 1)
                count[0] += 1

            def settled():
                v.wait_ge(sem("rt_step"), count[0])

            v.wait_ge(sem("rt_logits"), n + 1)
            pl = ps[:, bank, 0:TT * E].rearrange("p (i e) -> p i e", i=TT)
            if KIND[u] == MOE1:
                then(v.tensor_scalar(lg, pl, 50.0, -50.0, ALU.min, ALU.max))
            else:
                then(v.tensor_copy(lg, pl))
            settled()
            for i in range(TT):
                then(v.max(top8[:, i, :], lg[:, i, :]))
            settled()
            then(v.tensor_tensor(dl, lg, rep(top8[:, :, 0:1]), ALU.subtract))
            for i in range(TT):
                then(v.max_index(idx8[:, i, :], top8[:, i, :], lg[:, i, :]))
            settled()
            then(v.tensor_copy(idxf, idx8[:, :, 0:2]))
            settled()
            v.wait_ge(sem("const_iota"), 1)
            then(v.tensor_tensor(m0, iota8[:, :, :], rep(idxf[:, :, 0:1]), ALU.is_equal))
            then(v.tensor_tensor(m1, iota8[:, :, :], rep(idxf[:, :, 1:2]), ALU.is_equal))
            settled()
            then(v.tensor_tensor(mask, m0, m1, ALU.add))
            v.wait_ge(sem("rt_exp"), n + 1)
            settled()
            if KIND[u] == MOE1:
                then(v.tensor_tensor(wsel, ex, mask, ALU.mult))
                settled()
                then(v.tensor_reduce(rsum, wsel, AX_X, ALU.add))
                settled()
                then(v.reciprocal(rinv, rsum))
                settled()
                then(v.scalar_tensor_tensor(out=w_moe1, in0=wsel, scalar=0.5,
                                            in1=rep(rinv.rearrange("p (i o) -> p i o", o=1)),
                                            op0=ALU.mult, op1=ALU.mult))
            else:
                then(v.tensor_reduce(rsum, ex, AX_X, ALU.add))
                then(v.tensor_tensor(wsel, ex, mask, ALU.mult))
                settled()
                then(v.reciprocal(rinv, rsum))
                settled()
                v.wait_ge(sem("w_zero"), 1 + MOE2_AT[u] // 2)
                then(v.tensor_tensor(w_copies[:, :, :, 0:E],
                                     wsel.rearrange("p i (o e) -> p i o e", o=1).to_broadcast([P, TT, 2, E]),
                                     rinv.rearrange("p (i o n) -> p i o n", o=1, n=1).to_broadcast([P, TT, 2, E]),
                                     ALU.mult))
            settled()
            assert count[0] == base + R_OPS

        def pool_zero_w(g, units):
            g.wait_ge(sem("x_res"), 4 * units)
            g.memset(ffn_w[:, :, :], 0.0).then_inc(sem("w_zeros"), 1)
            g.wait_ge(sem("w_zeros"), 1 + (units > 10))
            g.memset(w_copies[:, :, :, E:E + 1], 1.0).then_inc(sem("w_zero"), 1)

        def act_router(s, u):
            n = ROUTED.index(u)
            s.wait_ge(sem("rt_step"), R_OPS * n + 6)
            s.activation(ex, dl, ACT.Exp).then_inc(sem("rt_exp"), 1)


        def ffn_loop(eng, u, step, first, last):
            n = CHUNKS[KIND[u]]
            first()
            if u in DELTA_UNITS:
                for j in range(2, n - 2):
                    step(j, j % 2)
            else:
                with eng.Fori(0, (n - 4) // 2) as i:
                    for p in range(2):
                        step(i * 2 + (2 + p), p)
            last(n)

        def pe_ffn(pe, u):
            b, f0, r0 = u % 2, FFN_AT[u], RAW0[u]
            moe = KIND[u] == MOE2

            def gate_up(j, p, early=False):
                pe.wait_ge(sem("w_gu"), f0 + 1 + j)
                if not early:
                    pe.wait_ge(sem("ffn_silu"), f0 - 1 + j)
                    pe.wait_ge(sem("ffn_h"), f0 - 1 + j)
                mm3c(pe, ps[:, 2 + p, :], [w(p, W_GATE + c * P) for c in range(DC)], [xT(b, c) for c in range(DC)])\
                    .then_inc(sem("ffn_gate"), 1)
                mm3c(pe, ps[:, 4 + p, :], [w(p, W_UP + c * P) for c in range(DC)], [xT(b, c) for c in range(DC)])\
                    .then_inc(sem("ffn_up"), 1)

            def spread(j, p):
                pe.wait_ge(sem("wt_lo"), MOE2_AT[u] + 1)
                pe.wait_ge(sem("w_split"), r0 + 1 + j)
                pe.matmul(ps[:, p, :], wh[:, p, W_IND:W_IND + P], ffn_wt[:, :], start=True, stop=True)\
                    .then_inc(sem("ffn_wbc"), 1)

            def down(j, p, first=False, final=False):
                pe.wait_ge(sem("ffn_lo"), f0 + 1 + j)
                if not moe:
                    pe.wait_ge(sem("w_split"), r0 + 1 + j)
                if first:
                    if positive(4 * u):
                        pe.wait_ge(sem("x_res"), 4 * u)
                for t in range(TT):
                    last = mm3(pe, acc(t), (ffn_hh[:, p, t * P:(t + 1) * P], ffn_hl[:, p, t * P:(t + 1) * P]),
                               w(p, W_DOWN, D), first and t % 2 == 0, final)
                    if final and t == 1:
                        last.then_inc(sem("ffn_half"), 1)
                last.then_inc(sem("w_used"), 1)

            def first():
                pe_ready(pe, u)
                if moe:
                    pe_logits(pe, u, 0)
                gate_up(0, 0, early=True)
                gate_up(1, 1, early=True)
                if u in DELTA_UNITS:
                    pe_delta(pe, u, 1)
                down(0, 0, first=True)
                if moe:
                    pe.wait_ge(sem("rt_step"), R_OPS * (ROUTED.index(u) + 1))
                    for i in range(TT):
                        last = pe.transpose(ps[:, 1, i * P:(i + 1) * P], ffn_w[:, i, :], ident[:, :])
                    last.then_inc(sem("wt_T"), 1)

            def step(j, p):
                gate_up(j, p)
                if u in DELTA_UNITS:
                    pe_delta(pe, u, j)
                if moe:
                    spread(j, p)
                down(j - 1, 1 - p)

            def last(n):
                step(n - 2, 0)
                step(n - 1, 1)
                if moe:
                    pe.wait_ge(sem("ffn_h"), f0 + n)
                if u in DELTA_UNITS:
                    pe_delta_end(pe, u)
                pe_T(pe, u + 1)
                down(n - 1, 1, final=True)

            ffn_loop(pe, u, step, first, last)

        def act_ffn(s, u):
            f0, g0 = FFN_AT[u], RING0[u]

            def step(j, p):
                s.wait_ge(sem("ffn_gate"), f0 + 1 + j)
                if positive(f0 - 1 + j):
                    s.wait_ge(sem("ffn_h"), f0 - 1 + j)
                s.activation(ffn_s[:, p, :], ps[:, 2 + p, :], ACT.Silu).then_inc(sem("ffn_silu"), 1)
                if u in DELTA_UNITS:
                    act_delta(s, u, j)
                s.wait_ge(sem("ffn_h"), f0 + 1 + j)
                if positive(g0 - 1 + j):
                    s.wait_ge(sem("w_used"), g0 - 1 + j)
                s.activation(ffn_hh[:, p, :], ffn_hf[:, p, :], ACT.Copy).then_inc(sem("ffn_hi"), 1)

            def first():
                if KIND[u] == MOE2:
                    act_router(s, u)
                    step(0, 0)
                    step(1, 1)
                    s.wait_ge(sem("wt_T"), MOE2_AT[u] + 1)
                    s.activation(ffn_wt[:, :], ps[:, 1, :], ACT.Copy).then_inc(sem("wt_hi"), 1)
                else:
                    step(0, 0)
                    step(1, 1)

            def last(n):
                step(n - 2, 0)
                step(n - 1, 1)
                act_T(s, u + 1)

            ffn_loop(s, u, step, first, last)

        def dve_ffn(v, u):
            f0, g0 = FFN_AT[u], RING0[u]
            moe = KIND[u] == MOE2

            def step(j, p, plain=not moe):
                v.wait_ge(sem("ffn_silu"), f0 + 1 + j)
                v.wait_ge(sem("ffn_up"), f0 + 1 + j)
                if positive(f0 - 1 + j):
                    v.wait_ge(sem("ffn_lo"), f0 - 1 + j)
                hf = ffn_hf[:, p, :]
                if not plain:
                    k0 = (CH2 - PLAIN2) * MOE2_AT[u] - PLAIN2
                    v.tensor_tensor(hf, ffn_s[:, p, :], ps[:, 4 + p, :], ALU.mult).then_inc(sem("ffn_h0"), 1)
                    v.wait_ge(sem("ffn_h0"), k0 + 1 + j)
                    v.wait_ge(sem("ffn_wbc"), k0 + 1 + j)
                    v.tensor_tensor(hf, hf, ps[:, p, :], ALU.mult).then_inc(sem("ffn_h"), 1)
                else:
                    v.tensor_tensor(hf, ffn_s[:, p, :], ps[:, 4 + p, :], ALU.mult).then_inc(sem("ffn_h"), 1)
                v.wait_ge(sem("ffn_hi"), f0 + 1 + j)
                if positive(g0 - 1 + j):
                    v.wait_ge(sem("w_used"), g0 - 1 + j)
                v.tensor_tensor(ffn_hl[:, p, :], hf, f32(ffn_hh[:, p, :]), ALU.subtract).then_inc(sem("ffn_lo"), 1)
                if u in DELTA_UNITS:
                    dve_delta(v, u, j)

            def first():
                if moe:
                    dve_router(v, u, 0)
                step(0, 0, plain=True)
                step(1, 1, plain=True)
                if moe:
                    v.wait_ge(sem("wt_hi"), MOE2_AT[u] + 1)
                    low = slice(W_LO, W_LO + E + 1)
                    v.tensor_tensor(ffn_wt[low, :], ps[low, 1, :], f32(ffn_wt[low, :]), ALU.subtract)\
                        .then_inc(sem("wt_lo"), 1)
                dve_stats(v, u + 1)

            def last(n):
                dve_norm(v, u + 1)
                step(n - 2, 0)
                step(n - 1, 1)
                dve_T(v, u + 1)
                dve_residual(v, u, 0.5, [("ffn_half", FFN_UNITS.index(u) + 1), ("w_used", g0 + n)])

            ffn_loop(v, u, step, first, last)

        FFN_UNITS = [u for u in range(N_UNITS) if KIND[u] in (FFN0, MOE2)]

        RG_IG, RG_AG, RG_WR = 1024, 1280, 1536
        def pe_rglru(pe, u):
            b = u % 2
            pe.wait_ge(sem("w_split"), RAW0["rglru"] + 2)
            pe_ready(pe, u)
            for m in range(4):
                mm3c(pe, ps[:, 2 + m, :], [rc(c * 512 + m * P, P) for c in range(DC)], [xT(b, c) for c in range(DC)])\
                    .then_inc(sem("rg_xy"), 1)
            for c in range(DC):
                pe.wait_ge(sem("rg_clo"), DC * b + c + 1)
                mm3(pe, ps[:, c, :], rc(RG_IG + c * P, P), (rg_ch[:, c, :], rg_cl[:, c, :]), True, True)\
                    .then_inc(sem("rg_gates"), 1)
                mm3(pe, ps[:, 2 + c, :], rc(RG_AG + c * P, P), (rg_ch[:, c, :], rg_cl[:, c, :]), True, True)\
                    .then_inc(sem("rg_gates"), 1)
            pe.wait_ge(sem("rg_sigm"), 4 * (b + 1))
            pe_T(pe, u + 1)
            pe.wait_ge(sem("rg_glo"), DC * (b + 1))
            pe.wait_ge(sem("x_res"), 4 * u)
            for t in range(TT):
                last = mm3c(pe, acc(t), [(rg_gh[:, c, t * P:(t + 1) * P], rg_gl[:, c, t * P:(t + 1) * P])
                                         for c in range(DC)], [rc(RG_WR + c * D, D) for c in range(DC)])
                if t % 2:
                    last.then_inc(sem("rg_out"), 1)

        def act_rglru(s, u):
            b = u % 2
            s.wait_ge(sem("const_rgp"), 1)
            for c in range(DC):
                s.wait_ge(sem("rg_xy"), 4 * b + c + 1)
                s.wait_ge(sem("rg_pad"), 1)
                s.activation(rg_xp[:, c, 3:3 + T], ps[:, 2 + c, :], ACT.Copy).then_inc(sem("rg_x"), 1)
            for c in range(DC):
                s.wait_ge(sem("rg_xy"), 4 * b + DC + c + 1)
                s.activation(rg_gy[:, c, :], ps[:, 4 + c, :], ACT.Gelu).then_inc(sem("rg_gelu"), 1)
            for c in range(DC):
                s.wait_ge(sem("rg_conv"), 8 * b + 4 * c + 4)
                s.activation(rg_ch[:, c, :], rg_xc[:, c, :], ACT.Copy).then_inc(sem("rg_chi"), 1)
            for c in range(DC):
                s.wait_ge(sem("rg_gates"), 4 * b + 2 * c + 1)
                s.activation(rg_gx[:, c, :], ps[:, c, :], ACT.Sigmoid, bias=rgp[:, c, 5:6])\
                    .then_inc(sem("rg_sigm"), 1)
                s.wait_ge(sem("rg_gates"), 4 * b + 2 * c + 2)
                s.activation(rg_ga[:, c, :], ps[:, 2 + c, :], ACT.Sigmoid, bias=rgp[:, c, 6:7])\
                    .then_inc(sem("rg_sigm"), 1)
            for c in range(DC):
                s.wait_ge(sem("rg_sigm"), 4 * b + 2 * c + 2)
                s.activation(rg_a[:, c, :], rg_ga[:, c, :], ACT.Exp, scale=rgp[:, c, 10:11])\
                    .then_inc(sem("rg_a"), 1)
                s.activation(rg_th[:, c, :], rg_ga[:, c, :], ACT.Tanh, scale=rgp[:, c, 10:11])\
                    .then_inc(sem("rg_th"), 1)
            for c in range(DC):
                s.wait_ge(sem("rg_m2"), DC * b + c + 1)
                s.activation(rg_th[:, c, :], rg_th[:, c, :], ACT.Sqrt, scale=-1.0).then_inc(sem("rg_sqrt"), 1)
            act_T(s, u + 1)
            for c in range(DC):
                s.wait_ge(sem("rg_g"), DC * b + c + 1)
                s.activation(rg_gh[:, c, :], rg_gy[:, c, :], ACT.Copy).then_inc(sem("rg_ghi"), 1)

        def dve_rglru(v, u):
            b = u % 2
            v.wait_ge(sem("const_rgp"), 1)
            if b == 0:
                v.memset(rg_xp[:, :, 0:3], 0.0).then_inc(sem("rg_pad"), 1)
                v.wait_ge(sem("rg_pad"), 1)
            for c in range(DC):
                v.wait_ge(sem("rg_x"), DC * b + c + 1)
                v.tensor_scalar(rg_xc[:, c, :], rg_xp[:, c, 0:T], rgp[:, c, 0:1], rgp[:, c, 4:5], ALU.mult, ALU.add)\
                    .then_inc(sem("rg_conv"), 1)
                for k in range(1, 4):
                    v.wait_ge(sem("rg_conv"), 8 * b + 4 * c + k)
                    v.scalar_tensor_tensor(out=rg_xc[:, c, :], in0=rg_xp[:, c, k:k + T], scalar=rgp[:, c, k:k + 1],
                                           in1=rg_xc[:, c, :], op0=ALU.mult, op1=ALU.add).then_inc(sem("rg_conv"), 1)
                v.wait_ge(sem("rg_chi"), DC * b + c + 1)
                v.tensor_tensor(rg_cl[:, c, :], rg_xc[:, c, :], f32(rg_ch[:, c, :]), ALU.subtract)\
                    .then_inc(sem("rg_clo"), 1)
            dve_stats(v, u + 1)
            for c in range(DC):
                v.wait_ge(sem("rg_sigm"), 4 * b + 2 * c + 1)
                v.tensor_tensor(rg_xc[:, c, :], rg_gx[:, c, :], rg_xc[:, c, :], ALU.mult).then_inc(sem("rg_n"), 1)
            for c in range(DC):
                v.wait_ge(sem("rg_a"), DC * b + c + 1)
                v.wait_ge(sem("rg_n"), 2 * DC * b + c + 1)
                v.tensor_tensor(rg_gx[:, c, :], rg_a[:, c, :], rg_a[:, c, :], ALU.mult).then_inc(sem("rg_a2"), 1)
                v.wait_ge(sem("rg_a2"), DC * b + c + 1)
                v.wait_ge(sem("rg_th"), DC * b + c + 1)
                v.scalar_tensor_tensor(out=rg_th[:, c, :], in0=rg_gx[:, c, :], scalar=1.0, in1=rg_th[:, c, :],
                                       op0=ALU.add, op1=ALU.mult).then_inc(sem("rg_m2"), 1)
            dve_norm(v, u + 1)
            for c in range(DC):
                v.wait_ge(sem("rg_sqrt"), DC * b + c + 1)
                v.tensor_tensor(rg_xc[:, c, :], rg_xc[:, c, :], rg_th[:, c, :], ALU.mult).then_inc(sem("rg_n"), 1)
            for c in range(DC):
                v.wait_ge(sem("rg_n"), 2 * DC * b + DC + c + 1)
                v.tensor_tensor_scan(rg_xc[:, c, :], rg_a[:, c, :], rg_xc[:, c, :], 0.0, ALU.mult, ALU.add)\
                    .then_inc(sem("rg_scan"), 1)
            for c in range(DC):
                v.wait_ge(sem("rg_scan"), DC * b + c + 1)
                v.wait_ge(sem("rg_gelu"), DC * b + c + 1)
                v.tensor_tensor(rg_gy[:, c, :], rg_gy[:, c, :], rg_xc[:, c, :], ALU.mult).then_inc(sem("rg_g"), 1)
            dve_T(v, u + 1)
            for c in range(DC):
                v.wait_ge(sem("rg_ghi"), DC * b + c + 1)
                v.tensor_tensor(rg_gl[:, c, :], rg_gy[:, c, :], f32(rg_gh[:, c, :]), ALU.subtract)\
                    .then_inc(sem("rg_glo"), 1)
            dve_residual(v, u, 1.0, [("rg_out", 2 * b + 1), ("rg_out", 2 * b + 2)])

        def pe_moe1(pe, u):
            b, m = u % 2, MOE_AT[u]
            pairs = E // 2
            pe_ready(pe, u)
            pe_logits(pe, u, 0)
            pe.wait_ge(sem("delta_lo"), 4)
            pe.wait_ge(sem("w_split"), RAW0["wt"] + 2)

            def pair(k):
                for t in range(TT):
                    if not isinstance(k, int) or k > 0:
                        pe.wait_ge(sem("moe_acc"), 2 * TT * pairs * m - 2 * TT + 2 * t + 2 + k * 2 * TT)
                    for c in range(DC):
                        at = (c * E + k * 2) * D
                        r = drh[:, bass.ds(at, 2 * D)], drl[:, bass.ds(at, 2 * D)]
                        last = mm3(pe, ps[:, 2 + t, :], xTt(b, c, t), r, c == 0, c == DC - 1)
                    last.then_inc(sem("moe_mm"), 1)

            pair(0)
            with pe.Fori(1, pairs) as k:
                pair(k)
            pe.wait_ge(sem("rt_step"), R_OPS * ROUTED.index(u) + 1)
            pe_T(pe, u + 1)
            pe.wait_ge(sem("x_res"), 4 * u)
            for t in range(TT):
                last = mm3c(pe, acc(t), [xTt(b, c, t) for c in range(DC)],
                            [dr(RES_AT["wt"] + c * D, D) for c in range(DC)])
                if t % 2:
                    last.then_inc(sem("moe_w"), 1)

        def act_moe1(s, u):
            act_router(s, u)
            act_T(s, u + 1)

        def dve_moe1(v, u):
            b, m = u % 2, MOE_AT[u]
            pairs = E // 2
            dve_router(v, u, 0)
            for k in range(pairs):
                for t in range(TT):
                    v.wait_ge(sem("moe_mm"), TT * pairs * m + TT * k + t + 1)
                    for e in range(2):
                        n = 2 * TT * pairs * m + 2 * (TT * k + t) + e
                        if positive(n):
                            v.wait_ge(sem("moe_acc"), n)
                        xt = x[:, TT * b + t, :]
                        v.scalar_tensor_tensor(out=xt, in0=ps[:, 2 + t, e * D:(e + 1) * D],
                                               scalar=w_moe1[:, t, 2 * k + e:2 * k + e + 1], in1=xt,
                                               op0=ALU.mult, op1=ALU.add).then_inc(sem("moe_acc"), 1)
                if k == 0:
                    dve_ln(v, u + 1)
                if k == 1 and KIND[min(u + 1, N_UNITS - 1)] == LIN1:
                    dve_norm2(v, u + 1)
            dve_T(v, u + 1)
            dve_residual(v, u, 0.5, [("moe_w", 2 * m + 1), ("moe_w", 2 * m + 2)])

        def act_T_next(s, u):
            act_T(s, u + 1)

        def pe_ffn3(pe, u):
            b, m = u % 2, F3_AT[u]
            pe_ready(pe, u)
            pe.wait_ge(sem("q3_ready"), 2)
            pe.wait_ge(sem("x_res"), 4 * u)
            for t in range(TT):
                n = 0
                for c in range(DC):
                    for half in xTt(b, c, t):
                        last = pe.matmul(acc(t), half, qt[:, c, :], start=(n == 0), stop=(n == 3))
                        n += 1
                if t % 2:
                    last.then_inc(sem("f3_out"), 1)
            pe_T(pe, u + 1)

        def dve_ffn3(v, u):
            b, m = u % 2, F3_AT[u]
            dve_ln(v, u + 1)
            v.wait_ge(sem("const_in"), 16 * CONSTS)
            for t in range(TT):
                xt = x[:, TT * b + t, :]
                v.scalar_tensor_tensor(out=xt, in0=bias3[:, :], scalar=0.5, in1=xt, op0=ALU.mult, op1=ALU.add)\
                    .then_inc(sem("f3_bias"), 1)
            v.wait_ge(sem("f3_bias"), 4 * (m + 1))
            dve_residual(v, u, 0.5, [("f3_out", 2 * m + 1), ("f3_out", 2 * m + 2)])
            dve_T(v, u + 1)

        F3_AT = {u: n for n, u in enumerate(v for v in range(N_UNITS) if KIND[v] == FFN3)}


        L_Q, L_WO = 1024, 1792

        def pool_rsqrt(g, dst, src, n, name, eps=None):
            g.tensor_tensor(dst, src, nhalf[:, 0:n], ALU.pow).then_inc(sem(name), 1)

        def pe_lin1(pe, u):
            b = u % 2
            pe.wait_ge(sem("w_split"), RAW0["lin1"] + 4)
            pe_ready(pe, u)
            for t in range(TT):
                mm3c(pe, ps[:, 2 + t, :], [xTt(b, c, t) for c in range(DC)], [rc(c * 2 * D, 2 * D) for c in range(DC)])\
                    .then_inc(sem("l_kvmm"), 1)
            for k in range(3):
                if k == 0:
                    pe.wait_ge(sem("l_kv"), TT * b + 3)
                mm3c(pe, ps[:, 2 + k, :], [rc(L_Q + (c * 3 + k) * P, P) for c in range(DC)],
                     [xT(b, c) for c in range(DC)]).then_inc(sem("l_qmm"), 1)
            pe.wait_ge(sem("x_res"), 4 * u)
            pe.wait_ge(sem("l_prod"), TT * (b + 1))
            for c in range(DC):
                for t in range(TT):
                    last = pe.matmul(ps[:, 6, c:c + 1], lin_xn[:, b, t, c * P:(c + 1) * P], ones[:, 0:1],
                                     start=(t == 0), stop=(t == TT - 1))
            last.then_inc(sem("l_sum"), 1)
            pe_T(pe, u + 1)
            pe.wait_ge(sem("l_qlo"), DC * (b + 1))
            for t in range(TT):
                last = mm3c(pe, acc(t), [(lin_qh[:, c, t * P:(t + 1) * P], lin_ql[:, c, t * P:(t + 1) * P])
                                         for c in range(DC)], [rc(L_WO + c * D, D) for c in range(DC)])
                if t % 2:
                    last.then_inc(sem("l_out"), 1)

        def act_lin1(s, u):
            b = u % 2
            for t in range(TT):
                s.wait_ge(sem("l_rope"), 4 * (TT * b + t + 1))
                s.activation(lin_sq[:, t, :], lin_kv[:, t, 0:D], ACT.Square, accum_out=lin_ss[:, t:t + 1])\
                    .then_inc(sem("l_ss"), 1)
            for c in range(DC):
                s.wait_ge(sem("l_qf"), 4 * b + 3 + c)
                s.activation(lin_qh[:, c, :], lin_qf[:, c, :], ACT.Copy).then_inc(sem("l_qhi"), 1)
            act_T(s, u + 1)

        lin_sq = lin_qf[:, :, :].rearrange("p c (a n) -> p (c a) n", a=2)
        lin_ss, lin_rn, lin_a = small[:, 320:324], small[:, 324:328], small[:, 328:330]
        l_mv, l_st, l_ve, l_rs = small[:, 336:344], small[:, 344:368], small[:, 368:372], small[:, 372:376]

        def pool_ln2(g, u):
            b = u % 2
            g.wait_ge(sem("l_aggr"), TT * (b + 1))
            g.tensor_scalar(l_ve, l_mv.rearrange("p (i k) -> p i k", k=2)[:, :, 1], EPS, 1.0, ALU.add, ALU.mult)\
                .then_inc(sem("l_ve"), 1)
            g.wait_ge(sem("l_ve"), b + 1)
            pool_rsqrt(g, l_rs, l_ve, TT, "l_rs")

        def pool_lin1(g, u):
            b = u % 2
            pool_ln(g, u + 1)
            if u == 8:
                pool_ln2(g, u + 1)
            for t in range(TT):
                g.wait_ge(sem("l_ss"), TT * b + t + 1)
                pool_rsqrt(g, lin_rn[:, t:t + 1], lin_ss[:, t:t + 1], 1, "l_rn")
            for i in range(TT):
                xt = x[:, TT * b + i, :]
                g.tensor_tensor(xt, xt, xn[:, b, i, :], ALU.add).then_inc(sem("l_xa"), 1)
            for i in range(TT):
                g.wait_ge(sem("l_xa"), TT * b + i + 1)
                xt = x[:, TT * b + i, :]
                g.tensor_tensor(xt, xt, lin_bout[:, :], ALU.add).then_inc(sem("l_xb"), 1)

        def dve_lin1(v, u):
            b = u % 2
            dve_ln(v, u + 1)
            v.wait_ge(sem("lin_in"), 48)
            for t in range(TT):
                v.wait_ge(sem("l_kvmm"), TT * b + t + 1)
                v.tensor_tensor(lin_kv[:, t, :], ps[:, 2 + t, :], lin_bkv[:, :], ALU.add).then_inc(sem("l_kv"), 1)
            for t in range(TT):
                v.wait_ge(sem("l_kv"), TT * b + t + 1)
                n = 4 * (TT * b + t)
                kk = lin_kv[:, t, 0:P].rearrange("p (n k) -> p n k", k=2)
                ks = lin_ks[:, t, :].rearrange("p (n k) -> p n k", k=2)
                sn = lin_tok[:, 1, t, :].rearrange("p (n k) -> p n k", k=2)
                v.tensor_tensor(lin_kr[:, t, :], lin_kv[:, t, 0:P], lin_tok[:, 0, t, :], ALU.mult).then_inc(sem("l_rope"), 1)
                v.tensor_tensor(ks[:, :, 0], kk[:, :, 1], sn[:, :, 0], ALU.mult).then_inc(sem("l_rope"), 1)
                v.tensor_tensor(ks[:, :, 1], kk[:, :, 0], sn[:, :, 1], ALU.mult).then_inc(sem("l_rope"), 1)
                v.wait_ge(sem("l_rope"), n + 3)
                v.tensor_tensor(lin_kv[:, t, 0:P], lin_kr[:, t, :], lin_ks[:, t, :], ALU.add).then_inc(sem("l_rope"), 1)
            if u == 8:
                dve_norm2(v, u + 1)
            for t in range(TT):
                v.wait_ge(sem("l_rn"), TT * b + t + 1)
                v.scalar_tensor_tensor(out=lin_xn[:, b, t, :], in0=lin_kv[:, t, 0:D], scalar=lin_rn[:, t:t + 1],
                                       in1=lin_kv[:, t, D:2 * D], op0=ALU.mult, op1=ALU.mult).then_inc(sem("l_prod"), 1)
            v.wait_ge(sem("l_qmm"), 3 * b + 1)
            v.scalar_tensor_tensor(out=lin_qa[:, :], in0=ps[:, 2, :], scalar=lin_cols[:, 4:5], in1=lin_feat[:, 0, :],
                                   op0=ALU.add, op1=ALU.mult).then_inc(sem("l_qf"), 1)
            v.wait_ge(sem("l_qmm"), 3 * b + 2)
            v.scalar_tensor_tensor(out=lin_qb[:, :], in0=ps[:, 3, :], scalar=lin_cols[:, 5:6], in1=lin_feat[:, 1, :],
                                   op0=ALU.add, op1=ALU.mult).then_inc(sem("l_qb"), 1)
            v.wait_ge(sem("l_qf"), 4 * b + 1)
            v.wait_ge(sem("l_qb"), b + 1)
            v.tensor_tensor(lin_qa[:, :], lin_qa[:, :], lin_qb[:, :], ALU.add).then_inc(sem("l_qf"), 1)
            v.wait_ge(sem("l_sum"), b + 1)
            v.tensor_copy(lin_a, ps[:, 6, 0:DC]).then_inc(sem("l_a"), 1)
            v.wait_ge(sem("l_a"), b + 1)
            v.wait_ge(sem("l_qf"), 4 * b + 2)
            v.tensor_scalar(lin_qf[:, 0, :], lin_qa[:, :], lin_a[:, 0:1], None, ALU.mult).then_inc(sem("l_qf"), 1)
            v.wait_ge(sem("l_qmm"), 3 * b + 3)
            v.tensor_scalar(lin_qf[:, 1, :], ps[:, 4, :], lin_cols[:, 6:7], lin_a[:, 1:2], ALU.add, ALU.mult)\
                .then_inc(sem("l_qf"), 1)
            for c in range(DC):
                v.wait_ge(sem("l_qhi"), DC * b + c + 1)
                v.tensor_tensor(lin_ql[:, c, :], lin_qf[:, c, :], f32(lin_qh[:, c, :]), ALU.subtract)\
                    .then_inc(sem("l_qlo"), 1)
            dve_T(v, u + 1)
            v.wait_ge(sem("l_xb"), TT * (b + 1))
            dve_residual(v, u, 1.0, [("l_out", 2 * b + 1), ("l_out", 2 * b + 2)])

        A2_HEADS = {14: 0, 15: H}
        A3_HEADS = {20: 2 * H, 21: 3 * H}
        A2_FILL = {14: 0, 15: 4 + 3 * H}
        A3_FILL = {20: 2 * (4 + 3 * H), 21: 2 * (4 + 3 * H) + 7 * H}

        def pe_scores(pe, n, q, k):
            for i in range(TT):
                if positive(n * TT - TT + max(i, 1) + 1):
                    pe.wait_ge(sem("at_exp"), n * TT - TT + max(i, 1) + 1)
                bank, at = S_AT[i]
                o = ps[:, bank, at:at + S_COLS[i]]
                if isinstance(q(i), tuple):
                    mm3(pe, o, q(i), k(S_COLS[i]), True, False)
                else:
                    pe.matmul(o, q(i), k(S_COLS[i]), start=True, stop=False, skip_group_check=True)
                pe.matmul(ps[:, bank, at + i * P:at + (i + 1) * P], identb[:, :], maskb[:, :], start=False, stop=True,
                          skip_group_check=True).then_inc(sem("at_s"), 1)

        def dve_max(v, n, par, scale, groups=((0, 1), (2,), (3,))):
            for tiles in groups:
                v.wait_ge(sem("at_s"), tiles[-1] + 1 + n * TT)
                for i in tiles:
                    bank, at = S_AT[i]
                    v.tensor_reduce(h_max[:, par, i:i + 1], ps[:, bank, at:at + KEYS[i]], AX_X, ALU.max)\
                        .then_inc(sem("at_mx"), 1)
                v.wait_ge(sem("at_mx"), tiles[-1] + 1 + n * TT)
                sl = slice(tiles[0], tiles[-1] + 1)
                v.tensor_scalar(h_nmx[:, par, sl], h_max[:, par, sl], -scale, None, ALU.mult)\
                    .then_inc(sem("at_nmx"), len(tiles))

        def act_exp(s, n, par, scale, p, tiles=range(TT)):
            for i in tiles:
                bank, at = S_AT[i]
                s.wait_ge(sem("at_nmx"), max(i, 1) + 1 + n * TT)
                s.activation(p[:, par, P_AT[i]:P_AT[i + 1]], ps[:, bank, at:at + KEYS[i]], ACT.Exp,
                             bias=h_nmx[:, par, i:i + 1], scale=scale, accum_out=h_sum[:, par, i:i + 1])\
                    .then_inc(sem("at_exp"), 1)

        def dve_rinv(v, n, par, parts=(0, 1)):
            for part in parts:
                sl = slice(0, TT - 1) if part == 0 else slice(TT - 1, TT)
                v.wait_ge(sem("at_exp"), TT - 1 + part + n * TT)
                v.reciprocal(h_inv[:, par, sl], h_sum[:, par, sl]).then_inc(sem("at_rinv"), 1)

        def pool_norm(g, n, par, p):
            for i in range(TT):
                if i in (0, TT - 1):
                    g.wait_ge(sem("at_rinv"), (1 if i == 0 else 2) + n * 2)
                    if not isinstance(n, int):
                        g.sem_inc(sem("pool_turn"), 1)
                pp = p[:, par, P_AT[i]:P_AT[i + 1]]
                g.tensor_scalar(pp, pp, h_inv[:, par, i:i + 1], 1.0, ALU.mult, ALU.mult).then_inc(sem("at_norm"), 1)

        def pe_fill_start(pe, earlier):
            pe.wait_ge(sem("at_flo"), earlier)

        def pe_transpose_p(pe, n, par, p, banks, earlier):
            pe.wait_ge(sem("at_norm"), TT + n * TT)
            for f, blocks in enumerate(FILLS):
                pe_fill_start(pe, earlier[f])
                for kb in blocks:
                    for i in range(kb, TT):
                        at = PT_AT[kb] - PT_AT[blocks[0]] + (i - kb) * P
                        last = pe.transpose(ps[:, banks[f], at:at + P], p[:, par, P_AT[i] + kb * P:P_AT[i] + (kb + 1) * P],
                                            ident[:, :])
                last.then_inc(sem("at_fill"), 1)

        def pe_pv(pe, o, fill, v, pth, ptl, start, stop):
            for kb in range(TT):
                if kb < len(FILLS):
                    pe.wait_ge(sem("at_flo"), fill + kb + 1)
                r = slice(PT_AT[kb], PT_AT[kb + 1])
                last = mm3(pe, o[:, kb * P:T], v(kb), (pth[:, r], ptl[:, r]), start and kb == 0, stop and kb == TT - 1)
            return last

        def act_fill(s, fill, bank, dst, cols=T, **how):
            s.wait_ge(sem("at_fill"), fill + 1)
            func = ACT.Identity if how else ACT.Copy
            s.activation(dst, ps[:, bank, 0:cols], func, **how).then_inc(sem("at_fhi"), 1)

        def dve_fill(v, fill, bank, dst, hi, cols=T, bias=None):
            v.wait_ge(sem("at_fhi"), fill + 1)
            if bias is None:
                ins = v.tensor_tensor(dst, ps[:, bank, 0:cols], f32(hi), ALU.subtract)
            else:
                ins = v.scalar_tensor_tensor(out=dst, in0=ps[:, bank, 0:cols], scalar=bias, in1=f32(hi),
                                             op0=ALU.add, op1=ALU.subtract)
            ins.then_inc(sem("at_flo"), 1)

        def pt_cols(f):
            return PT_AT[FILLS[f][0]], PT_AT[FILLS[f][-1] + 1]

        def a2_v(g, kb, j):
            lo = slice(j * P, j * P + P)
            if g == 0:
                return (drh[:, kb * 8 * VS:(kb + 1) * 8 * VS][:, lo], drl[:, kb * 8 * VS:(kb + 1) * 8 * VS][:, lo])
            return (a2_vh[:, kb, :, :].rearrange("p h n -> p (h n)")[:, lo],
                    a2_vl[:, kb, :, :].rearrange("p h n -> p (h n)")[:, lo])

        def a2_vslot(g, hi, kb):
            t = (drh if hi else drl)[:, kb * 8 * VS:(kb + 1) * 8 * VS] if g == 0 else \
                (a2_vh if hi else a2_vl)[:, kb, :, :].rearrange("p h n -> p (h n)")
            return t.rearrange("p (h n) -> p h n", h=8)[:, :, 0:HD2]

        def pe_att2(pe, u):
            b, n0, f0 = u % 2, A2_HEADS[u], A2_FILL[u]
            pe.wait_ge(sem("w_split"), RAW0["att2"] + 2)
            pe_ready(pe, u)
            for f in range(4):
                if f == 3:
                    pe_fill_start(pe, f0 + 1)
                at = (f // 2) * 512 + (f % 2) * P
                mm3c(pe, ps[:, f % 3, :], [rc(at + c * D, P) for c in range(DC)], [xT(b, c) for c in range(DC)])\
                    .then_inc(sem("at_fill"), 1)
            pe.wait_ge(sem("x_res"), 4 * u)
            for t in range(TT):
                last = mm3c(pe, acc(t), [xTt(b, c, t) for c in range(DC)], [rc(1024 + c * D, D) for c in range(DC)])
                if t % 2:
                    last.then_inc(sem("a2_v"), 1)

            def scores(h):
                pe.wait_ge(sem(f"a2_stack{h % 2}"), 16 * 6 * ((n0 + h) // 2 + 1))
                pe_scores(pe, n0 + h,
                          lambda i: a2_sq[:, h % 2, i * P:(i + 1) * P], lambda n: a2_sk[:, h % 2, 0:n])

            pe.wait_ge(sem("at_flo"), f0 + 4)
            scores(0)
            pe.wait_ge(sem("a2_vlo"), 4 * (b + 1))
            def context(h):
                pe_pv(pe, ps[:, 6 + h // 8, :], f0 + 4 + 3 * h, lambda kb: a2_v(h // 8, kb, h % 8), a2_pth, a2_ptl,
                      h % 8 == 0, h % 8 == 7).then_inc(sem("a2_pv"), 1)

            for h in range(H):
                f = f0 + 4 + 3 * h
                if h + 1 < H:
                    scores(h + 1)
                if h > 0:
                    context(h - 1)
                pe_transpose_p(pe, n0 + h, h % 2, a2_p, [0, 1, 2], [f - 2, f - 1, f] if h else [f0 + 4, f0 + 2, f0 + 3])
            context(H - 1)
            pe.wait_ge(sem("at_flo"), f0 + 4 + 3 * H)
            pe_T(pe, u + 1)
            pe.wait_ge(sem("a2_zlo"), 2 * (b + 1))
            for t in range(TT):
                last = mm3c(pe, acc(t), [xTt(b, c, t) for c in range(DC)], [rc(1536 + c * D, D) for c in range(DC)])
                if t % 2:
                    last.then_inc(sem("a2_out"), 1)

        def act_att2(s, u):
            b, n0, f0 = u % 2, A2_HEADS[u], A2_FILL[u]
            s.wait_ge(sem("const_in"), 16 * CONSTS)
            for f in range(4):
                dst = (a2_qh if f < 2 else a2_kh)[:, f % 2, :]
                act_fill(s, f0 + f, f % 3, dst, bias=att_cols[:, f:f + 1], scale=1.0)
            s.wait_ge(sem("a2_vzero"), 6)
            for t in range(TT):
                s.wait_ge(sem("a2_vf"), 4 * b + t + 1)
                for g in range(2):
                    s.activation(a2_vslot(g, True, t), a2_vf[:, t, g * P:(g + 1) * P].rearrange("p (h n) -> p h n", h=8),
                                 ACT.Copy).then_inc(sem("a2_vhi"), 1)
            act_exp(s, n0, 0, SCALE2, a2_p)
            for h in range(H):
                if h + 1 < H:
                    act_exp(s, n0 + h + 1, (h + 1) % 2, SCALE2, a2_p, (0, 1))
                if h == 8:
                    act_z(s, b, 0)
                for f in range(3):
                    if f > 0 and h + 1 < H:
                        act_exp(s, n0 + h + 1, (h + 1) % 2, SCALE2, a2_p, (f + 1,))
                    lo, hi = pt_cols(f)
                    act_fill(s, f0 + 4 + 3 * h + f, f, a2_pth[:, lo:hi], hi - lo)
            act_z(s, b, 1)
            act_T(s, u + 1)

        def act_z(s, b, g):
            s.wait_ge(sem("a2_pv"), H * b + 8 * (g + 1))
            s.activation(xh[:, b, g, :], ps[:, 6 + g, :], ACT.Copy).then_inc(sem("a2_zhi"), 1)

        def dve_z(v, b, g):
            v.wait_ge(sem("a2_zhi"), 2 * b + g + 1)
            v.tensor_tensor(xl[:, b, g, :], ps[:, 6 + g, :], f32(xh[:, b, g, :]), ALU.subtract).then_inc(sem("a2_zlo"), 1)

        def dve_att2(v, u):
            b, n0, f0 = u % 2, A2_HEADS[u], A2_FILL[u]
            v.wait_ge(sem("const_in"), 16 * CONSTS)
            for f in range(4):
                dst, hi = (a2_ql, a2_qh) if f < 2 else (a2_kl, a2_kh)
                dve_fill(v, f0 + f, f % 3, dst[:, f % 2, :], hi[:, f % 2, :], bias=att_cols[:, f:f + 1])
            v.wait_ge(sem("a2_bv_in"), 16)
            for t in range(TT):
                v.wait_ge(sem("a2_v"), 2 * b + t // 2 + 1)
                v.tensor_tensor(a2_vf[:, t, :], acc(t), a2_bv[:, :], ALU.add).then_inc(sem("a2_vf"), 1)
            dve_max(v, n0, 0, SCALE2)
            v.wait_ge(sem("a2_vzero"), 6)
            for t in range(TT):
                for g in range(2):
                    v.wait_ge(sem("a2_vhi"), 8 * b + 2 * t + g + 1)
                    ins = v.tensor_tensor(a2_vslot(g, False, t),
                                          a2_vf[:, t, g * P:(g + 1) * P].rearrange("p (h n) -> p h n", h=8),
                                          f32(a2_vslot(g, True, t)), ALU.subtract)
                    if g == 1:
                        ins.then_inc(sem("a2_vlo"), 1)
            dve_rinv(v, n0, 0)
            for h in range(H):
                if h == 1:
                    dve_stats(v, u + 1)
                if h == 3:
                    dve_norm(v, u + 1)
                if h + 1 < H:
                    dve_max(v, n0 + h + 1, (h + 1) % 2, SCALE2, ((0, 1), (2,), (3,)) if h == 0 else ((2,), (3,)))
                if h == 8:
                    dve_z(v, b, 0)
                for f in range(3):
                    if f > 0 and h + 1 < H:
                        if f == 2 and h + 2 < H:
                            dve_max(v, n0 + h + 2, h % 2, SCALE2, ((0, 1),))
                        dve_rinv(v, n0 + h + 1, (h + 1) % 2, (f - 1,))
                    lo, hi = pt_cols(f)
                    dve_fill(v, f0 + 4 + 3 * h + f, f, a2_ptl[:, lo:hi], a2_pth[:, lo:hi], hi - lo)
            dve_z(v, b, 1)
            dve_T(v, u + 1)
            v.wait_ge(sem("const_in"), 16 * CONSTS)
            for t in range(TT):
                xt = x[:, TT * b + t, :]
                v.tensor_tensor(xt, xt, att_bo[:, :], ALU.add).then_inc(sem("a2_xb"), 1)
            v.wait_ge(sem("a2_xb"), TT * (b + 1))
            dve_residual(v, u, 1.0, [("a2_out", 2 * b + 1), ("a2_out", 2 * b + 2)])

        def pool_zero_a2(g, t, units):
            g.wait_ge(sem("x_res"), 4 * units)
            g.memset(f32(t), 0.0).then_inc(sem("a2_vzero"), 1)

        def pool_att2(g, u):
            b, n0, f0 = u % 2, A2_HEADS[u], A2_FILL[u]

            for h in range(H):
                pool_norm(g, n0 + h, h % 2, a2_p)
                if h == 1:
                    pool_ln(g, u + 1)

        def sp_att2(sp, u):
            n0, f0 = A2_HEADS[u], A2_FILL[u]
            for h in range(H):
                if h == 0:
                    sp.wait_ge(sem("a2_szero"), 2)
                    sp.wait_ge(sem("at_flo"), f0 + 4)
                if n0 + h >= 2:
                    sp.wait_ge(sem("at_s"), TT * (n0 + h - 1))
                rows = slice((h % 8) * HD2, (h % 8 + 1) * HD2)
                for dst, parts in ((a2_sq, (a2_qh, a2_qh, a2_ql)), (a2_sk, (a2_kh, a2_kl, a2_kh))):
                    for k, src in enumerate(parts):
                        sp.dma_start(f32(dst[k * HD2:(k + 1) * HD2, h % 2, :]), f32(src[rows, h // 8, :]))\
                            .then_inc(sem(f"a2_stack{h % 2}"), 16)

        V_FILLS, BODY = 2, 14

        def pair_fills(last):
            names = [("v", 0, 0), ("v", 0, 1)]
            for hh in range(2):
                if not (last and hh == 1):
                    names += [("q", hh, 0), ("k", hh, 0)]
                names += [("p", hh, f) for f in range(3)] + [("z", hh, 0)]
            banks = [1, 2, 0, 1, 2, 0, 1, 2] + ([0, 1, 0, 2] if last else [0, 1, 0, 1, 2, 0])
            seen = {2: -2, 0: -1, 1: -3}
            out_ = {}
            for place, (name, bank) in enumerate(zip(names, banks)):
                out_[name] = (place, bank, seen[bank])
                seen[bank] = place
            return out_

        def pe_att3(pe, u):
            b, n0, f0, r0 = u % 2, A3_HEADS[u], A3_FILL[u], RAW0[u]

            def fill(base, place, bank, earlier):
                pe_fill_start(pe, base + earlier + 1)

            def qk(hh, banks, starts):
                for k in range(2):
                    pe_fill_start(pe, starts[k])
                    at = k * 2 * D + hh * P
                    mm3c(pe, ps[:, banks[k], :], [w(0, at + c * 2 * P) for c in range(DC)],
                         [xT(b, c) for c in range(DC)]).then_inc(sem("at_fill"), 1)

            def scores(n, fill_done):
                pe.wait_ge(sem("at_flo"), fill_done)
                pe_scores(pe, n, lambda i: (a3_qh[:, i * P:(i + 1) * P], a3_ql[:, i * P:(i + 1) * P]),
                          lambda k: (a3_kh[:, 0:k], a3_kl[:, 0:k]))

            def out_head(h, done, start=False, final=False):
                pe.wait_ge(sem("at_flo"), done)
                r = drh[:, bass.ds(h * D, D)], drl[:, bass.ds(h * D, D)]
                for t in range(TT):
                    last = mm3(pe, acc(t), (a3_zh[:, t * P:(t + 1) * P], a3_zl[:, t * P:(t + 1) * P]), r,
                               start and t % 2 == 0, final)
                    if final and t % 2:
                        last.then_inc(sem("a3_out"), 1)

            def pair(r, first=False, last=False):
                fills = pair_fills(last)
                base = f0 + 2 + r * BODY
                n = r * 2 + n0
                at = {k: base + v[0] for k, v in fills.items()}
                starts = {k: base + v[2] + 1 for k, v in fills.items()}
                bank = {k: v[1] for k, v in fills.items()}
                pe.wait_ge(sem("w_split"), r0 + 2 + r * 2)
                for f in range(2):
                    pe_fill_start(pe, starts["v", 0, f])
                    for t in (2 * f, 2 * f + 1):
                        m = mm3c(pe, ps[:, bank["v", 0, f], (t % 2) * D:(t % 2 + 1) * D], [xTt(b, c, t) for c in range(DC)],
                                 [w(1, c * 2 * P, 2 * P) for c in range(DC)])
                    m.then_inc(sem("at_fill"), 1)
                for hh in range(2):
                    done = last and hh == 1
                    if not done:
                        if hh == 1:
                            pe.wait_ge(sem("w_split"), r0 + 3 + r * 2)
                        qk(1 - hh, [bank["q", hh, 0], bank["k", hh, 0]], [starts["q", hh, 0], starts["k", hh, 0]])
                    if first and hh == 0:
                        pe.wait_ge(sem("x_res"), 4 * u)
                    else:
                        out_head(r * 2 + (hh - 1), (base if hh == 0 else at["z", 0, 0] + 1), start=first)
                    pe_transpose_p(pe, n + hh, hh, a3_p, [bank["p", hh, f] for f in range(3)],
                                   [starts["p", hh, f] for f in range(3)])
                    if not done:
                        scores(n + (hh + 1), at["k", hh, 0] + 1)
                    pe_fill_start(pe, starts["z", hh, 0])
                    pe_pv(pe, ps[:, bank["z", hh, 0], :], at["p", hh, 0],
                          lambda kb: (a3_vh[:, kb, hh * P:(hh + 1) * P], a3_vl[:, kb, hh * P:(hh + 1) * P]),
                          a3_pth, a3_ptl, True, True).then_inc(sem("at_fill"), 1)
                return at

            pe_ready(pe, u)
            pe.wait_ge(sem("w_split"), r0 + 1)
            pe.wait_ge(sem("w_split"), RAW0["wo3"] + 4)
            qk(0, [2, 0], [f0 - 1, f0])
            scores(n0, f0 + 2)
            pair(0, first=True)
            with pe.Fori(1, H // 2 - 1) as r:
                pair(r)
            at = pair(H // 2 - 1, last=True)
            pe.wait_ge(sem("at_flo"), f0 + 7 * H - 1)
            pe_T(pe, u + 1)
            out_head(H - 1, at["z", 1, 0] + 1, final=True)


        def act_att3(s, u):
            b, n0, f0 = u % 2, A3_HEADS[u], A3_FILL[u]

            def pair(r, last=False):
                fills = pair_fills(last)
                base, n = f0 + 2 + r * BODY, r * 2 + n0

                def one(key, dst, cols=T):
                    act_fill(s, base + fills[key][0], fills[key][1], dst, cols)

                for f in range(2):
                    one(("v", 0, f), a3_vh[:, 2 * f:2 * f + 2, :].rearrange("p t n -> p (t n)"))
                for hh in range(2):
                    done = last and hh == 1
                    if not done:
                        one(("q", hh, 0), a3_qh[:, :])
                        one(("k", hh, 0), a3_kh[:, :])
                    for f in range(3):
                        lo, hi = pt_cols(f)
                        one(("p", hh, f), a3_pth[:, lo:hi], hi - lo)
                    if not done:
                        act_exp(s, n + (hh + 1), 1 - hh, SCALE3, a3_p)
                    one(("z", hh, 0), a3_zh[:, :])

            act_fill(s, f0, 2, a3_qh[:, :])
            act_fill(s, f0 + 1, 0, a3_kh[:, :])
            act_exp(s, n0, 0, SCALE3, a3_p)
            pair(0)
            with s.Fori(1, H // 2 - 1) as r:
                pair(r)
            pair(H // 2 - 1, last=True)
            act_T(s, u + 1)

        def dve_att3(v, u):
            b, n0, f0 = u % 2, A3_HEADS[u], A3_FILL[u]

            def pair(r, last=False, first=False):
                fills = pair_fills(last)
                base, n = f0 + 2 + r * BODY, r * 2 + n0

                def one(key, dst, src, cols=T):
                    dve_fill(v, base + fills[key][0], fills[key][1], dst, src, cols)

                for f in range(2):
                    one(("v", 0, f), a3_vl[:, 2 * f:2 * f + 2, :].rearrange("p t n -> p (t n)"),
                        a3_vh[:, 2 * f:2 * f + 2, :].rearrange("p t n -> p (t n)"))
                for hh in range(2):
                    done = last and hh == 1
                    if not done:
                        one(("q", hh, 0), a3_ql[:, :], a3_qh[:, :])
                        one(("k", hh, 0), a3_kl[:, :], a3_kh[:, :])
                    for f in range(3):
                        lo, hi = pt_cols(f)
                        one(("p", hh, f), a3_ptl[:, lo:hi], a3_pth[:, lo:hi], hi - lo)
                    if not done:
                        dve_max(v, n + (hh + 1), 1 - hh, SCALE3)
                        dve_rinv(v, n + (hh + 1), 1 - hh)
                    one(("z", hh, 0), a3_zl[:, :], a3_zh[:, :])
                    if first and hh == 0:
                        dve_stats(v, u + 1)

            dve_fill(v, f0, 2, a3_ql[:, :], a3_qh[:, :])
            dve_fill(v, f0 + 1, 0, a3_kl[:, :], a3_kh[:, :])
            dve_max(v, n0, 0, SCALE3)
            dve_rinv(v, n0, 0)
            pair(0, first=True)
            with v.Fori(1, H // 2 - 1) as r:
                pair(r)
            dve_norm(v, u + 1)
            pair(H // 2 - 1, last=True)
            dve_T(v, u + 1)
            dve_residual(v, u, 1.0, [("a3_out", 2 * b + 1), ("a3_out", 2 * b + 2)])

        def pool_att3(g, u):
            n0 = A3_HEADS[u]

            def pair(r, last=False, first=False):
                for hh in range(2):
                    pool_norm(g, r * 2 + (n0 + hh), hh, a3_p)
                    if not last:
                        pool_chunks(g, u, r + 1, hh)
                if first:
                    pool_ln(g, u + 1)

            pair(0, first=True)
            with g.Fori(1, H // 2 - 1) as r:
                pair(r)
            pair(H // 2 - 1, last=True)



        SPARE = D * D
        NK = NS // P
        table = nc.dram_tensor("delta_table", [SPARE + NS, E], F32, kind="Internal").ap()
        d_sm = d_small[0:E, 0:NA]
        d_smT = d_small[0:NA, 64:72]
        d_max, d_sum, d_ri = d_small[0:E, 72:73], d_small[0:E, 73:74], d_small[0:E, 74:75]
        d_ew = d_small[0:E, 80:144]
        d_colf = d_small[:, 144:160]
        d_dest = d_small[:, 160:176]
        d_pos = d_small[:, 176:192]
        d_dup = d_small[:, 192:208]
        d_thr = d_small[:, 208:216]
        d_later = d_small[:, 216:232]
        d_sg, d_wt, d_r1, d_r2, d_cmb = [d_work[:, k, :] for k in range(5)]
        d_junk = d_rowi[:, :].bitcast(F32)

        DELTA_UNITS = (0, 1, 4)
        EQ_SLOTS = [[0], [1, 2], [3, 4], [5, 6], [7, 8, 9], [10, 11, 12], [13, 14, 15]]

        def sp_delta(sp):
            sp.dma_start(d_ew, a["expert_atoms"]).then_inc(sem("d_in"), 16)
            sp.dma_start(d_imp[:, :], a["importance"]).then_inc(sem("d_in"), 16)
            sp.dma_start(d_col[:, 0, :], a["idx_col"]).then_inc(sem("d_in"), 16)
            sp.dma_start(d_pos, a["pos"]).then_inc(sem("d_in"), 16)
            sp.dma_start(d_atoms[:, :], a["atoms"]).then_inc(sem("d_in"), 16)
            sp.dma_start(d_rowi[:, :], a["idx_row"].to_broadcast([P, NS])).then_inc(sem("d_in"), 16)

        def sp_zero(sp):
            sp.wait_ge(sem("const_set"), 3)
            flat = table.rearrange("(p r) e -> p (r e)", p=P)
            for k in range(4):
                sp.dma_start(flat[:, k * 1056:(k + 1) * 1056], d_zero).then_inc(sem("d_zeroed"), 16)
            sp.dma_start(d_q3[:, :, :], a["weight3"]).then_inc(sem("d_in_q3"), 16)

        def pool_scatter(g, ks):
            g.wait_ge(sem("d_dest"), 1)
            g.wait_ge(sem("d_cmb"), 3)
            g.wait_ge(sem("d_zeroed"), 64)
            for k in ks:
                g.indirect_dma_start(out=table[:, :], out_offset=bass.IndirectOffsetOnAxis(ap=d_desti[:, k:k + 1], axis=0),
                                     in_=d_cmb[:, k * E:(k + 1) * E], in_offset=None).then_inc(sem("d_scattered"), 16)

        def act_delta(s, u, j):
            if u == 0 and j == 3:
                act_softplus(s)
                s.wait_ge(sem("d_max"), 1)
                s.activation(d_sm, d_ew, ACT.Exp, bias=d_max, accum_out=d_sum).then_inc(sem("d_exp"), 1)
                s.activation(d_sg, d_imp[:, :], ACT.Exp, scale=-1.0).then_inc(sem("d_exp"), 1)
            if u == 1 and 1 <= j <= len(EQ_SLOTS):
                for k in EQ_SLOTS[j - 1]:
                    s.wait_ge(sem("d_eqtri"), k + 1)
                    if k >= 1:
                        s.wait_ge(sem("d_rows"), k)
                    s.activation(d_junk[:, 0:NS - k * P], d_eq[:, k % 3, k * P:NS], ACT.Copy,
                                 accum_out=d_later[:, k:k + 1]).then_inc(sem("d_rows"), 1)
            if u == 4 and j < 4:
                s.wait_ge(sem(f"d_back{j // 2}"), 16)
                src, hi, _ = delta_quarter(j)
                s.activation(hi, src, ACT.Copy).then_inc(sem("delta_hi"), 1)

        def act_table(s):
            s.wait_ge(sem("d_scattered"), 16 * NK)
            for c in range(DC):
                s.dma_start(d_back[:, c, :], table[c * P * D:(c + 1) * P * D, :].rearrange("(p r) e -> p (r e)", p=P))\
                    .then_inc(sem(f"d_back{c}"), 16)

        def delta_quarter(q):
            c, h = q // 2, q % 2
            src = d_back[:, c, :].rearrange("p (r e) -> p e r", e=E)[:, 4 * h:4 * h + 4, :]
            at = (c * E + 4 * h) * D
            return src, drh[:, at:at + 4 * D].rearrange("p (e r) -> p e r", e=4), \
                drl[:, at:at + 4 * D].rearrange("p (e r) -> p e r", e=4)

        def pe_delta(pe, u, j):
            if u == 0 and j == 4:
                pe.wait_ge(sem("d_sm"), 1)
                pe.transpose(ps[0:NA, 1, 0:E], d_sm, ident[0:E, 0:E]).then_inc(sem("d_smt"), 1)
            if u == 0 and j == 5:
                pe.wait_ge(sem("d_smtc"), 1)
                for k in range(NK):
                    last = pe.matmul(ps[:, 1, k * E:(k + 1) * E], d_atoms[:, k * P:(k + 1) * P], d_smT, start=True,
                                     stop=True)
                last.then_inc(sem("d_delta"), 1)
            if u == 1 and 1 <= j <= len(EQ_SLOTS):
                o = ps[:, 0, 0:NK * 25].rearrange("p (m n) -> p m n", m=NK)
                for k in EQ_SLOTS[j - 1]:
                    pe.wait_ge(sem("d_eqtri"), k + 1)
                    for m in range(k, NK):
                        pe.matmul(o[:, m, 0:24], d_eq[:, k % 3, m * P:(m + 1) * P], d_wb[:, k, 0:24],
                                  start=(k == 0 and m == 0), stop=False, skip_group_check=True)
                    pe.matmul(o[:, k, 24:25], d_tri[:, 1 + k % 2, :], d_wb[:, k, 24:25], start=False, stop=(k == NK - 1),
                              skip_group_check=True).then_inc(sem("d_comb"), 1)
            if u == 4 and j == 5:
                pe.wait_ge(sem("q_tern"), 1)
                for c in range(DC):
                    for oc in range(DC):
                        last = pe.transpose(ps[:, 1, c * D + oc * P:c * D + (oc + 1) * P],
                                            d_q3t[:, oc, c * P:(c + 1) * P], ident[:, :])
                last.then_inc(sem("q_T"), 1)

        def pe_delta_end(pe, u):
            if u == 0:
                pe.wait_ge(sem("d_wb"), 4)
            elif u == 1:
                pe.wait_ge(sem("d_dest"), 1)
            else:
                pe.wait_ge(sem("q3_ready"), 2)

        d_steps = [0]

        def dve_delta(v, u, j):
            def then(ins):
                ins.then_inc(sem("d_step"), 1)
                d_steps[0] += 1

            def settled():
                v.wait_ge(sem("d_step"), d_steps[0])

            if u == 0 and j == 1:
                v.wait_ge(sem("d_in"), 16 * 6)
                v.tensor_reduce(d_ri, d_ew, AX_X, ALU.max).then_inc(sem("d_mx0"), 1)
                v.wait_ge(sem("d_mx0"), 1)
                v.tensor_scalar(d_max, d_ri, -1.0, None, ALU.mult).then_inc(sem("d_max"), 1)
                v.wait_ge(sem("const_in"), 16 * CONSTS)
                then(v.tensor_copy(d_tri[:, 0, :], tri[:, :]))
                then(v.tensor_copy(d_row[:, :], d_rowi[:, :]))
                then(v.tensor_copy(d_colf, d_col[:, 0, :]))
                then(v.tensor_scalar(d_col[:, 1, :], d_col[:, 0, :], D - 1, 8, ALU.bitwise_and, ALU.logical_shift_left))
                then(v.tensor_scalar(d_col[:, 2, :], d_col[:, 0, :], 8, None, ALU.logical_shift_right))
            if u == 0 and j == 2:
                dve_softplus(v)
            if u == 0 and j == 5:
                dve_consts(v)
            if u == 0 and j == 3:
                v.wait_ge(sem("d_exp"), 1)
                then(v.reciprocal(d_ri, d_sum))
                settled()
                then(v.tensor_tensor(d_col[:, 3, :], d_col[:, 1, :], d_col[:, 2, :], ALU.bitwise_or))
                v.tensor_scalar(d_sm, d_sm, d_ri, None, ALU.mult).then_inc(sem("d_sm"), 1)
                v.wait_ge(sem("d_exp"), 2)
                then(v.tensor_scalar(d_sg, d_sg, 1.0, None, ALU.add))
                settled()
                then(v.reciprocal(d_sg, d_sg))
                then(v.tensor_copy(d_dest, d_col[:, 3, :]))
            if u == 0 and j == 4:
                v.wait_ge(sem("d_smt"), 1)
                v.tensor_copy(d_smT, ps[0:NA, 1, 0:E]).then_inc(sem("d_smtc"), 1)
            if u == 0 and j == 6:
                v.wait_ge(sem("d_delta"), 1)
                settled()
                then(v.tensor_tensor(d_wt, ps[:, 1, 0:P], d_sg, ALU.mult))
                settled()
                wk = d_wt.rearrange("p (k e) -> p k e", e=E)
                v.memset(d_wb[:, :, 24:25], 1.0).then_inc(sem("d_wb"), 1)
                v.tensor_copy(d_wb[:, :, 0:8], wk).then_inc(sem("d_wb"), 1)
                v.wait_ge(sem("d_wb"), 2)
                then(v.tensor_tensor(d_r1.rearrange("p (k e) -> p k e", e=E), wk, d_wb[:, :, 0:8], ALU.subtract))
                settled()
                r1, r2 = [x_.rearrange("p (k e) -> p k e", e=E) for x_ in (d_r1, d_r2)]
                v.tensor_copy(d_wb[:, :, 8:16], r1).then_inc(sem("d_wb"), 1)
                v.wait_ge(sem("d_wb"), 3)
                then(v.tensor_tensor(r2, r1, d_wb[:, :, 8:16], ALU.subtract))
                settled()
                v.tensor_copy(d_wb[:, :, 16:24], r2).then_inc(sem("d_wb"), 1)
            if u == 1 and j < len(EQ_SLOTS):
                for k in EQ_SLOTS[j]:
                    if k >= 3:
                        v.wait_ge(sem("d_comb"), k - 2)
                        v.wait_ge(sem("d_rows"), k - 2)
                    then(v.tensor_scalar(d_eq[:, k % 3, k * P:NS], d_row[:, k * P:NS], d_colf[:, k:k + 1], None,
                                         ALU.is_equal))
                    settled()
                    if k >= 2:
                        v.wait_ge(sem("d_comb"), k - 1)
                    v.tensor_tensor(d_tri[:, 1 + k % 2, :], d_eq[:, k % 3, k * P:(k + 1) * P], d_tri[:, 0, :], ALU.mult)\
                        .then_inc(sem("d_eqtri"), 1)
            if u == 1 and j == 7:
                v.wait_ge(sem("d_comb"), NK)
                o = ps[:, 0, 0:NK * 25].rearrange("p (m n) -> p m n", m=NK)
                cmb = d_cmb.rearrange("p (k e) -> p k e", e=E)
                v.tensor_copy(cmb, o[:, :, 0:8]).then_inc(sem("d_cmb"), 1)
                v.wait_ge(sem("d_rows"), NK)
                then(v.tensor_tensor(d_dup, d_later, o[:, :, 24], ALU.subtract))
                v.wait_ge(sem("d_cmb"), 1)
                v.tensor_tensor(cmb, cmb, o[:, :, 8:16], ALU.add).then_inc(sem("d_cmb"), 1)
                settled()
                then(v.tensor_scalar(d_dup, d_dup, 1.0, None, ALU.min))
                then(v.tensor_tensor(d_pos, d_pos, d_dest, ALU.subtract))
                v.wait_ge(sem("d_cmb"), 2)
                v.tensor_tensor(cmb, cmb, o[:, :, 16:24], ALU.add).then_inc(sem("d_cmb"), 1)
                settled()
                then(v.tensor_tensor(d_pos, d_pos, d_dup, ALU.mult))
                settled()
                then(v.tensor_tensor(d_dest, d_dest, d_pos, ALU.add))
                settled()
                v.tensor_copy(d_desti[:, :], d_dest).then_inc(sem("d_dest"), 1)
            if u == 4 and j < 4:
                src, hi, lo = delta_quarter(j)
                v.wait_ge(sem("delta_hi"), j + 1)
                v.tensor_tensor(lo, src, f32(hi), ALU.subtract).then_inc(sem("delta_lo"), 1)
            if u == 4 and j == 3:
                v.wait_ge(sem("d_in_q3"), 16)
                then(v.tensor_scalar(d_q3n[:, :, :], d_q3[:, :, :], -1.0, None, ALU.mult))
                settled()
                then(v.tensor_tensor(d_q3t[:, :, :], d_q3[:, :, :], d_q3n[:, :, :], ALU.max))
                settled()
                then(v.tensor_reduce(d_thr[:, 0:2], d_q3t[:, :, :], AX_X, ALU.add))
                settled()
                then(v.tensor_scalar(d_thr[:, 2:4], d_thr[:, 0:2], 1.0 / D, 0.7, ALU.mult, ALU.mult))
            if u == 4 and j == 4:
                settled()
                for oc in range(DC):
                    then(v.tensor_scalar(d_q3[:, oc, :], d_q3[:, oc, :], d_thr[:, 2 + oc:3 + oc], None, ALU.is_gt))
                    then(v.tensor_scalar(d_q3n[:, oc, :], d_q3n[:, oc, :], d_thr[:, 2 + oc:3 + oc], None, ALU.is_gt))
                settled()
                v.tensor_tensor(d_q3t[:, :, :], d_q3[:, :, :], d_q3n[:, :, :], ALU.subtract).then_inc(sem("q_tern"), 1)
            if u == 4 and j == 5:
                v.wait_ge(sem("q_T"), 1)
                v.tensor_copy(qt[:, :, :].rearrange("p c n -> p (c n)"), ps[:, 1, :]).then_inc(sem("q3_ready"), 2)


        def sp_start(sp):
            for b in range(NB):
                sp.dma_start(x[:, TT * b:TT * (b + 1), :], a["x"][b].rearrange("(i p) d -> p i d", p=P))\
                    .then_inc(sem(f"x_in{b}"), 16)
            sp_chunks(sp, 0, 0, 0)
            sp_chunks(sp, 0, 0, 1)
            sp_delta(sp)

        CONSTS = 11

        def act_start(s):
            for dst, name, signal in ((ident, "ident", "ident_in"), (maskcol, "mask", "const_in"), (tri, "tri", "const_in"),
                                      (iota8, "iota8", "const_in"), (headmask, "headmask", "const_in"),
                                      (router_w, "router", "const_in"), (rgp, "rg_params", "const_in"),
                                      (lin_cols, "lin_cols", "const_in"), (att_cols, "att_cols", "const_in")):
                full = dst[tuple(slice(None) for _ in dst.shape)]
                s.dma_start(full, a[name]).then_inc(sem(signal), 16)
            s.dma_start(bias3[:, :], a["bias3"].to_broadcast([P, D])).then_inc(sem("const_in"), 16)
            s.dma_start(lin_bout[:, :], a["lin_bout"].to_broadcast([P, D])).then_inc(sem("const_in"), 16)
            s.dma_start(att_bo[:, :], a["att_bo"].to_broadcast([P, D])).then_inc(sem("const_in"), 16)

        def act_softplus(s):
            s.wait_ge(sem("sp_abs"), 1)
            s.activation(sp_y, sp_abs, ACT.Exp, scale=-1.0).then_inc(sem("sp_y"), 1)
            s.wait_ge(sem("sp_u"), 1)
            s.activation(sp_ln, sp_u, ACT.Ln).then_inc(sem("sp_ln"), 1)

        sp_abs, sp_y, sp_u, sp_v, sp_ln, sp_z, sp_m, sp_t = [small[:, 380 + 2 * k:382 + 2 * k] for k in range(8)]

        def pool_start(g):
            g.memset(nhalf[:, :], -0.5).then_inc(sem("const_set"), 1)
            g.memset(ones[:, :], 1.0).then_inc(sem("const_set"), 1)
            g.memset(d_zero, 0.0).then_inc(sem("const_set"), 1)

        def dve_start(v):
            v.wait_ge(sem("ident_in"), 16)
            v.tensor_copy(identb[:, :], ident[:, :]).then_inc(sem("const_ident"), 1)
            dve_ln(v, 0)
            dve_T(v, 0)

        def dve_consts(v):
            v.wait_ge(sem("const_in"), 16 * CONSTS)
            v.tensor_copy(maskb[:, :], maskcol[:, :]).then_inc(sem("const_mask"), 1)
            v.wait_ge(sem("const_in"), 16 * CONSTS)
            v.tensor_copy(rwh[:, :, :, :], router_w[:, :, :, :]).then_inc(sem("rw_hi"), 1)
            v.wait_ge(sem("rw_hi"), 1)
            v.tensor_tensor(rwl[:, :, :, :], router_w[:, :, :, :], f32(rwh[:, :, :, :]), ALU.subtract)\
                .then_inc(sem("const_router"), 1)
            v.wait_ge(sem("const_in"), 16 * CONSTS)
            v.tensor_scalar(iota8[:, :, :], iota8[:, :, :], 1.0, None, ALU.mult).then_inc(sem("const_iota"), 1)
            v.wait_ge(sem("const_in"), 16 * CONSTS)

        def dve_softplus(v):
            v.wait_ge(sem("const_in"), 16 * CONSTS)
            p = rgp[:, :, 7]
            v.tensor_scalar(sp_t, p, -1.0, None, ALU.mult).then_inc(sem("sp_1"), 1)
            v.wait_ge(sem("sp_1"), 1)
            v.tensor_tensor(sp_abs, p, sp_t, ALU.max).then_inc(sem("sp_abs"), 1)
            v.wait_ge(sem("sp_y"), 1)
            v.tensor_scalar(sp_u, sp_y, 1.0, None, ALU.add).then_inc(sem("sp_u"), 1)
            v.wait_ge(sem("sp_u"), 1)
            v.tensor_scalar(sp_v, sp_u, 1.0, None, ALU.subtract).then_inc(sem("sp_2"), 1)
            v.wait_ge(sem("sp_2"), 1)
            v.tensor_scalar(sp_z, sp_v, 0.0, None, ALU.is_equal).then_inc(sem("sp_2"), 1)
            v.wait_ge(sem("sp_2"), 2)
            v.tensor_tensor(sp_v, sp_v, sp_z, ALU.add).then_inc(sem("sp_2"), 1)
            v.wait_ge(sem("sp_2"), 3)
            v.reciprocal(sp_v, sp_v).then_inc(sem("sp_2"), 1)
            v.wait_ge(sem("sp_2"), 4)
            v.wait_ge(sem("sp_ln"), 1)
            v.tensor_tensor(sp_ln, sp_ln, sp_v, ALU.mult).then_inc(sem("sp_2"), 1)
            v.wait_ge(sem("sp_2"), 5)
            v.tensor_tensor(sp_ln, sp_ln, sp_z, ALU.add).then_inc(sem("sp_2"), 1)
            v.wait_ge(sem("sp_2"), 6)
            v.tensor_tensor(sp_ln, sp_ln, sp_y, ALU.mult).then_inc(sem("sp_2"), 1)
            v.tensor_scalar(sp_m, p, 0.0, None, ALU.max).then_inc(sem("sp_2"), 1)
            v.wait_ge(sem("sp_2"), 8)
            v.tensor_tensor(sp_ln, sp_ln, sp_m, ALU.add).then_inc(sem("sp_2"), 1)
            v.wait_ge(sem("sp_2"), 9)
            v.tensor_scalar(rgp[:, :, 10], sp_ln, -8.0, None, ALU.mult).then_inc(sem("const_rgp"), 1)

        PE_OF = {FFN0: pe_ffn, RGLRU: pe_rglru, MOE1: pe_moe1, LIN1: pe_lin1, MOE2: pe_ffn, ATT2: pe_att2, FFN3: pe_ffn3,
                 ATT3: pe_att3}
        ACT_OF = {FFN0: act_ffn, RGLRU: act_rglru, MOE1: act_moe1, LIN1: act_lin1, MOE2: act_ffn, ATT2: act_att2,
                  FFN3: act_T_next, ATT3: act_att3}
        DVE_OF = {FFN0: dve_ffn, RGLRU: dve_rglru, MOE1: dve_moe1, LIN1: dve_lin1, MOE2: dve_ffn, ATT2: dve_att2,
                  FFN3: dve_ffn3, ATT3: dve_att3}
        RES_STOP = dict(rglru=2, wt=2, lin1=4, att2=12, wo3=17)

        @block.sync
        def _(sp):
            sp_start(sp)
            for kind, what in ORDER:
                if kind == "r":
                    if stop > RES_STOP[what]:
                        sp_resident(sp, what)
                elif what < stop:
                    n = CHUNKS[KIND[what]] // 2
                    with sp.Fori(1 if what == 0 else 0, n) as i:
                        for p in range(2):
                            sp_chunks(sp, what, i, p)
                if what == "wt":
                    sp_zero(sp)
                if what == "lin1" and stop > 8:
                    sp.wait_ge(sem("x_res"), 4 * 6)
                    sp.dma_start(lin_tok[:, :, :, :], a["rope_tok"]).then_inc(sem("lin_in"), 16)
                    sp.dma_start(lin_feat[:, :, :], a["rope_feat"]).then_inc(sem("lin_in"), 16)
                    sp.dma_start(lin_bkv[:, :], a["lin_bkv"].to_broadcast([P, 2 * D])).then_inc(sem("lin_in"), 16)
                if what == "att2" and stop > 14:
                    sp.wait_ge(sem("x_res"), 4 * 14)
                    sp.dma_start(a2_bv[:, :], a["att_bv"].to_broadcast([P, D])).then_inc(sem("a2_bv_in"), 16)
                    sp_att2(sp, 14)
                    sp_att2(sp, 15)
            for b in range(NB):
                sp.wait_ge(sem("x_res"), 4 * (stop - 1 + b))
                sp.dma_start(out[b].rearrange("(i p) d -> p i d", p=P), x[:, TT * b:TT * (b + 1), :])\
                    .then_inc(sem("stored"), 16)
            sp.wait_ge(sem("stored"), 32)

        @block.gpsimd
        def _(g):
            pool_start(g)
            started = set()

            def pre(u):
                if u < stop:
                    pool_chunks(g, u, 0, 0)
                    pool_chunks(g, u, 0, 1)

            def rest(u):
                if u < stop:
                    for p in range(2):
                        pool_chunks(g, u, 1, p)
                    pool_ln(g, u + 1)
                    if u in (12, 13):
                        t = drh if u == 12 else drl
                        n = t.shape[1] // 2
                        pool_zero_a2(g, t[:, 0:n], 12)
                        for p in range(2):
                            pool_chunks(g, u, 2, p)
                        pool_zero_a2(g, t[:, n:2 * n], 12)
                    with g.Fori(3 if u in (12, 13) else 2, CHUNKS[KIND[u]] // 2) as i:
                        for p in range(2):
                            pool_chunks(g, u, i, p)

            def some(u, f, *args):
                if u < stop:
                    f(*args)

            pool_ln(g, 0)
            pre(0)
            rest(0)
            pre(1)
            rest(1)
            some(2, pool_resident, g, "rglru")
            some(2, pool_resident, g, "wt")
            some(2, pool_scatter, g, range(NK // 2))
            pool_ln(g, 3)
            some(2, pool_scatter, g, range(NK // 2, NK))
            pre(4)
            pool_ln(g, 4)
            rest(4)
            pre(5)
            rest(5)
            some(4, pool_resident, g, "lin1", 3)
            pool_ln(g, 7)
            pool_ln(g, 8)
            some(8, pool_ln2, g, 8)
            some(8, pool_lin1, g, 8)
            some(9, pool_lin1, g, 9)
            some(12, pool_zero_a2, g, a2_vh[:, :, :, :], 10)
            if stop > 12:
                for t in (a2_sq, a2_sk):
                    g.memset(f32(t[:, :, :]), 0.0).then_inc(sem("a2_szero"), 1)
            pool_ln(g, 11)
            some(12, pool_zero_a2, g, a2_vl[:, :, :, :], 10)
            some(12, pool_zero_w, g, 10)
            pre(12)
            pool_ln(g, 12)
            rest(12)
            pre(13)
            rest(13)
            some(12, pool_resident, g, "att2", 9)
            some(14, pool_att2, g, 14)
            some(15, pool_att2, g, 15)
            some(16, pool_zero_w, g, 16)
            pre(16)
            rest(16)
            pre(17)
            rest(17)
            some(17, pool_resident, g, "wo3", 15, (0, 1))
            pool_ln(g, 19)
            some(17, pool_resident, g, "wo3", 15, (2,))
            pool_ln(g, 20)
            some(17, pool_resident, g, "wo3", 15, (3,))
            pre(20)
            some(20, pool_att3, g, 20)
            pre(21)
            some(21, pool_att3, g, 21)
            pool_ln(g, 23)

        @block.tensor
        def _(pe):
            pe_T(pe, 0)
            for u in range(stop):
                PE_OF[KIND[u]](pe, u)

        @block.scalar
        def _(s):
            act_start(s)
            act_T(s, 0)
            for u in range(stop):
                if u == 4:
                    act_table(s)
                ACT_OF[KIND[u]](s, u)

        @block.vector
        def _(v):
            dve_start(v)
            for u in range(stop):
                DVE_OF[KIND[u]](v, u)


def layout(**t):
    f = {k: np.asarray(v) for k, v in t.items()}
    one = np.float32
    a = {"x": f["L0_attn_x"]}

    def ffn_chunks(gate, up, down, n, extra):
        rows = n * P

        def padded(m):
            return np.concatenate([m, np.zeros((rows - m.shape[0], m.shape[1]), m.dtype)]) if m.shape[0] < rows else m

        def cols(m):
            return padded(m).reshape(n, P, DC, P).transpose(0, 3, 2, 1).reshape(n, P, DC * P)

        parts = [cols(gate), cols(up), padded(down).reshape(n, P, D)] + extra
        return np.ascontiguousarray(np.concatenate(parts, axis=2))

    def rows_by_chunk(m):
        return m.reshape(DC, P, -1).transpose(1, 0, 2).reshape(P, -1)

    a["w0"] = ffn_chunks(f["L0_ffn_w_gate"], f["L0_ffn_w_up"], f["L0_ffn_w_down"].T, CH0, [])
    member = np.zeros((CH2 * P, P), one)
    member[:FS, E] = 1
    for e in range(E):
        member[FS + e * FE:FS + (e + 1) * FE, e] = 1
    member[:, W_LO:W_LO + E + 1] = member[:, 0:E + 1]
    a["w2"] = ffn_chunks(np.concatenate([f["L2_ffn_Wsg"], f["L2_ffn_Wg"].reshape(E * FE, D)]),
                         np.concatenate([f["L2_ffn_Wsu"], f["L2_ffn_Wu"].reshape(E * FE, D)]),
                         np.concatenate([f["L2_ffn_Wsd"].T, f["L2_ffn_Wd"].transpose(0, 2, 1).reshape(E * FE, D)]),
                         CH2, [member.reshape(CH2, P, P).transpose(0, 2, 1)])

    def block_diag(m):
        o = np.zeros((DC, P, P), one)
        for n in range(H):
            i = n % 8
            o[n // 8, 16 * i:16 * i + 16, 16 * i:16 * i + 16] = m[n]
        return o.transpose(1, 0, 2).reshape(P, DC * P)

    a["rglru"] = np.concatenate([rows_by_chunk(f["L0_attn_W_xy"].T), block_diag(f["L0_attn_ig_w"]),
                                 block_diag(f["L0_attn_ag_w"]), rows_by_chunk(f["L0_attn_W_resid"].T)], axis=1)
    cp = np.zeros((P, DC, 16), one)
    for k in range(4):
        cp[:, :, k] = f["L0_attn_conv_w"][k].reshape(DC, P).T
    for k, name in enumerate(("conv_b", "ig_b", "ag_b", "a_param")):
        cp[:, :, 4 + k] = f["L0_attn_" + name].reshape(DC, P).T
    a["rg_params"] = cp

    a["wt"] = rows_by_chunk(f["L1_ffn_W"].T)
    idx = f["L1_ffn_mask_idx"]
    a["idx_row"] = idx.reshape(1, NS)
    a["idx_col"] = np.ascontiguousarray(idx.reshape(NS // P, P).T)
    a["pos"] = np.ascontiguousarray((D * D + np.arange(NS, dtype=one)).reshape(NS // P, P).T)
    a["atoms"] = f["L1_ffn_atoms"]
    a["expert_atoms"] = f["L1_ffn_expert_atom_weights"]
    a["importance"] = np.ascontiguousarray(f["L1_ffn_importance"].T.reshape(NS // P, P, E).transpose(1, 0, 2).reshape(P, P))
    a["router"] = np.ascontiguousarray(np.stack([m.T.reshape(DC, P, E).transpose(1, 0, 2)
                                                 for m in (f["L1_ffn_gate_w"], f["L2_ffn_Wr"])], axis=1))
    w_in, b_in = f["L1_attn_W_in"], f["L1_attn_b_in"]
    swap = np.arange(P).reshape(-1, 2)[:, ::-1].reshape(-1)
    q = w_in[:, 0:D]
    qs = np.concatenate([q[:, 0:P], q[:, swap], q[:, P:D]], axis=1)
    a["lin1"] = np.concatenate([rows_by_chunk(w_in[:, D:3 * D]), rows_by_chunk(qs), rows_by_chunk(f["L1_attn_W_out"])], axis=1)
    cols = np.zeros((P, 8), one)
    cols[:, 0:2] = f["L1_attn_ln_w"].reshape(DC, P).T
    cols[:, 2:4] = f["L1_attn_ln_b"].reshape(DC, P).T
    cols[:, 4], cols[:, 5], cols[:, 6] = b_in[0:P], b_in[swap], b_in[P:D]
    a["lin_cols"] = cols
    a["lin_bkv"] = b_in[D:3 * D].reshape(1, 2 * D)
    a["lin_bout"] = f["L1_attn_b_out"].reshape(1, D)
    rot = D // 2
    inv = (one(1.0) / np.power(one(10000.0), (np.arange(0, rot, 2, dtype=one) / one(rot)))).astype(one)
    ang = np.repeat((np.arange(T, dtype=one)[:, None] * inv[None, :]).astype(one), 2, axis=1)
    sign = np.where(np.arange(rot) % 2 == 0, -1, 1).astype(one)
    tab = np.stack([np.cos(ang), np.sin(ang) * sign]).astype(one)
    a["rope_tok"] = np.ascontiguousarray(tab.reshape(2, TT, P, rot).transpose(2, 0, 1, 3))
    a["rope_feat"] = np.ascontiguousarray(tab.transpose(2, 0, 1))

    a["att2"] = np.concatenate([rows_by_chunk(f["L2_attn_W" + k].T) for k in "qkvo"], axis=1)
    a["att_cols"] = np.ascontiguousarray(np.concatenate([f["L2_attn_bq"].reshape(DC, P).T, f["L2_attn_bk"].reshape(DC, P).T], axis=1))
    a["att_bv"] = f["L2_attn_bv"].reshape(1, D)
    a["att_bo"] = f["L2_attn_bo"].reshape(1, D)

    def by_pair(m):
        return m.reshape(H // 2, 2, HD3, DC, P).transpose(0, 4, 3, 1, 2).reshape(H // 2, P, DC * 2 * HD3)

    a["qk3"] = np.ascontiguousarray(np.concatenate([by_pair(f["L3_attn_W_Q"]), by_pair(f["L3_attn_W_K"])], axis=2))
    a["v3"] = np.ascontiguousarray(by_pair(f["L3_attn_W_V"]))
    a["wo3"] = np.ascontiguousarray(f["L3_attn_W_O"].transpose(2, 0, 1).reshape(P, H * D))
    a["weight3"] = np.ascontiguousarray(f["L3_ffn_weight"].reshape(DC, P, D).transpose(1, 0, 2))
    a["bias3"] = f["L3_ffn_bias"].reshape(1, D)
    a["ident"] = np.eye(P, dtype=one)
    a["mask"] = np.where(np.arange(P)[None, :] > np.arange(P)[:, None], one(NEG), one(0))
    a["tri"] = (np.arange(P)[:, None] <= np.arange(P)[None, :]).astype(one)
    a["iota8"] = np.ascontiguousarray(np.broadcast_to(np.arange(E, dtype=one), (P, TT, E)))
    a["headmask"] = (np.arange(P)[:, None] // HD2 == np.arange(8)[None, :]).astype(one)
    return {k: np.ascontiguousarray(v) for k, v in a.items()}


def kernel(**inputs):
    import concourse.bacc as bacc
    from concourse.bass_utils import run_bass_kernel_spmd

    arrays = layout(**inputs)
    nc = bacc.Bacc("TRN2", target_bir_lowering=False, num_devices=1)
    aps = {k: nc.dram_tensor(f"in_{k}", v.shape, mybir.dt.from_np(v.dtype), kind="ExternalInput").ap()
           for k, v in arrays.items()}
    out = nc.dram_tensor("out", (NB, T, D), F32, kind="ExternalOutput").ap()
    build(nc, aps, out)
    r = run_bass_kernel_spmd(nc, [{f"in_{k}": v for k, v in arrays.items()}], core_ids=[0])
    return r.results[0]["out"]
```
